# Optimizing a Trainium2 kernel written in Bass

```python
import numpy as np
import jax
import jax.numpy as jnp

def _softmax(x, axis=-1):
    return jax.nn.softmax(x, axis=axis)

def _gelu(x):
    return jax.nn.gelu(x, approximate=True)

def _silu(x):
    return jax.nn.silu(x)

def _sigmoid(x):
    return jax.nn.sigmoid(x)

def _layernorm(x, axis=-1, eps=1e-05):
    m = jnp.mean(x, axis=axis, keepdims=True)
    v = jnp.var(x, axis=axis, keepdims=True)
    return (x - m) / jnp.sqrt(v + eps)

def _scatter_add(tgt, idx, src, axis=0):
    return tgt.at[idx].add(src)

def _segment_sum(src, seg, n):
    return jax.ops.segment_sum(src, seg, n)
kernel_name = 'mk_decoder_preln_d2_seqx_r4_556fad'

def setup_inputs(seed: int=0):
    np.random.seed(seed)
    _w = jnp.asarray

    def _rec_inputs():
        import jax
        import jax.numpy as jnp
        _rk = jax.random.key(seed)
        x = -0.0002928 + 1 * jax.random.normal(jax.random.fold_in(_rk, 1), (16, 112, 256), jnp.float32)
        _lenS = 112 - jax.random.randint(jax.random.fold_in(_rk, 7), (16,), 0, max(1, 112 // 4) + 1, jnp.int32)
        _lenS2 = 375 - jax.random.randint(jax.random.fold_in(_rk, 8), (16,), 0, max(1, 375 // 4) + 1, jnp.int32)
        _ctx_1024P = jax.random.normal(jax.random.fold_in(_rk, 11), (16, 16, 256), jnp.float32)
        _ctx_1024c = jax.random.dirichlet(jax.random.fold_in(_rk, 511), 0.3 * jnp.ones((16,), jnp.float32), (16, 375))
        _ctx_1024t = jnp.einsum('bsk,bkd->bsd', _ctx_1024c, _ctx_1024P)
        _ctx_1024t = _ctx_1024t * jax.lax.rsqrt(jnp.mean(jnp.square(_ctx_1024t)) + 1e-12) * 0.953939
        ctx_1024 = 1.43633e-05 + 1.0001 * (_ctx_1024t + 0.3 * jax.random.normal(jax.random.fold_in(_rk, 611), (16, 375, 256), jnp.float32))
        return (x, ctx_1024)
    x, ctx_1024 = _rec_inputs()

    def _L0_attn_setup():
        import jax, jax.numpy as jnp
        import numpy as np
        import math
        E = 256
        H = 64
        B = 4
        S = 512
        key = jax.random.key(seed)
        ks = jax.random.split(key, 9)
        x = jax.random.normal(ks[0], (B, S, E), dtype=jnp.float32)

        def he(k, fan_in, shape):
            return jax.random.normal(k, shape, dtype=jnp.float32) * jnp.sqrt(2.0 / fan_in)
        wq = he(ks[1], E, (E, H))
        bq = jnp.zeros((H,), jnp.float32)
        wk = he(ks[2], E, (E, H))
        bk = jnp.zeros((H,), jnp.float32)
        wv = he(ks[3], E, (E, H))
        bv = jnp.zeros((H,), jnp.float32)
        wo = he(ks[4], H, (H, E))
        bo = jnp.zeros((E,), jnp.float32)
        return {'x': x, 'wq': wq, 'bq': bq, 'wk': wk, 'bk': bk, 'wv': wv, 'bv': bv, 'wo': wo, 'bo': bo}
    _L0_attn_all = _L0_attn_setup()
    _L0_attn_in = {k: v for k, v in _L0_attn_all.items() if k in ('wq', 'bq', 'wk', 'bk', 'wv', 'bv', 'wo', 'bo')}
    del _L0_attn_all

    def _L0_xattn_setup():
        import jax, jax.numpy as jnp
        import numpy as np
        D, H = (256, 16)
        DH = D // H

        def _split_heads(z):
            b, t, _ = z.shape
            return z.reshape(b, t, H, DH).transpose(0, 2, 1, 3)
        key = jax.random.key(seed)
        ks = jax.random.split(key, 11)
        b, t, ta = (2, 512, 375)
        s = 1.0 / np.sqrt(D)
        return {'x': jax.random.normal(ks[0], (b, t, D), dtype=jnp.float32), 'xa': jax.random.normal(ks[1], (b, ta, D), dtype=jnp.float32), 'Wqkv': jax.random.normal(ks[2], (D, 3 * D), dtype=jnp.float32) * s, 'bqkv': jax.random.normal(ks[3], (3 * D,), dtype=jnp.float32) * 0.01, 'Wqkv_aux': jax.random.normal(ks[4], (D, 3 * D), dtype=jnp.float32) * s, 'bqkv_aux': jax.random.normal(ks[5], (3 * D,), dtype=jnp.float32) * 0.01, 'Wo': jax.random.normal(ks[6], (D, D), dtype=jnp.float32) * s, 'bo': jax.random.normal(ks[7], (D,), dtype=jnp.float32) * 0.01, 'g': jnp.zeros((H,), dtype=jnp.float32)}
    _L0_xattn_all = _L0_xattn_setup()
    _L0_xattn_in = {k: v for k, v in _L0_xattn_all.items() if k in ('Wqkv', 'bqkv', 'Wqkv_aux', 'bqkv_aux', 'Wo', 'bo', 'g')}
    del _L0_xattn_all

    def _L0_ffn_setup():
        import jax, jax.numpy as jnp
        import numpy as np
        D_MODEL = 256
        EXPANSION = 4
        D_HIDDEN = D_MODEL * EXPANSION
        NUM_STAGES = int(np.log2(D_HIDDEN))

        def butterfly(y, weights, dim):
            lead = y.shape[:-1]
            for stage in range(weights.shape[0]):
                s = 2 ** stage
                nb = dim // (2 * s)
                yr = y.reshape(*lead, nb, 2, s)
                a = yr[..., 0, :]
                b = yr[..., 1, :]
                w = weights[stage].reshape(nb, s, 2, 2)
                na = w[..., 0, 0] * a + w[..., 0, 1] * b
                nb2 = w[..., 1, 0] * a + w[..., 1, 1] * b
                y = jnp.stack([na, nb2], axis=-2).reshape(*lead, dim)
            return y
        key = jax.random.key(seed)
        ks = jax.random.split(key, 6)
        B, S = (4, 512)
        x = jax.random.normal(ks[0], (B, S, D_MODEL), jnp.float32)
        W_exp = jax.random.normal(ks[1], (D_MODEL, D_HIDDEN), jnp.float32) * 0.02
        b_exp = jnp.zeros((D_HIDDEN,), jnp.float32)
        up_weights = jax.random.normal(ks[2], (NUM_STAGES, D_HIDDEN // 2, 2, 2), jnp.float32) * 0.02
        up_bias = jnp.zeros((D_HIDDEN,), jnp.float32)
        down_weights = jax.random.normal(ks[3], (NUM_STAGES, D_HIDDEN // 2, 2, 2), jnp.float32) * 0.02
        W_con = jax.random.normal(ks[4], (D_HIDDEN, D_MODEL), jnp.float32) * 0.02
        b_con = jnp.zeros((D_MODEL,), jnp.float32)
        down_bias = jnp.zeros((D_MODEL,), jnp.float32)
        return dict(x=x, W_exp=W_exp, b_exp=b_exp, up_weights=up_weights, up_bias=up_bias, down_weights=down_weights, W_con=W_con, b_con=b_con, down_bias=down_bias)
    _L0_ffn_all = _L0_ffn_setup()
    _L0_ffn_in = {k: v for k, v in _L0_ffn_all.items() if k in ('W_exp', 'b_exp', 'up_weights', 'up_bias', 'down_weights', 'W_con', 'b_con', 'down_bias')}
    del _L0_ffn_all

    def _L1_attn_setup():
        import jax, jax.numpy as jnp
        import numpy as np
        EMB = 256
        HEADS = 16
        HEAD_DIM = EMB // HEADS
        BLOCK = 64
        N_GLOBAL = 4
        WINDOW = 128
        ROPE_BASE = 10000.0

        def rotate_half(x):
            x1 = x[..., ::2]
            x2 = x[..., 1::2]
            return jnp.stack((-x2, x1), axis=-1).reshape(x.shape)

        def rope_cos_sin(seq_len, dtype=jnp.float32):
            inv_freq = 1.0 / ROPE_BASE ** (jnp.arange(0, HEAD_DIM, 2, dtype=jnp.float32) / HEAD_DIM)
            pos = jnp.arange(seq_len, dtype=jnp.float32)
            freqs = jnp.outer(pos, inv_freq)
            emb = jnp.concatenate([freqs, freqs], -1)
            return (jnp.cos(emb)[None, None].astype(dtype), jnp.sin(emb)[None, None].astype(dtype))

        def block_mask(seq_len):
            i = jnp.arange(seq_len)[:, None]
            j = jnp.arange(seq_len)[None, :]
            blk = i // BLOCK == j // BLOCK
            glob = (i < N_GLOBAL) | (j < N_GLOBAL)
            slide = jnp.abs(i - j) <= WINDOW
            return (blk | glob | slide) & (j <= i)
        key = jax.random.key(seed)
        kx, kq, ko = jax.random.split(key, 3)
        B, S = (2, 512)
        x = jax.random.normal(kx, (B, S, EMB), jnp.float32)
        qkv_w = jax.random.normal(kq, (3 * EMB, EMB), jnp.float32) * EMB ** (-0.5)
        out_w = jax.random.normal(ko, (EMB, EMB), jnp.float32) * EMB ** (-0.5)
        return {'x': x, 'qkv_w': qkv_w, 'out_w': out_w}
    _L1_attn_all = _L1_attn_setup()
    _L1_attn_in = {k: v for k, v in _L1_attn_all.items() if k in ('qkv_w', 'out_w')}
    del _L1_attn_all

    def _L1_xattn_setup():
        import jax, jax.numpy as jnp
        import numpy as np
        DIM = 256
        NHEADS = 16
        HEAD_DIM = DIM // NHEADS
        EPS = 1e-06

        def _rms_norm(t):
            mean_sq = jnp.mean(t * t, axis=-1, keepdims=True)
            return t * jax.lax.rsqrt(mean_sq + EPS)
        key = jax.random.key(seed)
        k1, k2, k3, k4 = jax.random.split(key, 4)
        B, Sq, Skv = (2, 512, 512)
        x = jax.random.normal(k1, (B, Sq, DIM), dtype=jnp.float32)
        context = jax.random.normal(k2, (B, Skv, DIM), dtype=jnp.float32)
        W_q = jax.random.normal(k3, (DIM, DIM), dtype=jnp.float32) * 0.02
        W_kv = jax.random.normal(k4, (DIM, 2 * DIM), dtype=jnp.float32) * 0.02
        return {'x': x, 'context': context, 'W_q': W_q, 'W_kv': W_kv}
    _L1_xattn_all = _L1_xattn_setup()
    _L1_xattn_in = {k: v for k, v in _L1_xattn_all.items() if k in ('W_q', 'W_kv')}
    del _L1_xattn_all

    def _L1_ffn_setup():
        import jax, jax.numpy as jnp
        import numpy as np
        BLOCK = 16
        _GRID = jnp.array([0.0, 0.5, 1.0, 1.5, 2.0, 3.0, 4.0, 6.0], dtype=jnp.float32)
        _MID = jnp.array([0.25, 0.75, 1.25, 1.75, 2.5, 3.5, 5.0], dtype=jnp.float32)

        def fp4_quant_dequant(x):
            shape = x.shape
            xb = x.reshape(shape[:-1] + (shape[-1] // BLOCK, BLOCK))
            scale = jnp.max(jnp.abs(xb), axis=-1, keepdims=True) / 6.0
            scale = jnp.maximum(scale, jnp.float32(1e-12))
            xn = xb / scale
            idx = jnp.searchsorted(_MID, jnp.abs(xn))
            q = _GRID[idx] * jnp.sign(xn) * scale
            return q.reshape(shape)

        def fp4_linear(x, w):
            xq = fp4_quant_dequant(x)
            wq = fp4_quant_dequant(w)
            return jnp.einsum('bsk,nk->bsn', xq, wq)
        key = jax.random.key(seed)
        k1, k2, k3, k4 = jax.random.split(key, 4)
        H, I = (256, 704)
        x = jax.random.normal(k1, (4, 1024, H), dtype=jnp.float32)
        w_gate = jax.random.normal(k2, (I, H), dtype=jnp.float32) * 0.02
        w_up = jax.random.normal(k3, (I, H), dtype=jnp.float32) * 0.02
        w_down = jax.random.normal(k4, (H, I), dtype=jnp.float32) * 0.02
        return {'x': x, 'w_gate': w_gate, 'w_up': w_up, 'w_down': w_down}
    _L1_ffn_all = _L1_ffn_setup()
    _L1_ffn_in = {k: v for k, v in _L1_ffn_all.items() if k in ('w_gate', 'w_up', 'w_down')}
    del _L1_ffn_all
    return {'x': x, 'ctx_1024': ctx_1024, 'L0_attn_wq': _L0_attn_in['wq'], 'L0_attn_bq': _L0_attn_in['bq'], 'L0_attn_wk': _L0_attn_in['wk'], 'L0_attn_bk': _L0_attn_in['bk'], 'L0_attn_wv': _L0_attn_in['wv'], 'L0_attn_bv': _L0_attn_in['bv'], 'L0_attn_wo': _L0_attn_in['wo'], 'L0_attn_bo': _L0_attn_in['bo'], 'L0_xattn_Wqkv': _L0_xattn_in['Wqkv'], 'L0_xattn_bqkv': _L0_xattn_in['bqkv'], 'L0_xattn_Wqkv_aux': _L0_xattn_in['Wqkv_aux'], 'L0_xattn_bqkv_aux': _L0_xattn_in['bqkv_aux'], 'L0_xattn_Wo': _L0_xattn_in['Wo'], 'L0_xattn_bo': _L0_xattn_in['bo'], 'L0_xattn_g': _L0_xattn_in['g'], 'L0_ffn_W_exp': _L0_ffn_in['W_exp'], 'L0_ffn_b_exp': _L0_ffn_in['b_exp'], 'L0_ffn_up_weights': _L0_ffn_in['up_weights'], 'L0_ffn_up_bias': _L0_ffn_in['up_bias'], 'L0_ffn_down_weights': _L0_ffn_in['down_weights'], 'L0_ffn_W_con': _L0_ffn_in['W_con'], 'L0_ffn_b_con': _L0_ffn_in['b_con'], 'L0_ffn_down_bias': _L0_ffn_in['down_bias'], 'L1_attn_qkv_w': _L1_attn_in['qkv_w'], 'L1_attn_out_w': _L1_attn_in['out_w'], 'L1_xattn_W_q': _L1_xattn_in['W_q'], 'L1_xattn_W_kv': _L1_xattn_in['W_kv'], 'L1_ffn_w_gate': _L1_ffn_in['w_gate'], 'L1_ffn_w_up': _L1_ffn_in['w_up'], 'L1_ffn_w_down': _L1_ffn_in['w_down']}

def reference(x, ctx_1024, L0_attn_wq, L0_attn_bq, L0_attn_wk, L0_attn_bk, L0_attn_wv, L0_attn_bv, L0_attn_wo, L0_attn_bo, L0_xattn_Wqkv, L0_xattn_bqkv, L0_xattn_Wqkv_aux, L0_xattn_bqkv_aux, L0_xattn_Wo, L0_xattn_bo, L0_xattn_g, L0_ffn_W_exp, L0_ffn_b_exp, L0_ffn_up_weights, L0_ffn_up_bias, L0_ffn_down_weights, L0_ffn_W_con, L0_ffn_b_con, L0_ffn_down_bias, L1_attn_qkv_w, L1_attn_out_w, L1_xattn_W_q, L1_xattn_W_kv, L1_ffn_w_gate, L1_ffn_w_up, L1_ffn_w_down):
    import jax
    import jax.numpy as jnp

    def _L0_attn_ref(x, wq, bq, wk, bk, wv, bv, wo, bo):
        import jax, jax.numpy as jnp
        import numpy as np
        import math
        E = 256
        H = 64
        B = 4
        S = 512
        q = x @ wq + bq
        k = x @ wk + bk
        v = x @ wv + bv
        scale = 1.0 / math.sqrt(H)
        w = jnp.einsum('bqh,bkh->bqk', q, k) * scale
        seq = x.shape[1]
        mask = jnp.triu(jnp.ones((1, seq, seq), dtype=w.dtype), 1) * -100000000000.0
        w = w + mask
        w = jax.nn.softmax(w, axis=-1)
        z = jnp.einsum('bqk,bkh->bqh', w, v)
        z = z @ wo + bo
        return z

    def _L0_xattn_ref(x, xa, Wqkv, bqkv, Wqkv_aux, bqkv_aux, Wo, bo, g):
        import jax, jax.numpy as jnp
        import numpy as np
        D, H = (256, 16)
        DH = D // H

        def _split_heads(z):
            b, t, _ = z.shape
            return z.reshape(b, t, H, DH).transpose(0, 2, 1, 3)
        qkv = x @ Wqkv + bqkv
        qkv_a = xa @ Wqkv_aux + bqkv_aux
        q, k, v = (_split_heads(c) for c in jnp.split(qkv, 3, axis=-1))
        qa, ka, va = (_split_heads(c) for c in jnp.split(qkv_a, 3, axis=-1))
        scale = 1.0 / jnp.sqrt(jnp.float32(DH))
        dots = jnp.einsum('bhqd,bhkd->bhqk', q, k) * scale
        dots_aux = jnp.einsum('bhqd,bhkd->bhqk', q, ka) * scale
        p = jax.nn.softmax(dots, axis=-1)
        pa = jax.nn.softmax(dots_aux, axis=-1)
        h_main = jnp.einsum('bhqk,bhkd->bhqd', p, v)
        h_aux = jnp.einsum('bhqk,bhkd->bhqd', pa, va)
        gate = jax.nn.sigmoid(g).reshape(1, H, 1, 1)
        out = h_main * (1.0 - gate) + h_aux * gate
        b, _, t, _ = out.shape
        out = out.transpose(0, 2, 1, 3).reshape(b, t, H * DH)
        return out @ Wo + bo

    def _L0_ffn_ref(x, W_exp, b_exp, up_weights, up_bias, down_weights, W_con, b_con, down_bias):
        import jax, jax.numpy as jnp
        import numpy as np
        D_MODEL = 256
        EXPANSION = 4
        D_HIDDEN = D_MODEL * EXPANSION
        NUM_STAGES = int(np.log2(D_HIDDEN))

        def butterfly(y, weights, dim):
            lead = y.shape[:-1]
            for stage in range(weights.shape[0]):
                s = 2 ** stage
                nb = dim // (2 * s)
                yr = y.reshape(*lead, nb, 2, s)
                a = yr[..., 0, :]
                b = yr[..., 1, :]
                w = weights[stage].reshape(nb, s, 2, 2)
                na = w[..., 0, 0] * a + w[..., 0, 1] * b
                nb2 = w[..., 1, 0] * a + w[..., 1, 1] * b
                y = jnp.stack([na, nb2], axis=-2).reshape(*lead, dim)
            return y
        h = jnp.einsum('bsd,dh->bsh', x, W_exp) + b_exp
        h = butterfly(h, up_weights, D_HIDDEN)
        h = jax.nn.gelu(h + up_bias, approximate=False)
        h = butterfly(h, down_weights, D_HIDDEN)
        y = jnp.einsum('bsh,hd->bsd', h, W_con) + b_con
        return y + down_bias

    def _L1_attn_ref(x, qkv_w, out_w):
        import jax, jax.numpy as jnp
        import numpy as np
        EMB = 256
        HEADS = 16
        HEAD_DIM = EMB // HEADS
        BLOCK = 64
        N_GLOBAL = 4
        WINDOW = 128
        ROPE_BASE = 10000.0

        def rotate_half(x):
            x1 = x[..., ::2]
            x2 = x[..., 1::2]
            return jnp.stack((-x2, x1), axis=-1).reshape(x.shape)

        def rope_cos_sin(seq_len, dtype=jnp.float32):
            inv_freq = 1.0 / ROPE_BASE ** (jnp.arange(0, HEAD_DIM, 2, dtype=jnp.float32) / HEAD_DIM)
            pos = jnp.arange(seq_len, dtype=jnp.float32)
            freqs = jnp.outer(pos, inv_freq)
            emb = jnp.concatenate([freqs, freqs], -1)
            return (jnp.cos(emb)[None, None].astype(dtype), jnp.sin(emb)[None, None].astype(dtype))

        def block_mask(seq_len):
            i = jnp.arange(seq_len)[:, None]
            j = jnp.arange(seq_len)[None, :]
            blk = i // BLOCK == j // BLOCK
            glob = (i < N_GLOBAL) | (j < N_GLOBAL)
            slide = jnp.abs(i - j) <= WINDOW
            return (blk | glob | slide) & (j <= i)
        B, S, E = x.shape
        scale = HEAD_DIM ** (-0.5)
        qkv = x @ qkv_w.T
        qkv = qkv.reshape(B, S, 3, HEADS, HEAD_DIM)
        qkv = jnp.transpose(qkv, (2, 0, 3, 1, 4))
        q, k, v = (qkv[0], qkv[1], qkv[2])
        cos, sin = rope_cos_sin(S, x.dtype)
        q = q * cos + rotate_half(q) * sin
        k = k * cos + rotate_half(k) * sin
        mask = block_mask(S)
        scores = jnp.einsum('bhqd,bhkd->bhqk', q, k) * scale
        scores = jnp.where(mask[None, None], scores, jnp.finfo(scores.dtype).min)
        attn = jax.nn.softmax(scores, axis=-1)
        out = jnp.einsum('bhqk,bhkd->bhqd', attn, v)
        out = jnp.transpose(out, (0, 2, 1, 3)).reshape(B, S, E)
        return out @ out_w.T

    def _L1_xattn_ref(x, context, W_q, W_kv):
        import jax, jax.numpy as jnp
        import numpy as np
        DIM = 256
        NHEADS = 16
        HEAD_DIM = DIM // NHEADS
        EPS = 1e-06

        def _rms_norm(t):
            mean_sq = jnp.mean(t * t, axis=-1, keepdims=True)
            return t * jax.lax.rsqrt(mean_sq + EPS)
        B, Sq, D = x.shape
        Skv = context.shape[1]
        H, hd = (NHEADS, HEAD_DIM)
        q = (x @ W_q).reshape(B, Sq, H, hd)
        kv = (context @ W_kv).reshape(B, Skv, H, hd, 2)
        k = kv[..., 0]
        v = kv[..., 1]
        q = _rms_norm(q)
        k = _rms_norm(k)
        scale = 1.0 / jnp.sqrt(jnp.asarray(hd, dtype=q.dtype))
        scores = jnp.einsum('bqhd,bkhd->bhqk', q, k) * scale
        attn = jax.nn.softmax(scores, axis=-1)
        out = jnp.einsum('bhqk,bkhd->bqhd', attn, v)
        return out.reshape(B, Sq, D)

    def _L1_ffn_ref(x, w_gate, w_up, w_down):
        import jax, jax.numpy as jnp
        import numpy as np
        BLOCK = 16
        _GRID = jnp.array([0.0, 0.5, 1.0, 1.5, 2.0, 3.0, 4.0, 6.0], dtype=jnp.float32)
        _MID = jnp.array([0.25, 0.75, 1.25, 1.75, 2.5, 3.5, 5.0], dtype=jnp.float32)

        def fp4_quant_dequant(x):
            shape = x.shape
            xb = x.reshape(shape[:-1] + (shape[-1] // BLOCK, BLOCK))
            scale = jnp.max(jnp.abs(xb), axis=-1, keepdims=True) / 6.0
            scale = jnp.maximum(scale, jnp.float32(1e-12))
            xn = xb / scale
            idx = jnp.searchsorted(_MID, jnp.abs(xn))
            q = _GRID[idx] * jnp.sign(xn) * scale
            return q.reshape(shape)

        def fp4_linear(x, w):
            xq = fp4_quant_dequant(x)
            wq = fp4_quant_dequant(w)
            return jnp.einsum('bsk,nk->bsn', xq, wq)
        gate = fp4_linear(x, w_gate)
        y = fp4_linear(x, w_up)
        h = jax.nn.silu(gate) * y
        return fp4_linear(h, w_down)
    x = x + _L0_attn_ref(_layernorm(x, axis=-1), L0_attn_wq, L0_attn_bq, L0_attn_wk, L0_attn_bk, L0_attn_wv, L0_attn_bv, L0_attn_wo, L0_attn_bo)
    x = x + _L0_xattn_ref(_layernorm(x, axis=-1), ctx_1024, L0_xattn_Wqkv, L0_xattn_bqkv, L0_xattn_Wqkv_aux, L0_xattn_bqkv_aux, L0_xattn_Wo, L0_xattn_bo, L0_xattn_g)
    x = x + _L0_ffn_ref(_layernorm(x, axis=-1), L0_ffn_W_exp, L0_ffn_b_exp, L0_ffn_up_weights, L0_ffn_up_bias, L0_ffn_down_weights, L0_ffn_W_con, L0_ffn_b_con, L0_ffn_down_bias)
    x = x + _L1_attn_ref(_layernorm(x, axis=-1), L1_attn_qkv_w, L1_attn_out_w)
    x = x + _L1_xattn_ref(_layernorm(x, axis=-1), ctx_1024, L1_xattn_W_q, L1_xattn_W_kv)
    x = x + _L1_ffn_ref(_layernorm(x, axis=-1), L1_ffn_w_gate, L1_ffn_w_up, L1_ffn_w_down)
    return x

_drawn_inputs = setup_inputs


def setup_inputs(seed=0):
    import zlib

    import numpy as np

    out = dict(_drawn_inputs(seed))
    spreads = {'L0_attn_bq': (0.0, 0.1),
     'L0_attn_bk': (0.0, 0.8),
     'L0_attn_bv': (0.0, 0.1),
     'L0_attn_bo': (0.0, 0.1),
     'L0_xattn_g': (0.0, 0.527),
     'L0_ffn_b_exp': (0.0, 0.1),
     'L0_ffn_up_bias': (0.0, 0.1),
     'L0_ffn_b_con': (0.0, 0.1),
     'L0_ffn_down_bias': (0.0, 0.1)}
    factors = {'L0_xattn_bqkv': 8.0,
     'L0_xattn_bqkv_aux': 8.0,
     'L0_xattn_bo': 6.918,
     'L1_ffn_w_gate': 2.952,
     'L1_ffn_w_up': 2.79,
     'L1_ffn_w_down': 2.781}
    for name, (base, spread) in spreads.items():
        noise = np.random.default_rng([zlib.crc32(name.encode()), seed]).standard_normal(out[name].shape)
        drawn = base * np.exp(spread * noise) if base else spread * noise
        out[name] = jnp.asarray(drawn.astype(out[name].dtype))
    for name, factor in factors.items():
        out[name] = (out[name] * factor).astype(out[name].dtype)
    return out
```

```python
from contextlib import ExitStack

import concourse.bass as bass
from concourse import mybir

F32 = mybir.dt.float32
BF16 = mybir.dt.bfloat16
I32 = mybir.dt.int32
ACT = mybir.ActivationFunctionType
ALU = mybir.AluOpType
AX = mybir.AxisListType

B, T, D = 16, 112, 256
TC, KT = 375, 125
NK = TC // KT
KD = D // 128
G = 4
NG = B // G
H, HD = 16, 16
HS = 64
HID = 1024
NHT = HID // 128
FF = 704
BLK = 16
LN_EPS = 1e-5
RMS_EPS = 1e-6
MIDS = (0.25, 0.75, 1.25, 1.75, 2.5, 3.5, 5.0)


FINAL = {1: ("a_x", NG), 2: ("x_x", B), 3: ("f_x", B), 4: ("r_x", B), 5: ("c_x", B), 6: ("m_x", B)}

NORMS = {"a": 0, "x": NG, "f": NG + B, "r": 2 * NG + B, "c": 2 * NG + 2 * B, "m": 2 * NG + 3 * B}
TURNS = {"a": 0, "x": NG, "r": NG + B, "c": NG + 2 * B}
CROSS = {"x": 0, "c": B}
HEADS = {"x": 0, "r": B, "c": 2 * B}


class Sems:

    def __init__(self, nc, ctx):
        self.nc, self.ctx, self.made = nc, ctx, {}

    def __call__(self, name):
        if name not in self.made:
            self.made[name] = self.ctx.enter_context(self.nc.semaphore(name))
        return self.made[name]


def bcast(ap, dim, n):
    shape = list(ap.shape)
    shape.insert(dim, n)
    return ap.unsqueeze(dim).broadcast_to(shape)


def build(nc, a, c, out, parts=6):
    with ExitStack() as ctx:
        def sb(name, shape, dt=F32):
            return ctx.enter_context(nc.sbuf_tensor(name, shape, dt))

        def ps(name, shape, dt=F32):
            return ctx.enter_context(nc.psum_tensor(name, shape, dt))

        s = Sems(nc, ctx)

        PS = ps("PS", [128, 4, 512])
        PT = ps("PT", [128, 2, 512])
        PO = ps("PO", [128, 2, 512])

        X = sb("X", [T, B, D])
        ident = sb("ident", [128, 128])
        identb = sb("identb", [T, T], BF16)
        causal = sb("causal", [T, T])
        causal4 = sb("causal4", [T, 4, T], BF16)
        headmask = sb("headmask", [128, 8])
        headsum = sb("headsum", [128, 128])
        cosq = sb("cosq", [128, T])
        sinq = sb("sinq", [128, T])

        a_wqk = sb("a_wqk", [128, KD, 2, HS])
        a_wv = sb("a_wv", [128, KD, HS])
        a_wo = sb("a_wo", [HS, D])
        a_bqk = sb("a_bqk", [HS, 2])
        a_bv = sb("a_bv", [T, HS])
        a_bo = sb("a_bo", [T, D])
        x_w = sb("x_w", [128, KD, 3 * D])
        x_wa = sb("x_wa", [128, KD, 2 * D])
        x_wo = sb("x_wo", [128, KD, D])
        x_bqk = sb("x_bqk", [128, 2, KD])
        x_bka = sb("x_bka", [128, KD])
        x_bv = sb("x_bv", [T, D])
        x_bva = sb("x_bva", [KT, D])
        x_bo = sb("x_bo", [T, D])
        x_g = sb("x_g", [T, H])
        x_gate = sb("x_gate", [T, 2, H])

        f_up = sb("f_up", [128, KD, HID])
        f_down = sb("f_down", [128, NHT, D])
        f_hb = sb("f_hb", [128, NHT])
        f_bo = sb("f_bo", [T, D])
        f_bd = sb("f_bd", [T, D])
        r_w = sb("r_w", [128, KD, 3 * D])
        r_wr = sb("r_wr", [128, KD, 2 * D])
        r_wo = sb("r_wo", [128, KD, D])
        c_wq = sb("c_wq", [128, KD, D])
        c_wk = sb("c_wk", [128, KD, D])
        c_wv = sb("c_wv", [128, KD, D])
        m_wgu = sb("m_wgu", [128, KD, 2, FF])
        m_wd = sb("m_wd", [128, 6, D])
        m_rs = sb("m_rs", [128, 64])

        stats = sb("stats", [T, G, 6])
        meanvar = sb("meanvar", [T, G, 2])
        logvar = sb("logvar", [T, G])
        rstd = sb("rstd", [T, G])
        xn = sb("xn", [T, G, D])
        xnT = sb("xnT", [128, KD, G * T])
        tick_v = sb("tick_v", [1, 1])
        tick_g = sb("tick_g", [1, 3])
        eps_ln = sb("eps_ln", [128, 1])
        eps_rms = sb("eps_rms", [128, 1])

        qT = sb("qT", [128, KD, 4 * T])
        kT = sb("kT", [128, KD, T + TC])
        vv = sb("vv", [KT, NK + 1, H, HD + 1])
        qm = sb("qm", [128, H, T])
        ctxn = sb("ctxn", [KT, NK, D])
        ctxT = sb("ctxT", [128, KD, TC])
        prob = sb("prob", [T, 2, 2, T + TC])
        probT = sb("probT", [KT, 2, NK + 1, T])
        negmax = sb("negmax", [T, H, 2])
        sums = sb("sums", [T, 2, H])
        rden = sb("rden", [T, 2, H])
        o_main = sb("o_main", [T, H, HD])
        o_aux = sb("o_aux", [T, H, HD])
        oT = sb("oT", [128, KD, T])
        xnall = sb("xnall", [128, B, D])
        big = sb("big", [128, 8704])

        def ln_vector(v, n, src, w, nb, dst=None):
            for j in range(nb):
                last = v.bn_stats(stats[:, j, :], src(j))
            last.then_inc(s("ln_stats"), 1)
            v.wait_ge(s("ln_stats"), w + NORMS[n])
            v.memset(tick_v[:], 0.0)
            for j in range(nb):
                last = v.bn_aggr(meanvar[:, j, :], stats[:, j, :])
            last.then_inc(s("ln_meanvar"), 1)
            v.wait_ge(s("ln_rstd"), w + NORMS[n])
            for j in range(nb):
                last = v.tensor_scalar(dst(j) if dst else xn[:, j, :], src(j), meanvar[:, j, 0:1], rstd[:, j:j + 1],
                                       ALU.subtract, ALU.mult)
            last.then_inc(s("ln_xn"), 1)

        def ln_scalar(act, n, w, nb):
            act.wait_ge(s("ln_meanvar"), w + NORMS[n])
            act.activation(logvar[:, 0:nb], meanvar[:, 0:nb, 1], ACT.Ln,
                           bias=eps_ln[0:T, :]).then_inc(s("ln_logvar"), 1)
            act.wait_ge(s("ln_logvar"), w + NORMS[n])
            act.activation(rstd[:, 0:nb], logvar[:, 0:nb], ACT.Exp,
                           scale=-0.5).then_inc(s("ln_rstd"), 1)

        def ln_tensor(pe, n, w, nb, src=xn):
            pe.wait_ge(s("ln_xn"), w + NORMS[n])
            for k in range(KD):
                for j in range(nb):
                    last = pe.transpose(PS[:, k, j * T:(j + 1) * T], src[:, j, k * 128:(k + 1) * 128],
                                        ident[0:T, 0:T])
            last.then_inc(s("ln_tr"), 1)

        def ln_copy(act, n, w, nb):
            act.wait_ge(s("ln_tr"), w + TURNS[n])
            act.activation(xnT[:, :, 0:nb * T], PS[:, 0:KD, 0:nb * T], ACT.Copy).then_inc(s("ln_xnT"), 1)

        def take_wait(gp):
            gp.tensor_tensor(tick_g[:, 0:1], tick_g[:, 1:2], tick_g[:, 2:3], ALU.add)

        def p1_vector(v):
            with v.Fori(0, NG, 1) as g:
                w = g + 1
                if True:
                    ln_vector(v, "a", lambda j: Xg[:, g, j, :], w, G)
                v.wait_ge(s("a_qkv"), w)
                v.tensor_scalar(kT[0:HS, 0, 0:G * T], PS[0:HS, 3, 0:G * T], a_bqk[:, 1:2], None,
                                ALU.add).then_inc(s("a_k"), 1)
                v.tensor_tensor(p1v, PO[0:T, 0, 0:G * HS].rearrange("p (j h) -> p j h", j=G),
                                bcast(a_bv[:], 1, G), ALU.add).then_inc(s("a_v"), 1)
                v.wait_ge(s("a_scores"), w)
                v.scalar_tensor_tensor(out=p1s, in0=PT[0:T, 0, 0:G * T].rearrange("p (j k) -> p j k", j=G),
                                       scalar=HS ** -0.5, in1=bcast(causal[:], 1, G),
                                       op0=ALU.mult, op1=ALU.add).then_inc(s("a_masked"), 1)
                v.wait_ge(s("a_masked"), w)
                v.tensor_reduce(negmax[:, 0:G, 0], p1s, AX.X, ALU.max, negate=True).then_inc(s("a_max"), 1)
                v.wait_ge(s("a_probs"), w)
                v.reciprocal(rden[:, 0, 0:G], sums[:, 0, 0:G]).then_inc(s("a_rden"), 1)
                v.wait_ge(s("a_rden"), w)
                v.wait_ge(s("a_out"), w)
                v.wait_ge(s("a_xb"), w)
                for j in range(G):
                    last = v.scalar_tensor_tensor(out=Xg[:, g, j, :], in0=PS[0:T, j // 2, (j % 2) * D:(j % 2 + 1) * D],
                                                  scalar=rden[:, 0, j:j + 1], in1=Xg[:, g, j, :],
                                                  op0=ALU.mult, op1=ALU.add)
                last.then_inc(s("a_x"), 1)

        def p1_gpsimd(gp):
            with gp.Fori(0, NG, 1) as g:
                gp.wait_ge(s("ln_xn"), g + 1 + NORMS["a"])
                take_wait(gp)
                gp.tensor_tensor(Xg[:, g, :, :], Xg[:, g, :, :], bcast(a_bo[:], 1, G),
                                 ALU.add).then_inc(s("a_xb"), 1)

        def p1_scalar(act):
            with act.Fori(0, NG, 1) as g:
                w = g + 1
                ln_scalar(act, "a", w, G)
                ln_copy(act, "a", w, G)
                act.wait_ge(s("a_qkv"), w)
                act.activation(qT[0:HS, 0, 0:G * T], PS[0:HS, 2, 0:G * T], ACT.Identity,
                               bias=a_bqk[:, 0:1]).then_inc(s("a_q"), 1)
                act.wait_ge(s("a_max"), w)
                for j in range(G):
                    last = act.activation(p1p[:, j, :], p1s[:, j, :], ACT.Exp, bias=negmax[:, j, 0:1],
                                          accum_out=sums[:, 0, j:j + 1])
                last.then_inc(s("a_probs"), 1)
                act.wait_ge(s("a_ptr"), w)
                act.activation(p1pT, PT[0:T, 1, 0:G * T], ACT.Copy).then_inc(s("a_pT"), 1)
                act.wait_ge(s("a_z"), w)
                act.activation(p1z, PO[0:HS, 1, 0:G * T], ACT.Copy).then_inc(s("a_zT"), 1)

        def p1_tensor(pe):
            with pe.Fori(0, NG, 1) as g:
                w = g + 1
                ln_tensor(pe, "a", w, G)
                pe.wait_ge(s("ln_xnT"), w + TURNS["a"])
                for i in range(2):
                    for k in range(KD):
                        pe.matmul(PS[0:HS, 2 + i, 0:G * T], a_wqk[:, k, i, :], xnT[:, k, :],
                                  start=k == 0, stop=k == KD - 1)
                for j in range(G):
                    for k in range(KD):
                        last = pe.matmul(PO[0:T, 0, j * HS:(j + 1) * HS], xnT[:, k, j * T:(j + 1) * T],
                                         a_wv[:, k, :], start=k == 0, stop=k == KD - 1)
                last.then_inc(s("a_qkv"), 1)
                pe.wait_ge(s("a_q"), w)
                pe.wait_ge(s("a_k"), w)
                for j in range(G):
                    last = pe.matmul(PT[0:T, 0, j * T:(j + 1) * T], qT[0:HS, 0, j * T:(j + 1) * T],
                                     kT[0:HS, 0, j * T:(j + 1) * T], start=True, stop=True)
                last.then_inc(s("a_scores"), 1)
                pe.wait_ge(s("a_probs"), w)
                for j in range(G):
                    last = pe.transpose(PT[0:T, 1, j * T:(j + 1) * T], p1p[:, j, :], ident[0:T, 0:T])
                last.then_inc(s("a_ptr"), 1)
                pe.wait_ge(s("a_pT"), w)
                pe.wait_ge(s("a_v"), w)
                for j in range(G):
                    last = pe.matmul(PO[0:HS, 1, j * T:(j + 1) * T], p1v[:, j, :],
                                     p1pT[:, j * T:(j + 1) * T], start=True, stop=True)
                last.then_inc(s("a_z"), 1)
                pe.wait_ge(s("a_zT"), w)
                for j in range(G):
                    last = pe.matmul(PS[0:T, j // 2, (j % 2) * D:(j % 2 + 1) * D],
                                     p1z[:, j * T:(j + 1) * T], a_wo[:], start=True, stop=True)
                last.then_inc(s("a_out"), 1)

        NP = H // 2

        ctx_tiles = a["ctx_1024"].rearrange("b (k p) d -> b p k d", p=KT)

        def ctx_load(sp, n, count):
            with sp.Fori(0, count, 1) as b:
                sp.wait_ge(s("ctx_tr"), b + 1 + CROSS[n])
                sp.dma_start(ctxn[:], ctx_tiles[b + 1]).then_inc(s("ctx"), 16)

        def ctx_tensor(pe, n, b):
            pe.wait_ge(s("ctx"), b * 16 + 16 * (CROSS[n] + 1))
            for k in range(KD):
                for t in range(NK):
                    last = pe.transpose(PS[:, 2 + k, t * KT:(t + 1) * KT], ctxn[:, t, k * 128:(k + 1) * 128],
                                        ident[0:KT, 0:KT])
            last.then_inc(s("ctx_tr"), 1)

        def queries_gpsimd(gp, n, b):
            gp.wait_ge(s("queries"), b + 1 + HEADS[n])
            for m in range(KD):
                last = gp.tensor_tensor(qm[:, m * 8:(m + 1) * 8, :], bcast(qT[:, m, 0:T], 1, 8),
                                        bcast(headmask[:], 2, T), ALU.mult)
            last.then_inc(s("queries_by_head"), 1)

        def project_tensor(pe, n, b, wo, n_o):
            pe.wait_ge(s(n + "_o"), b * n_o + n_o)
            for k in range(KD):
                last = pe.transpose(PT[:, 0, k * T:(k + 1) * T],
                                    o_main[:].rearrange("p h e -> p (h e)")[:, k * 128:(k + 1) * 128], ident[0:T, 0:T])
            last.then_inc(s("heads_otr"), 1)
            pe.wait_ge(s("heads_oT"), b + 1 + HEADS[n])
            for k in range(KD):
                last = pe.matmul(PO[0:T, 0, 0:D], oT[:, k, :], wo[:, k, :], start=k == 0, stop=k == KD - 1)
            last.then_inc(s("heads_out"), 1)

        def project_scalar(act, n, b):
            act.wait_ge(s("heads_otr"), b + 1 + HEADS[n])
            act.activation(oT[:].rearrange("p k t -> p (k t)"), PT[:, 0, 0:KD * T], ACT.Copy).then_inc(s("heads_oT"), 1)

        def residual_vector(v, n, b):
            v.wait_ge(s("heads_out"), b + 1 + HEADS[n])
            v.tensor_tensor(X[:, b, :], PO[0:T, 0, 0:D], X[:, b, :], ALU.add).then_inc(s(n + "_x"), 1)

        def p2_tensor(pe):
            def scores(b, i):
                for e in range(2):
                    h = 2 * i + e
                    last = pe.matmul(PS[0:T, 2 * (i % 2) + e, 0:T + TC], qm[:, h, :], kT[:, h // 8, :],
                                     start=True, stop=True)
                last.then_inc(s("x_scores"), 1)

            def weigh(b, i):
                pe.wait_ge(s("x_pTs"), b * NP + (i + 1))
                pe.wait_ge(s("x_pTv"), b * NP + (i + 1))
                for e in range(2):
                    h = 2 * i + e
                    pe.matmul(PO[0:T, 0, h * HD:(h + 1) * HD], probT[0:T, e, NK, :], vv[0:T, NK, h, 0:HD],
                              start=True, stop=True)
                    for t in range(NK):
                        last = pe.matmul(PO[0:T, 1, h * HD:(h + 1) * HD], probT[:, e, t, :], vv[:, t, h, 0:HD],
                                         start=t == 0, stop=t == NK - 1)
                last.then_inc(s("x_pv"), 1)

            with pe.Fori(0, B, 1) as b:
                w = b + 1
                ln_tensor(pe, "x", w, 1)
                ctx_tensor(pe, "x", b)
                pe.wait_ge(s("ln_xnT"), w + TURNS["x"])
                pe.wait_ge(s("ctxT"), w + CROSS["x"])
                for m in range(KD):
                    for k in range(KD):
                        pe.matmul(PT[:, 0, m * T:(m + 1) * T], x_w[:, k, m * 128:(m + 1) * 128], xnT[:, k, 0:T],
                                  start=k == 0, stop=k == KD - 1)
                for m in range(KD):
                    for k in range(KD):
                        pe.matmul(PS[:, m, 0:T], x_w[:, k, D + m * 128:D + (m + 1) * 128], xnT[:, k, 0:T],
                                  start=k == 0, stop=k == KD - 1)
                    for k in range(KD):
                        last = pe.matmul(PS[:, m, T:T + TC], x_wa[:, k, m * 128:(m + 1) * 128], ctxT[:, k, :],
                                         start=k == 0, stop=k == KD - 1)
                last.then_inc(s("x_qk"), 1)
                for k in range(KD):
                    pe.matmul(PO[0:T, 0, 0:D], xnT[:, k, 0:T], x_w[:, k, 2 * D:3 * D], start=k == 0, stop=k == KD - 1)
                for t in range(NK):
                    dst = PO[0:KT, 1, t * D:(t + 1) * D] if t < 2 else PT[0:KT, 1, 0:D]
                    for k in range(KD):
                        last = pe.matmul(dst, ctxT[:, k, t * KT:(t + 1) * KT], x_wa[:, k, D:2 * D],
                                         start=k == 0, stop=k == KD - 1)
                last.then_inc(s("x_vp"), 1)
                pe.wait_ge(s("x_kT"), w * 2)
                pe.wait_ge(s("queries_by_head"), w + HEADS["x"])
                scores(b, 0)
                scores(b, 1)
                for i in range(NP):
                    pe.wait_ge(s("x_probs"), b * NP + (i + 1))
                    if i == 0:
                        pe.wait_ge(s("x_v"), w)
                    for e in range(2):
                        for t in range(NK):
                            pe.transpose(PT[0:KT, e, t * T:(t + 1) * T],
                                         prob[:, i % 2, e, T + t * KT:T + (t + 1) * KT], ident[0:T, 0:T])
                        last = pe.transpose(PT[0:T, e, NK * T:(NK + 1) * T], prob[:, i % 2, e, 0:T], ident[0:T, 0:T])
                    last.then_inc(s("x_ptr"), 1)
                    if i + 2 < NP:
                        scores(b, i + 2)
                    weigh(b, i)
                project_tensor(pe, "x", b, x_wo, 4)

        def p2_scalar(act):
            with act.Fori(0, B, 1) as b:
                w = b + 1
                ln_scalar(act, "x", w, 1)
                ln_copy(act, "x", w, 1)
                act.wait_ge(s("x_qk"), w)
                for m in range(KD):
                    last = act.activation(qT[:, m, 0:T], PT[:, 0, m * T:(m + 1) * T], ACT.Identity,
                                          bias=x_bqk[:, 0, m:m + 1])
                last.then_inc(s("queries"), 1)
                act.activation(kT[:, 0, 0:T], PS[:, 0, 0:T], ACT.Identity, bias=x_bqk[:, 1, 0:1])
                act.activation(kT[:, 0, T:T + TC], PS[:, 0, T:T + TC], ACT.Identity, bias=x_bka[:, 0:1]).then_inc(s("x_kT"), 1)
                for i in range(NP):
                    act.wait_ge(s("x_max"), b * NP + (i + 1))
                    for e in range(2):
                        for part, (lo, hi) in enumerate(((0, T), (T, T + TC))):
                            last = act.activation(prob[:, i % 2, e, lo:hi], PS[0:T, 2 * (i % 2) + e, lo:hi], ACT.Exp,
                                                  bias=negmax[:, 2 * i + e, part:part + 1],
                                                  accum_out=sums[:, part, 2 * i + e:2 * i + e + 1])
                    last.then_inc(s("x_probs"), 1)
                    act.wait_ge(s("x_ptr"), b * NP + (i + 1))
                    if i > 0:
                        act.wait_ge(s("x_pv"), b * NP + i)
                    act.activation(probT[:, 0, :, :].rearrange("p t q -> p (t q)"), PT[0:KT, 0, 0:(NK + 1) * T],
                                   ACT.Copy).then_inc(s("x_pTs"), 1)
                project_scalar(act, "x", b)

        def p2_vector(v):
            with v.Fori(0, B, 1) as b:
                w = b + 1
                ln_vector(v, "x", lambda j: X[:, b, :], w, 1)
                v.wait_ge(s("ctx_tr"), w + CROSS["x"])
                v.tensor_copy(ctxT[:], PS[:, 2:4, 0:TC]).then_inc(s("ctxT"), 1)
                v.wait_ge(s("x_qk"), w)
                v.tensor_scalar(kT[:, 1, 0:T], PS[:, 1, 0:T], x_bqk[:, 1, 1:2], None, ALU.add)
                v.tensor_scalar(kT[:, 1, T:T + TC], PS[:, 1, T:T + TC], x_bka[:, 1:2], None, ALU.add).then_inc(s("x_kT"), 1)
                v.wait_ge(s("x_vp"), w)
                v.tensor_tensor(vv[0:T, NK, :, 0:HD], PO[0:T, 0, 0:D].rearrange("p (h e) -> p h e", h=H),
                                x_bv[:].rearrange("p (h e) -> p h e", h=H), ALU.add)
                for t in range(NK):
                    src = PO[0:KT, 1, t * D:(t + 1) * D] if t < 2 else PT[0:KT, 1, 0:D]
                    last = v.tensor_tensor(vv[:, t, :, 0:HD], src.rearrange("p (h e) -> p h e", h=H),
                                           x_bva[:].rearrange("p (h e) -> p h e", h=H), ALU.add)
                last.then_inc(s("x_v"), 1)

                def maxima(i):
                    v.wait_ge(s("x_scores"), b * NP + (i + 1))
                    for part, (lo, hi) in enumerate(((0, T), (T, T + TC))):
                        last = v.tensor_reduce(negmax[:, 2 * i:2 * i + 2, part],
                                               PS[0:T, 2 * (i % 2):2 * (i % 2) + 2, lo:hi], AX.X, ALU.max, negate=True)
                    last.then_inc(s("x_max"), 1)

                maxima(0)
                for i in range(NP):
                    if i + 1 < NP:
                        maxima(i + 1)
                    v.wait_ge(s("x_ptr"), b * NP + (i + 1))
                    if i > 0:
                        v.wait_ge(s("x_pv"), b * NP + i)
                    v.tensor_copy(probT[:, 1, :, :].rearrange("p t q -> p (t q)"),
                                  PT[0:KT, 1, 0:(NK + 1) * T]).then_inc(s("x_pTv"), 1)
                v.wait_ge(s("x_probs"), b * NP + NP)
                v.reciprocal(rden[:], sums[:]).then_inc(s("x_o"), 1)
                v.wait_ge(s("x_o"), b * 4 + 1)
                v.tensor_tensor(rden[:], rden[:], x_gate[:], ALU.mult).then_inc(s("x_o"), 1)
                v.wait_ge(s("x_o"), b * 4 + 2)
                v.wait_ge(s("x_pv"), b * NP + NP)
                v.tensor_tensor(o_main[:], PO[0:T, 0, 0:D].rearrange("p (h e) -> p h e", h=H),
                                bcast(rden[:, 0, :], 2, HD), ALU.mult)
                v.tensor_tensor(o_aux[:], PO[0:T, 1, 0:D].rearrange("p (h e) -> p h e", h=H),
                                bcast(rden[:, 1, :], 2, HD), ALU.mult).then_inc(s("x_o"), 1)
                v.wait_ge(s("x_o"), b * 4 + 3)
                v.tensor_tensor(o_main[:], o_main[:], o_aux[:], ALU.add).then_inc(s("x_o"), 1)
                v.wait_ge(s("x_xb"), w)
                residual_vector(v, "x", b)

        def p2_gpsimd(gp):
            with gp.Fori(0, B, 1) as b:
                gp.wait_ge(s("ln_xn"), b + 1 + NORMS["x"])
                take_wait(gp)
                gp.tensor_tensor(X[:, b, :], X[:, b, :], x_bo[:], ALU.add).then_inc(s("x_xb"), 1)
                queries_gpsimd(gp, "x", b)

        def norm_all_vector(v, n):
            with v.Fori(0, NG, 1) as g:
                ln_vector(v, n, lambda j: Xg[:, g, j, :], g + 1, G, dst=lambda j: xnallg[:, g, j, :])

        def norm_all_scalar(act, n):
            with act.Fori(0, NG, 1) as g:
                ln_scalar(act, n, g + 1, G)

        def p3_tensor(pe):
            with pe.Fori(0, NG, 1) as g:
                w = g + 1
                pe.wait_ge(s("f_xs"), w)
                for k in range(KD):
                    for j in range(G):
                        last = pe.transpose(PT[:, k, j * T:(j + 1) * T], xn[:, j, k * 128:(k + 1) * 128],
                                            ident[0:T, 0:T])
                last.then_inc(s("f_tr"), 1)
                pe.wait_ge(s("f_xnT"), w)
                for t in range(NHT):
                    if t >= 4:
                        pe.wait_ge(s("f_h"), g * NHT + (t - 3))
                    for k in range(KD):
                        last = pe.matmul(PS[:, t % 4, 0:G * T], f_up[:, k, t * 128:(t + 1) * 128], xnT[:, k, :],
                                         start=k == 0, stop=k == KD - 1)
                    last.then_inc(s("f_hp"), 1)
                pe.wait_ge(s("f_h"), g * NHT + NHT)
                for j in range(G):
                    if j >= 2:
                        pe.wait_ge(s("f_x"), g * G + (j - 1))
                    for t in range(NHT):
                        last = pe.matmul(PO[0:T, j % 2, 0:D], hT[:, t, j * T:(j + 1) * T], f_down[:, t, :],
                                         start=t == 0, stop=t == NHT - 1)
                    last.then_inc(s("f_y"), 1)

        def p3_scalar(act):
            with act.Fori(0, NG, 1) as g:
                for t in range(NHT):
                    act.wait_ge(s("f_hp"), g * NHT + (t + 1))
                    act.activation(hT[:, t, :], PS[:, t % 4, 0:G * T], ACT.Gelu,
                                   bias=f_hb[:, t:t + 1]).then_inc(s("f_h"), 1)

        def p3_vector(v):
            with v.Fori(0, NG, 1) as g:
                w = g + 1
                v.wait_ge(s("f_tr"), w + 1)
                v.tensor_copy(xnT[:], PT[:, :, 0:G * T]).then_inc(s("f_xnT"), 1)
                v.wait_ge(s("f_xb"), w)
                for j in range(G):
                    v.wait_ge(s("f_y"), g * G + (j + 1))
                    v.tensor_tensor(Xg[:, g, j, :], PO[0:T, j % 2, 0:D], Xg[:, g, j, :], ALU.add).then_inc(s("f_x"), 1)

        def p3_gpsimd(gp):
            gp.sem_inc(s("f_tr"), 1)
            with gp.Fori(0, NG, 1) as g:
                w = g + 1
                gp.wait_ge(s("ln_xn"), w + NORMS["f"])
                gp.wait_ge(s("f_tr"), w)
                take_wait(gp)
                gp.tensor_copy(xn[:], xnallg[:, g, :, :]).then_inc(s("f_xs"), 1)
                gp.tensor_tensor(Xg[:, g, :, :], Xg[:, g, :, :], bcast(f_bo[:], 1, G), ALU.add).then_inc(s("f_xb"), 1)

        NQ = H // 4
        prob4 = prob[:].rearrange("p s e c -> p s (e c)")[:, :, 0:4 * T]
        probT4 = probT[:].rearrange("p s t q -> p s (t q)")

        def p4_tensor(pe):
            def scores(b, i):
                pe.matmul(PS[0:T, i % 2, 0:4 * T], identb[:], causal4[:].rearrange("p h k -> p (h k)"),
                          start=True, stop=False, skip_group_check=True)
                for e in range(4):
                    h = 4 * i + e
                    last = pe.matmul(PS[0:T, i % 2, e * T:(e + 1) * T], qm[:, h, :], kT[:, h // 8, 0:T],
                                     start=False, stop=e == 3, skip_group_check=True)
                last.then_inc(s("r_scores"), 1)

            def weigh(b, i):
                pe.wait_ge(s("r_pT"), b * NQ + (i + 1))
                for e in range(4):
                    h = 4 * i + e
                    last = pe.matmul(PO[0:T, 0, h * HD:(h + 1) * HD], probT4[0:T, i % 2, e * T:(e + 1) * T],
                                     vv[0:T, NK, h, 0:HD], start=True, stop=True)
                last.then_inc(s("r_pv"), 1)

            with pe.Fori(0, B, 1) as b:
                w = b + 1
                ln_tensor(pe, "r", w, 1)
                pe.wait_ge(s("ln_xnT"), w + TURNS["r"])
                for i in range(2 * KD):
                    for r, wt in enumerate((r_w, r_wr)):
                        for k in range(KD):
                            last = pe.matmul(PS[:, 2 + r, i * T:(i + 1) * T], wt[:, k, i * 128:(i + 1) * 128],
                                             xnT[:, k, 0:T], start=k == 0, stop=k == KD - 1)
                last.then_inc(s("r_qk"), 1)
                for k in range(KD):
                    last = pe.matmul(PO[0:T, 1, 0:D], xnT[:, k, 0:T], r_w[:, k, 2 * D:3 * D],
                                     start=k == 0, stop=k == KD - 1)
                last.then_inc(s("r_vp"), 1)
                pe.wait_ge(s("queries"), w + HEADS["r"])
                pe.wait_ge(s("queries_by_head"), w + HEADS["r"])
                scores(b, 0)
                scores(b, 1)
                pe.wait_ge(s("r_v"), w)
                for i in range(NQ):
                    pe.wait_ge(s("r_probs"), b * NQ + (i + 1))
                    for e in range(4):
                        last = pe.transpose(PT[0:T, i % 2, e * T:(e + 1) * T], prob4[:, i % 2, e * T:(e + 1) * T],
                                            ident[0:T, 0:T])
                    last.then_inc(s("r_ptr"), 1)
                    if i + 2 < NQ:
                        scores(b, i + 2)
                    weigh(b, i)
                project_tensor(pe, "r", b, r_wo, 2)

        def p4_scalar(act):
            with act.Fori(0, B, 1) as b:
                w = b + 1
                ln_scalar(act, "r", w, 1)
                ln_copy(act, "r", w, 1)
                act.wait_ge(s("r_vp"), w)
                act.activation(vv[0:T, NK, :, 0:HD], PO[0:T, 1, 0:D].rearrange("p (h e) -> p h e", h=H),
                               ACT.Copy).then_inc(s("r_v"), 1)
                for i in range(NQ):
                    act.wait_ge(s("r_max"), b * NQ + (i + 1))
                    for e in range(4):
                        h = 4 * i + e
                        last = act.activation(prob4[:, i % 2, e * T:(e + 1) * T], PS[0:T, i % 2, e * T:(e + 1) * T],
                                              ACT.Exp, bias=negmax[:, h, 0:1], accum_out=sums[:, 0, h:h + 1])
                    last.then_inc(s("r_probs"), 1)
                    act.wait_ge(s("r_ptr"), b * NQ + (i + 1))
                    act.activation(probT4[0:T, i % 2, :], PT[0:T, i % 2, 0:4 * T], ACT.Copy).then_inc(s("r_pT"), 1)
                project_scalar(act, "r", b)

        def p4_vector(v):
            with v.Fori(0, B, 1) as b:
                w = b + 1
                ln_vector(v, "r", lambda j: X[:, b, :], w, 1)
                v.wait_ge(s("r_qk"), w)
                v.tensor_tensor(rot[:, 0, :, :], PS[:, 2, 0:4 * T].rearrange("p (i t) -> p i t", i=4),
                                bcast(cosq[:], 1, 4), ALU.mult)
                v.tensor_tensor(rot[:, 1, :, :], PS[:, 3, 0:4 * T].rearrange("p (i t) -> p i t", i=4),
                                bcast(sinq[:], 1, 4), ALU.mult).then_inc(s("r_rot"), 1)
                v.wait_ge(s("r_rot"), w)
                v.tensor_tensor(qT[:, :, 0:T], rot[:, 0, 0:2, :], rot[:, 1, 0:2, :], ALU.add)
                v.tensor_tensor(kT[:, :, 0:T], rot[:, 0, 2:4, :], rot[:, 1, 2:4, :], ALU.add).then_inc(s("queries"), 1)
                for i in range(NQ):
                    v.wait_ge(s("r_scores"), b * NQ + (i + 1))
                    v.tensor_reduce(negmax[:, 4 * i:4 * i + 4, 0],
                                    PS[0:T, i % 2, 0:4 * T].rearrange("p (h k) -> p h k", h=4),
                                    AX.X, ALU.max, negate=True).then_inc(s("r_max"), 1)
                v.wait_ge(s("r_probs"), b * NQ + NQ)
                v.reciprocal(rden[:, 0, :], sums[:, 0, :]).then_inc(s("r_o"), 1)
                v.wait_ge(s("r_o"), b * 2 + 1)
                v.wait_ge(s("r_pv"), b * NQ + NQ)
                v.tensor_tensor(o_main[:], PO[0:T, 0, 0:D].rearrange("p (h e) -> p h e", h=H),
                                bcast(rden[:, 0, :], 2, HD), ALU.mult).then_inc(s("r_o"), 1)
                residual_vector(v, "r", b)

        def p4_gpsimd(gp):
            with gp.Fori(0, B, 1) as b:
                queries_gpsimd(gp, "r", b)

        NT5 = NQ * NK
        prob5 = big[:, 0:2 * NK * 4 * T].rearrange("p (s t q) -> p s t q", s=2, t=NK)

        def p5_tensor(pe):
            def scores(b, n):
                i, t = n // NK, n % NK
                pe.matmul(PS[0:KT, n % 4, 0:4 * T], kT[:, i // 2, T + t * KT:T + (t + 1) * KT],
                          qm[:, 4 * i:4 * i + 4, :].rearrange("p h q -> p (h q)"),
                          start=True, stop=True).then_inc(s("c_scores"), 1)

            def weigh(b, i):
                pe.wait_ge(s("c_probs"), b * NT5 + (i + 1) * NK)
                for e in range(4):
                    h = 4 * i + e
                    for t in range(NK):
                        last = pe.matmul(PO[0:T, 0, h * (HD + 1):(h + 1) * (HD + 1)],
                                         prob5[0:KT, i % 2, t, e * T:(e + 1) * T], vv[:, t, h, :],
                                         start=t == 0, stop=t == NK - 1)
                last.then_inc(s("c_pv"), 1)

            with pe.Fori(0, B, 1) as b:
                w = b + 1
                ln_tensor(pe, "c", w, 1)
                ctx_tensor(pe, "c", b)
                pe.wait_ge(s("ln_xnT"), w + TURNS["c"])
                pe.wait_ge(s("ctxT"), w + CROSS["c"])
                for m in range(KD):
                    for k in range(KD):
                        pe.matmul(PS[:, m, 0:T], c_wq[:, k, m * 128:(m + 1) * 128], xnT[:, k, 0:T],
                                  start=k == 0, stop=k == KD - 1)
                    for k in range(KD):
                        last = pe.matmul(PS[:, m, T:T + TC], c_wk[:, k, m * 128:(m + 1) * 128], ctxT[:, k, :],
                                         start=k == 0, stop=k == KD - 1)
                last.then_inc(s("c_qk"), 1)
                for t in range(NK):
                    dst = PO[0:KT, 1, t * D:(t + 1) * D] if t < 2 else PT[0:KT, 1, 0:D]
                    for k in range(KD):
                        last = pe.matmul(dst, ctxT[:, k, t * KT:(t + 1) * KT], c_wv[:, k, :],
                                         start=k == 0, stop=k == KD - 1)
                last.then_inc(s("c_vp"), 1)
                pe.wait_ge(s("c_sq"), w)
                for m in range(KD):
                    last = pe.matmul(PS[:, 2 + m, 0:T + TC], headsum[:], sq[:, m, :], start=True, stop=True)
                last.then_inc(s("c_ss"), 1)
                pe.wait_ge(s("c_v"), w)
                pe.wait_ge(s("c_kT"), w)
                pe.wait_ge(s("queries_by_head"), w + HEADS["c"])
                for n in range(4):
                    scores(b, n)
                for i in range(NQ):
                    for t in range(NK):
                        n = i * NK + t
                        if n + 4 < NT5:
                            pe.wait_ge(s("c_probs"), b * NT5 + (n + 1))
                            scores(b, n + 4)
                    weigh(b, i)

        def p5_scalar(act):
            with act.Fori(0, B, 1) as b:
                w = b + 1
                ln_scalar(act, "c", w, 1)
                ln_copy(act, "c", w, 1)
                act.wait_ge(s("c_qk"), w)
                act.activation(sq[:], PS[:, 0:2, 0:T + TC], ACT.Square).then_inc(s("c_sq"), 1)
                act.wait_ge(s("c_ss"), w)
                act.activation(sq[:], PS[:, 2:4, 0:T + TC], ACT.Ln, scale=1.0 / HD, bias=eps_rms[:]).then_inc(s("c_ln"), 1)
                act.wait_ge(s("c_ln"), w)
                act.activation(sq[:], sq[:], ACT.Exp, scale=-0.5).then_inc(s("c_rs"), 1)
                for n in range(NT5):
                    i, t = n // NK, n % NK
                    act.wait_ge(s("c_scores"), b * NT5 + (n + 1))
                    if t == 0 and i >= 2:
                        act.wait_ge(s("c_pv"), b * NQ + (i - 1))
                    act.activation(prob5[0:KT, i % 2, t, :], PS[0:KT, n % 4, 0:4 * T], ACT.Exp).then_inc(s("c_probs"), 1)

        def p5_vector(v):
            with v.Fori(0, B, 1) as b:
                w = b + 1
                ln_vector(v, "c", lambda j: X[:, b, :], w, 1)
                v.wait_ge(s("ctx_tr"), w + CROSS["c"])
                v.tensor_copy(ctxT[:], PS[:, 2:4, 0:TC]).then_inc(s("ctxT"), 1)
                v.wait_ge(s("c_vp"), w)
                for t in range(NK):
                    src = PO[0:KT, 1, t * D:(t + 1) * D] if t < 2 else PT[0:KT, 1, 0:D]
                    last = v.tensor_copy(vv[:, t, :, 0:HD], src.rearrange("p (h e) -> p h e", h=H))
                last.then_inc(s("c_v"), 1)
                v.wait_ge(s("c_rs"), w)
                v.tensor_tensor(qT[:, :, 0:T], PS[:, 0:2, 0:T], sq[:, :, 0:T], ALU.mult).then_inc(s("queries"), 1)
                v.tensor_tensor(kT[:, :, T:T + TC], PS[:, 0:2, T:T + TC], sq[:, :, T:T + TC], ALU.mult).then_inc(s("c_kT"), 1)
                v.wait_ge(s("c_pv"), b * NQ + NQ)
                o5 = PO[0:T, 0, 0:H * (HD + 1)].rearrange("p (h e) -> p h e", h=H)
                v.reciprocal(rden[:, 0, :], o5[:, :, HD]).then_inc(s("c_o"), 1)
                v.wait_ge(s("c_o"), b * 2 + 1)
                v.tensor_tensor(o_main[:], o5[:, :, 0:HD], bcast(rden[:, 0, :], 2, HD), ALU.mult).then_inc(s("c_o"), 1)
                v.wait_ge(s("c_o"), b * 2 + 2)
                v.tensor_tensor(X[:, b, :], o_main[:].rearrange("p h e -> p (h e)"), X[:, b, :], ALU.add).then_inc(s("c_x"), 1)

        def p5_gpsimd(gp):
            with gp.Fori(0, B, 1) as b:
                queries_gpsimd(gp, "c", b)

        def quantize(v, done, at, src, dst, rs, sc, xr, xa, sg, cc):
            k = [0]

            def step(ins):
                ins.then_inc(done, 1)
                k[0] += 1
                v.wait_ge(done, at + k[0])

            step(v.tensor_reduce(sc, src, AX.X, ALU.max, apply_absolute_value=True))
            step(v.tensor_scalar(sc, sc, 1.0 / 6.0, 1e-12, ALU.mult, ALU.max))
            step(v.reciprocal(rs, sc))
            step(v.tensor_tensor(xr, src, bcast(rs, 2, BLK), ALU.mult))
            v.tensor_scalar(sg, xr, 0.0, None, ALU.is_ge)
            step(v.scalar_tensor_tensor(out=xa, in0=xr, scalar=-1.0, in1=xr, op0=ALU.mult, op1=ALU.max))
            v.tensor_scalar(sg, sg, 2.0, -1.0, ALU.mult, ALU.add)
            v.tensor_scalar(cc, xa, MIDS[6], 4.0, ALU.is_gt, ALU.mult)
            step(v.tensor_scalar(xr, xa, MIDS[5], 2.0, ALU.is_gt, ALU.mult))
            step(v.tensor_tensor(cc, cc, xr, ALU.add))
            step(v.tensor_scalar(xr, xa, MIDS[4], 2.0, ALU.is_gt, ALU.mult))
            step(v.tensor_tensor(cc, cc, xr, ALU.add))
            for m in MIDS[0:4]:
                step(v.scalar_tensor_tensor(out=cc, in0=xa, scalar=m, in1=cc, op0=ALU.is_gt, op1=ALU.add))
            step(v.scalar_tensor_tensor(out=cc, in0=cc, scalar=0.5, in1=sg, op0=ALU.mult, op1=ALU.mult))
            step(v.tensor_tensor(dst, cc, bcast(sc, 2, BLK), ALU.mult))
            return k[0]

        NQB = FF // BLK
        NTD = -(-FF // 128)
        FH = FF // 2
        xq = big[0:T, 0:D]
        gated = big[0:T, 256:256 + FF]
        hid = big[0:T, 1024:1024 + FF]
        qwork = [big[:, 2048 + i * 1024:2048 + (i + 1) * 1024] for i in range(4)]
        hqT = big[:, 6144:6144 + 6 * T].rearrange("p (t q) -> p t q", t=6)
        NQX = 15

        def blocks(ap, n):
            return ap[:, 0:n * BLK].rearrange("p (n e) -> p n e", e=BLK)

        def p6_tensor(pe):
            with pe.Fori(0, B, 1) as b:
                w = b + 1
                pe.wait_ge(s("m_q"), b * (NQX + 1 + NQX) + NQX)
                for k in range(KD):
                    last = pe.transpose(PT[:, 0, k * T:(k + 1) * T], xq[:, k * 128:(k + 1) * 128], ident[0:T, 0:T])
                last.then_inc(s("m_tr"), 1)
                pe.wait_ge(s("m_xT"), w)
                for gu in range(2):
                    for i in range(2):
                        for k in range(KD):
                            last = pe.matmul(PS[0:T, 2 * gu + i, 0:FH], xnT[:, k, 0:T],
                                             m_wgu[:, k, gu, i * FH:(i + 1) * FH], start=k == 0, stop=k == KD - 1)
                last.then_inc(s("m_gu"), 1)
                pe.wait_ge(s("m_q"), b * (NQX + 1 + NQX) + (NQX + 1 + NQX))
                for t in range(NTD):
                    n = min(128, FF - t * 128)
                    last = pe.transpose(PT[0:n, t // 4, (t % 4) * T:(t % 4 + 1) * T], hid[:, t * 128:t * 128 + n],
                                        ident[0:T, 0:T])
                last.then_inc(s("m_htr"), 1)
                pe.wait_ge(s("m_hT"), w)
                for t in range(NTD):
                    n = min(128, FF - t * 128)
                    last = pe.matmul(PO[0:T, 0, 0:D], hqT[0:n, t, :], m_wd[0:n, t, :], start=t == 0, stop=t == NTD - 1)
                last.then_inc(s("m_out"), 1)

        def p6_scalar(act):
            with act.Fori(0, B, 1) as b:
                w = b + 1
                act.wait_ge(s("m_tr"), w)
                act.activation(xnT[:, :, 0:T], PT[:, 0, 0:KD * T].rearrange("p (k t) -> p k t", k=KD),
                               ACT.Copy).then_inc(s("m_xT"), 1)
                act.wait_ge(s("m_gu"), w)
                act.activation(gated.rearrange("p (i n) -> p i n", i=2), PS[0:T, 0:2, 0:FH], ACT.Silu).then_inc(s("m_silu"), 1)
                act.wait_ge(s("m_htr"), w)
                act.activation(hqT[:, 0:4, :], PT[:, 0, 0:4 * T].rearrange("p (t q) -> p t q", t=4), ACT.Copy)
                act.activation(hqT[:, 4:6, :], PT[:, 1, 0:2 * T].rearrange("p (t q) -> p t q", t=2),
                               ACT.Copy).then_inc(s("m_hT"), 1)

        def p6_vector(v):
            with v.Fori(0, B, 1) as b:
                w = b + 1
                at = b * (NQX + 1 + NQX)
                n = quantize(v, s("m_q"), at, xnall[0:T, b, :].rearrange("p (n e) -> p n e", e=BLK), blocks(xq, 16),
                             m_rs[0:T, 0:16], m_sc[0:T, 0:16], *[blocks(q[0:T], 16) for q in qwork])
                assert n == NQX
                v.wait_ge(s("m_silu"), w)
                v.tensor_tensor(hid.rearrange("p (i n) -> p i n", i=2), PS[0:T, 2:4, 0:FH],
                                gated.rearrange("p (i n) -> p i n", i=2), ALU.mult).then_inc(s("m_q"), 1)
                v.wait_ge(s("m_q"), at + (NQX + 1))
                quantize(v, s("m_q"), at + (NQX + 1), blocks(hid, NQB), blocks(hid, NQB),
                         m_rs[0:T, 0:NQB], m_sc[0:T, 0:NQB], *[blocks(q[0:T], NQB) for q in qwork])
                v.wait_ge(s("m_out"), w)
                v.tensor_tensor(X[:, b, :], PO[0:T, 0, 0:D], X[:, b, :], ALU.add).then_inc(s("m_x"), 1)

        NS = 7
        W2 = 2 * NHT
        pair_sel = xnall[0:64, 0:7, :].rearrange("p k (r f) -> p k r f", r=2)
        pong = xnall[:].rearrange("p b d -> p (b d)")[:, 1792:1792 + NHT * (D + 1)].rearrange("p (t d) -> p t d", t=NHT)
        o = 0
        perm = big[:, 0:NS * 256].rearrange("p (k r f) -> p k r f", k=NS, r=2)
        stage = big[:, 1792:1792 + 2048].rearrange("p (u f) -> p u f", u=W2)
        chain = big[:, 3840:3840 + 2048].rearrange("p (u f) -> p u f", u=W2)
        wexpT = big[:, 5888:5888 + NHT * (D + 1)].rearrange("p (t d) -> p t d", t=NHT)
        pair_w = big[0:64, 7944:7944 + NS * W2 * 4].rearrange("p (k u c) -> p k u c", k=NS, u=W2)
        row_w = big[:, 8392:8392 + NS * W2 * 2].rearrange("p (k u c) -> p k u c", k=NS, u=W2)
        raw_r = big[:, 0:8 * D].rearrange("p (m d) -> p m d", m=8)
        raw_gu = big[0:88, 0:4096].rearrange("p (g t d) -> p g t d", g=2, t=8)
        raw_d = xnall[:].rearrange("p b d -> p (b d)")[:, 0:2 * FF].rearrange("p (m k) -> p m k", m=2)
        raw_kv = sb("raw_kv", [128, KD, 2 * D])
        high_w = sb("high_w", [128, 2, 3, 4, 4])
        f_upb = sb("f_upb", [128, NHT])
        m_sc = sb("m_sc", [128, 64])
        swork = [big[:, 4096 + i * 1024:4096 + (i + 1) * 1024] for i in range(4)]

        def setup_loads_1(sp):
            sp.dma_start(f_up[:], a["L0_ffn_W_exp"].rearrange("(k p) n -> p k n", p=128)).then_inc(s("ld_f"), 16)
            sp.dma_start(f_down[:], a["L0_ffn_W_con"].rearrange("(t p) n -> p t n", p=128)).then_inc(s("ld_f"), 16)
            for i, n in enumerate(("up", "down")):
                src = a[f"L0_ffn_{n}_weights"]
                for k in range(NS):
                    sp.dma_start(pair_w[:, k, i * NHT:(i + 1) * NHT, :],
                                 src[k].rearrange("(t p) r c -> p t (r c)", p=64)).then_inc(s("ld_f"), 16)
                for k in range(3):
                    sp.dma_start(high_w[:, i, k, :, :],
                                 src[NS + k].rearrange("(q p) r c -> p q (r c)", p=128)).then_inc(s("ld_f"), 16)
            sp.dma_start(perm, c["perm"]).then_inc(s("ld_f"), 16)
            sp.dma_start(pair_sel, c["pair_sel"]).then_inc(s("ld_f"), 16)
            sp.dma_start(wexpT[:, :, D], a["L0_ffn_b_exp"].rearrange("(t p) -> p t", p=128)).then_inc(s("ld_f"), 16)
            sp.dma_start(f_upb[:], a["L0_ffn_up_bias"].rearrange("(t p) -> p t", p=128)).then_inc(s("ld_f"), 16)
            sp.dma_start(f_bo[:], a["L0_ffn_b_con"].partition_broadcast(T)).then_inc(s("ld_f"), 16)
            sp.dma_start(f_bd[:], a["L0_ffn_down_bias"].partition_broadcast(T)).then_inc(s("ld_f"), 16)

        NF = 2 + 2 * (NS + 3) + 6

        def fold_scalar(act):
            act.wait_ge(s("ld_f"), 16 * NF)
            act.wait_ge(s("row_w"), 1)
            for n, k in enumerate(reversed(range(NS))):
                if n > 0:
                    act.wait_ge(s("chain_mm"), n)
                for u in range(W2):
                    last = act.activation(stage[:, u, :], perm[:, k, 0, :], ACT.Copy, scale=row_w[:, k, u, 0:1])
                last.then_inc(s("stage_a"), 1)
                act.wait_ge(s("chain_mm"), n + 1)
                act.activation(chain, PS[:].rearrange("p b (u f) -> p (b u) f", f=128), ACT.Copy).then_inc(s("chain"), 1)
            act.wait_ge(s("wexp_tr"), 1)
            act.activation(wexpT[:, :, 0:D], PS[:].rearrange("p b (t d) -> p (b t) d", d=D), ACT.Copy).then_inc(s("wexpT"), 1)
            for i in range(2):
                act.wait_ge(s("up_low"), i + 1)
                act.activation(wexpT[:, 4 * i:4 * i + 4, :], PS[:, :, 0:D + 1], ACT.Copy).then_inc(s("up_lowc"), 1)
            act.wait_ge(s("up_tr"), 1)
            act.activation(f_up[:], PS[:].rearrange("p (k i) n -> p k (i n)", k=KD), ACT.Copy).then_inc(s("f_ready"), 1)
            for i in range(2):
                act.wait_ge(s("down_low"), i + 1)
                act.activation(f_down[:, 4 * i:4 * i + 4, :], PS[:, :, 0:D], ACT.Copy).then_inc(s("down_lowc"), 1)

        def fold_tensor(pe):
            pe.wait_ge(s("ld_f"), 16 * NF)
            for k in range(NS):
                for r in range(2):
                    last = pe.matmul(PT[:, 0, k * 32:(k + 1) * 32], pair_sel[:, k, r, :],
                                     pair_w[:, k, :, 2 * r:2 * r + 2], start=r == 0, stop=r == 1)
            last.then_inc(s("row_wp"), 1)
            for n, k in enumerate(reversed(range(NS))):
                pe.wait_ge(s("stage_b"), n + 1)
                if n > 0:
                    pe.wait_ge(s("chain"), n)
                for u in range(W2):
                    before = ident[:] if n == 0 else chain[:, u, :]
                    left, right = stage[:, u, :], before
                    if k == 0 and u >= NHT:
                        left, right = before, stage[:, u, :]
                    last = pe.matmul(PS[:, u // 4, (u % 4) * 128:(u % 4 + 1) * 128], left, right, start=True, stop=True)
                last.then_inc(s("chain_mm"), 1)
            pe.wait_ge(s("chain"), NS)
            for t in range(NHT):
                for k in range(KD):
                    last = pe.transpose(PS[:, t // 2, (t % 2) * D + k * 128:(t % 2) * D + (k + 1) * 128],
                                        f_up[:, k, t * 128:(t + 1) * 128], ident[:])
            last.then_inc(s("wexp_tr"), 1)
            pe.wait_ge(s("wexpT"), 1)
            for i in range(2):
                if i > 0:
                    pe.wait_ge(s("up_lowc"), i)
                for t in range(4 * i, 4 * i + 4):
                    last = pe.matmul(PS[:, t % 4, 0:D + 1], chain[:, t, :], wexpT[:, t, :], start=True, stop=True)
                last.then_inc(s("up_low"), 1)
            pe.wait_ge(s("up_lowc"), 2)
            pe.wait_ge(s("high"), 6)
            for k in range(KD):
                for t in range(NHT):
                    last = pe.transpose(PS[:, 2 * k + t // 4, (t % 4) * 128:(t % 4 + 1) * 128],
                                        pong[:, t, k * 128:(k + 1) * 128], ident[:])
            last.then_inc(s("up_tr"), 1)
            pe.wait_ge(s("f_ready"), 1)
            pe.wait_ge(s("high"), 13)
            for i in range(2):
                if i > 0:
                    pe.wait_ge(s("down_lowc"), i)
                for t in range(4 * i, 4 * i + 4):
                    last = pe.matmul(PS[:, t % 4, 0:D], chain[:, NHT + t, :], pong[:, t, 0:D], start=True, stop=True)
                last.then_inc(s("down_low"), 1)

        def fold_vector(v):
            v.wait_ge(s("ld_f"), 16 * NF)
            v.wait_ge(s("row_wp"), 1)
            v.tensor_copy(row_w, PT[:, 0, 0:NS * 32].rearrange("p (k u c) -> p k u c", k=NS, u=W2)).then_inc(s("row_w"), 1)
            v.wait_ge(s("row_w"), 1)
            for n, k in enumerate(reversed(range(NS))):
                v.wait_ge(s("stage_a"), n + 1)
                for u in range(W2):
                    last = v.scalar_tensor_tensor(out=stage[:, u, :], in0=perm[:, k, 1, :], scalar=row_w[:, k, u, 1:2],
                                                  in1=stage[:, u, :], op0=ALU.mult, op1=ALU.add)
                last.then_inc(s("stage_b"), 1)
            done = [0]

            def high(src, dst, i, k, width):
                pairs = [(lo, lo | 1 << k) for lo in range(NHT) if not lo >> k & 1]

                def coef(q, r, col):
                    at = 2 * r + col if i == 0 else 2 * col + r
                    return high_w[:, i, k, q, at:at + 1]

                for q, ab in enumerate(pairs):
                    for r in range(2):
                        last = v.tensor_scalar(dst[:, ab[r], 0:width], src[:, ab[1], 0:width], coef(q, r, 1), None, ALU.mult)
                last.then_inc(s("high"), 1)
                done[0] += 1
                v.wait_ge(s("high"), done[0])
                for q, ab in enumerate(pairs):
                    for r in range(2):
                        last = v.scalar_tensor_tensor(out=dst[:, ab[r], 0:width], in0=src[:, ab[0], 0:width],
                                                      scalar=coef(q, r, 0), in1=dst[:, ab[r], 0:width],
                                                      op0=ALU.mult, op1=ALU.add)
                last.then_inc(s("high"), 1)
                done[0] += 1
                v.wait_ge(s("high"), done[0])

            v.wait_ge(s("up_lowc"), 2)
            high(wexpT, pong, 0, 0, D + 1)
            high(pong, wexpT, 0, 1, D + 1)
            high(wexpT, pong, 0, 2, D + 1)
            v.tensor_tensor(f_hb[:], pong[:, :, D], f_upb[:], ALU.add).then_inc(s("high"), 1)
            done[0] += 1
            v.wait_ge(s("high"), done[0])
            v.wait_ge(s("up_tr"), 1)
            high(f_down, pong, 1, 2, D)
            high(pong, f_down, 1, 1, D)
            high(f_down, pong, 1, 0, D)

        def setup_loads_2(sp):
            sp.dma_start(raw_kv[:], a["L1_xattn_W_kv"].rearrange("(k p) n -> p k n", p=128)).then_inc(s("ld_r"), 16)
            sp.dma_start(c_wq[:], a["L1_xattn_W_q"].rearrange("(k p) n -> p k n", p=128)).then_inc(s("ld_r"), 16)
            sp.wait_ge(s("down_lowc"), 2)
            sp.dma_start(raw_r[:, 0:6, :], a["L1_attn_qkv_w"].rearrange("(m p) d -> p m d", p=128)).then_inc(s("ld_r"), 16)
            sp.dma_start(raw_r[:, 6:8, :], a["L1_attn_out_w"].rearrange("(m p) d -> p m d", p=128)).then_inc(s("ld_r"), 16)
            sp.dma_start(raw_d, a["L1_ffn_w_down"].rearrange("(m p) k -> p m k", p=128)).then_inc(s("ld_d"), 16)
            sp.wait_ge(s("r_wtr"), 1)
            for i, n in enumerate(("gate", "up")):
                sp.dma_start(raw_gu[:, i, :, :], a["L1_ffn_w_" + n].rearrange("(t p) d -> p t d", p=88)).then_inc(s("ld_d"), 16)

        def weights_tensor(pe):
            pe.wait_ge(s("ld_r"), 64)
            pe.wait_ge(s("down_lowc"), 2)
            for k in range(KD):
                for m in range(8):
                    last = pe.transpose(PS[:, 2 * k + m // 4, (m % 4) * 128:(m % 4 + 1) * 128],
                                        raw_r[:, m, k * 128:(k + 1) * 128], ident[:])
            last.then_inc(s("r_wtr"), 1)
            for i in range(2):
                pe.wait_ge(s("m_wcopy"), i + 1)
                pe.wait_ge(s("m_wq"), NQX * 2 * (i + 1))
                for k in range(KD):
                    for t in range(8):
                        last = pe.transpose(PS[:, 2 * k + t // 4, (t % 4) * 88:(t % 4 + 1) * 88],
                                            raw_gu[:, i, t, k * 128:(k + 1) * 128], ident[0:88, 0:88])
                last.then_inc(s("m_wtr"), 1)
            pe.wait_ge(s("m_wcopy"), 3)
            pe.wait_ge(s("m_wq"), NQX * 6)
            for t in range(NTD):
                n = min(128, FF - t * 128)
                for m in range(2):
                    last = pe.transpose(PS[0:n, t // 2, (t % 2) * D + m * 128:(t % 2) * D + (m + 1) * 128],
                                        raw_d[:, m, t * 128:t * 128 + n], ident[:])
            last.then_inc(s("m_wtr"), 1)

        def weights_vector(v):
            v.memset(vv[:, :, :, HD:HD + 1], 1.0).then_inc(s("consts2"), 1)
            v.wait_ge(s("consts2"), 1)
            v.wait_ge(s("r_wtr"), 1)
            for k in range(KD):
                v.tensor_copy(r_w[:, k, 0:512], PS[:, 2 * k, :])
                v.tensor_copy(r_w[:, k, 512:768], PS[:, 2 * k + 1, 0:256])
                last = v.tensor_copy(r_wo[:, k, :], PS[:, 2 * k + 1, 256:512])
            last.then_inc(s("m_wcopy"), 1)
            v.wait_ge(s("m_wcopy"), 1)
            for k in range(KD):
                pairs = r_w[:, k, 0:512].rearrange("p (n e) -> p n e", e=2)
                turned = r_wr[:, k, :].rearrange("p (n e) -> p n e", e=2)
                v.tensor_scalar(turned[:, :, 0], pairs[:, :, 1], -1.0, None, ALU.mult)
                v.tensor_copy(turned[:, :, 1], pairs[:, :, 0])
            v.wait_ge(s("ld_r"), 64)
            v.tensor_copy(c_wk[:], raw_kv[:].rearrange("p k (n e) -> p k n e", e=2)[:, :, :, 0])
            v.tensor_copy(c_wv[:], raw_kv[:].rearrange("p k (n e) -> p k n e", e=2)[:, :, :, 1]).then_inc(s("w_done"), 1)
            v.wait_ge(s("ld_d"), 48)
            at = 0
            for i in range(2):
                for half in range(2):
                    src = raw_gu[:, i, 4 * half:4 * half + 4, :].rearrange("p t (n e) -> p (t n) e", e=BLK)
                    at += quantize(v, s("m_wq"), at, src, src, m_rs[0:88, 0:64], m_sc[0:88, :],
                                   *[blocks(q[0:88], 64) for q in swork])
            for m in range(2):
                src = raw_d[:, m, :].rearrange("p (n e) -> p n e", e=BLK)
                at += quantize(v, s("m_wq"), at, src, src, m_rs[:, 0:NQB], m_sc[:, 0:NQB],
                               *[blocks(q, NQB) for q in swork])
            for i in range(2):
                v.wait_ge(s("m_wtr"), i + 1)
                for k in range(KD):
                    for j in range(2):
                        last = v.tensor_copy(m_wgu[:, k, i, j * FH:(j + 1) * FH], PS[:, 2 * k + j, 0:FH])
                last.then_inc(s("m_wcopy"), 1)
            v.wait_ge(s("m_wtr"), 3)
            v.tensor_copy(m_wd[:, 0:4, :], PS[:, 0:2, :].rearrange("p b (t n) -> p (b t) n", n=D))
            v.tensor_copy(m_wd[:, 4, :], PS[:, 2, 0:D])
            v.tensor_copy(m_wd[0:64, 5, :], PS[0:64, 2, D:2 * D]).then_inc(s("w_done"), 1)

        Xg = X[:].rearrange("p (g j) d -> p g j d", j=G)
        xnallg = xnall[0:T].rearrange("p (g j) d -> p g j d", j=G)
        hT = big[:, 0:NHT * G * T].rearrange("p (t q) -> p t q", t=NHT)
        rot = big[:, 0:2 * 4 * T].rearrange("p (r i t) -> p r i t", r=2, i=4)
        sq = sb("sq", [128, KD, T + TC])
        p1v = sb("p1v", [T, G, HS])[:]
        p1s = sb("p1s", [T, G, T])[:]
        p1p = sb("p1p", [T, G, T])
        p1pT = sb("p1pT", [T, G * T])[:]
        p1z = sb("p1z", [HS, G * T])[:]

        NCONST, NW = 6, 10
        block = ctx.enter_context(nc.Block())

        @block.sync
        def _(sp):
            with nc.allow_non_contiguous_dma(reason="small biases, feature on partition"):
                sp.dma_start(X[:], a["x"].rearrange("b t d -> t b d")).then_inc(s("ld_x"), 16)
                for i, n in enumerate(("wq", "wk")):
                    sp.dma_start(a_wqk[:, :, i, :], a["L0_attn_" + n].rearrange("(k p) h -> p k h", p=128)).then_inc(s("ld_a"), 16)
                sp.dma_start(a_wv[:], a["L0_attn_wv"].rearrange("(k p) h -> p k h", p=128)).then_inc(s("ld_a"), 16)
                sp.dma_start(a_wo[:], a["L0_attn_wo"]).then_inc(s("ld_a"), 16)
                sp.dma_start(a_bqk[:, 0:1], a["L0_attn_bq"].unsqueeze(1)).then_inc(s("ld_a"), 16)
                sp.dma_start(a_bqk[:, 1:2], a["L0_attn_bk"].unsqueeze(1)).then_inc(s("ld_a"), 16)
                sp.dma_start(a_bv[:], a["L0_attn_bv"].partition_broadcast(T)).then_inc(s("ld_a"), 16)
                sp.dma_start(a_bo[:], a["L0_attn_bo"].partition_broadcast(T)).then_inc(s("ld_a"), 16)
                for t, src in ((x_w, a["L0_xattn_Wqkv"]), (x_wa, a["L0_xattn_Wqkv_aux"][:, D:3 * D]), (x_wo, a["L0_xattn_Wo"])):
                    sp.dma_start(t[:], src.rearrange("(k p) n -> p k n", p=128)).then_inc(s("ld_w"), 16)
                for i in range(2):
                    sp.dma_start(x_bqk[:, i, :], a["L0_xattn_bqkv"][i * D:(i + 1) * D].rearrange("(m p) -> p m", p=128)).then_inc(s("ld_w"), 16)
                sp.dma_start(x_bka[:], a["L0_xattn_bqkv_aux"][D:2 * D].rearrange("(m p) -> p m", p=128)).then_inc(s("ld_w"), 16)
                sp.dma_start(x_bv[:], a["L0_xattn_bqkv"][2 * D:3 * D].partition_broadcast(T)).then_inc(s("ld_w"), 16)
                sp.dma_start(x_bva[:], a["L0_xattn_bqkv_aux"][2 * D:3 * D].partition_broadcast(KT)).then_inc(s("ld_w"), 16)
                sp.dma_start(x_bo[:], a["L0_xattn_bo"].partition_broadcast(T)).then_inc(s("ld_w"), 16)
                sp.dma_start(x_g[:], a["L0_xattn_g"].partition_broadcast(T)).then_inc(s("ld_w"), 16)
                setup_loads_1(sp)
                setup_loads_2(sp)
            sp.dma_start(ctxn[:], ctx_tiles[0]).then_inc(s("ctx"), 16)
            ctx_load(sp, "x", B - 1)
            sp.wait_ge(s("ctx_tr"), B)
            sp.dma_start(ctxn[:], ctx_tiles[0]).then_inc(s("ctx"), 16)
            ctx_load(sp, "c", B - 1)
            sp.wait_ge(s(FINAL[parts][0]), FINAL[parts][1])
            sp.dma_start(out.rearrange("b t d -> t b d"), X[:]).then_inc(s("stored"), 16)
            sp.wait_ge(s("stored"), 16)

        @block.gpsimd
        def _(gp):
            gp.memset(tick_g[:], 0.0).then_inc(s("tick"), 1)
            gp.wait_ge(s("tick"), 1)
            for t, n in ((ident, "ident"), (causal, "causal"), (headmask, "headmask"), (headsum, "headsum")):
                gp.dma_start(t[:], c[n]).then_inc(s("ld_c"), 16)
            gp.dma_start(cosq[:], c["cos"]).then_inc(s("ld_c"), 16)
            gp.dma_start(sinq[:], c["sin"]).then_inc(s("ld_c"), 16)
            gp.wait_ge(s("ld_a"), 16 * 8)
            gp.wait_ge(s("ld_c"), 16 * NCONST)
            gp.wait_ge(s("ld_w"), 16 * NW)
            gp.wait_ge(s("ld_f"), 16 * NF)
            gp.tensor_tensor(f_bo[:], f_bo[:], f_bd[:], ALU.add).then_inc(s("f_bias"), 1)
            p1_gpsimd(gp)
            p2_gpsimd(gp)
            gp.wait_ge(s("f_bias"), 1)
            p3_gpsimd(gp)
            p4_gpsimd(gp)
            p5_gpsimd(gp)

        @block.scalar
        def _(act):
            act.wait_ge(s("ld_a"), 16 * 8)
            act.wait_ge(s("ld_w"), 16 * NW)
            act.wait_ge(s("consts"), 3)
            act.preload_act_table_set("natural_log_exp_and_others")
            act.activation(x_gate[:, 1, :], x_g[:], ACT.Exp, scale=-1.0).then_inc(s("gate_exp"), 1)
            fold_scalar(act)
            p1_scalar(act)
            p2_scalar(act)
            norm_all_scalar(act, "f")
            act.preload_act_table(ACT.Gelu)
            p3_scalar(act)
            act.preload_act_table_set("natural_log_exp_and_others")
            p4_scalar(act)
            p5_scalar(act)
            norm_all_scalar(act, "m")
            act.preload_act_table(ACT.Silu)
            p6_scalar(act)

        @block.vector
        def _(v):
            v.memset(eps_ln[:], LN_EPS).then_inc(s("consts"), 1)
            v.memset(eps_rms[:], RMS_EPS).then_inc(s("consts"), 1)
            v.memset(PT[:], 0.0).then_inc(s("consts"), 1)
            v.wait_ge(s("ld_x"), 16)
            v.wait_ge(s("ld_a"), 16 * 8)
            v.wait_ge(s("ld_c"), 16 * NCONST)
            v.wait_ge(s("ld_w"), 16 * NW)
            v.tensor_copy(identb[:], ident[0:T, 0:T]).then_inc(s("consts"), 1)
            v.tensor_scalar(causal4[:], bcast(causal[:], 1, 4), 1e19, None, ALU.mult).then_inc(s("consts"), 1)
            v.wait_ge(s("gate_exp"), 1)
            v.tensor_scalar(x_gate[:, 1, :], x_gate[:, 1, :], 1.0, None, ALU.add).then_inc(s("gate"), 1)
            v.wait_ge(s("gate"), 1)
            v.reciprocal(x_gate[:, 1, :], x_gate[:, 1, :]).then_inc(s("gate"), 1)
            v.wait_ge(s("gate"), 2)
            v.tensor_scalar(x_gate[:, 0, :], x_gate[:, 1, :], -1.0, 1.0, ALU.mult, ALU.add).then_inc(s("gate"), 1)
            fold_vector(v)
            weights_vector(v)
            v.wait_ge(s("w_done"), 2)
            p1_vector(v)
            v.wait_ge(s("gate"), 3)
            p2_vector(v)
            v.wait_ge(s("x_x"), B)
            norm_all_vector(v, "f")
            p3_vector(v)
            v.wait_ge(s("f_x"), B)
            p4_vector(v)
            v.wait_ge(s("r_x"), B)
            p5_vector(v)
            v.wait_ge(s("c_x"), B)
            norm_all_vector(v, "m")
            v.wait_ge(s("ln_xn"), NG + NORMS["m"])
            p6_vector(v)

        @block.tensor
        def _(pe):
            pe.wait_ge(s("ld_a"), 16 * 8)
            pe.wait_ge(s("ld_c"), 16 * NCONST)
            pe.wait_ge(s("ld_w"), 16 * NW)
            pe.wait_ge(s("consts"), 5)
            fold_tensor(pe)
            weights_tensor(pe)
            p1_tensor(pe)
            p2_tensor(pe)
            p3_tensor(pe)
            p4_tensor(pe)
            p5_tensor(pe)
            p6_tensor(pe)


def constants():
    import numpy as np
    c = {}
    c["ident"] = np.eye(128, dtype=np.float32)
    up = np.triu(np.ones((T, T), np.float32), 1)
    c["causal"] = up * np.float32(-1e11)
    head = np.arange(128) // HD
    c["headmask"] = (head[:, None] == np.arange(8)[None, :]).astype(np.float32) * np.float32(HD ** -0.5)
    c["headsum"] = (head[:, None] == head[None, :]).astype(np.float32)
    freq = 1.0 / np.float32(10000.0) ** (np.arange(0, HD, 2, dtype=np.float32) / np.float32(HD))
    angle = np.outer(np.arange(T, dtype=np.float32), freq.astype(np.float32)).astype(np.float32)
    rows = angle.T[(np.arange(128) % HD) % (HD // 2)]
    c["cos"], c["sin"] = np.cos(rows).astype(np.float32), np.sin(rows).astype(np.float32)
    p = np.arange(128)
    perm, sel = np.zeros((128, 7, 2, 128), np.float32), np.zeros((64, 7, 2, 128), np.float32)
    for k in range(7):
        perm[p, k, 0, p & ~(1 << k)] = 1
        perm[p, k, 1, p | (1 << k)] = 1
        sel[((p >> (k + 1)) << k) + (p & ((1 << k) - 1)), k, (p >> k) & 1, p] = 1
    c["perm"], c["pair_sel"] = perm, sel
    return c


def kernel(**inputs):
    import numpy as _np
    import concourse.bacc as _bacc
    from concourse import mybir as _mybir
    from concourse.bass_utils import run_bass_kernel_spmd as _run

    nc = _bacc.Bacc("TRN2", target_bir_lowering=False, num_devices=1)
    arrays, args, consts = {}, {}, {}
    for name, value in inputs.items():
        v = _np.ascontiguousarray(value)
        arrays[f"in_{name}"] = v
        args[name] = nc.dram_tensor(f"in_{name}", v.shape, _mybir.dt.from_np(v.dtype), kind="ExternalInput").ap()
    for name, v in constants().items():
        arrays[f"const_{name}"] = v
        consts[name] = nc.dram_tensor(f"const_{name}", v.shape, _mybir.dt.from_np(v.dtype), kind="ExternalInput").ap()
    out = nc.dram_tensor("out", (B, T, D), F32, kind="ExternalOutput").ap()
    build(nc, args, consts, out)
    r = _run(nc, [arrays], core_ids=[0])
    return r.results[0]["out"]
```

```python
from contextlib import ExitStack

import concourse.bass as bass
from concourse import mybir

F32 = mybir.dt.float32
BF16 = mybir.dt.bfloat16
I32 = mybir.dt.int32
ACT = mybir.ActivationFunctionType
ALU = mybir.AluOpType
AX = mybir.AxisListType

B, T, D = 16, 112, 256
TC, KT = 375, 125
NK = TC // KT
KD = D // 128
G = 4
NG = B // G
H, HD = 16, 16
HS = 64
HID = 1024
NHT = HID // 128
FF = 704
BLK = 16
LN_EPS = 1e-5
RMS_EPS = 1e-6
MIDS = (0.25, 0.75, 1.25, 1.75, 2.5, 3.5, 5.0)


FINAL = {1: ("a_x", NG), 2: ("x_x", B), 3: ("f_x", B), 4: ("r_x", B), 5: ("c_x", B), 6: ("m_x", B + 1)}

NORMS = {n: i * NG for i, n in enumerate("axfrcm")}
TURNS = {"a": 0}
HEADS = {"x": 0}


class Sems:

    def __init__(self, nc, ctx):
        self.nc, self.ctx, self.made = nc, ctx, {}

    def __call__(self, name):
        if name not in self.made:
            self.made[name] = self.ctx.enter_context(self.nc.semaphore(name))
        return self.made[name]


def bcast(ap, dim, n):
    shape = list(ap.shape)
    shape.insert(dim, n)
    return ap.unsqueeze(dim).broadcast_to(shape)


def build(nc, a, c, out, parts=6):
    with ExitStack() as ctx:
        def sb(name, shape, dt=F32):
            return ctx.enter_context(nc.sbuf_tensor(name, shape, dt))

        def ps(name, shape, dt=F32):
            return ctx.enter_context(nc.psum_tensor(name, shape, dt))

        s = Sems(nc, ctx)

        PS = ps("PS", [128, 4, 512])
        PT = ps("PT", [128, 2, 512])
        PO = ps("PO", [128, 2, 512])

        X = sb("X", [T, B, D])
        ident = sb("ident", [128, 128])
        identb = sb("identb", [T, T], BF16)
        causal = sb("causal", [T, T])
        causal4 = sb("causal4", [T, 4, T], BF16)
        headmask = sb("headmask", [128, 8])
        headsum = sb("headsum", [128, 128])
        cosq = sb("cosq", [128, T])
        sinq = sb("sinq", [128, T])

        a_wqk = sb("a_wqk", [128, KD, 2, HS])
        a_wv = sb("a_wv", [128, KD, HS])
        a_wo = sb("a_wo", [HS, D])
        a_bqk = sb("a_bqk", [HS, 2])
        a_bv = sb("a_bv", [T, HS])
        a_bo = sb("a_bo", [T, D])
        x_w = sb("x_w", [128, KD, 3 * D])
        x_wa = sb("x_wa", [128, KD, 2 * D])
        x_wo = sb("x_wo", [128, KD, D])
        x_bqk = sb("x_bqk", [128, 2, KD])
        x_bka = sb("x_bka", [128, KD])
        x_bv = sb("x_bv", [T, D])
        x_bva = sb("x_bva", [KT, D])
        x_bo = sb("x_bo", [T, D])
        x_g = sb("x_g", [T, H])
        x_gate = sb("x_gate", [T, 2, H])

        f_up = sb("f_up", [128, KD, HID])
        f_down = sb("f_down", [128, NHT, D])
        f_hb = sb("f_hb", [128, NHT])
        f_bo = sb("f_bo", [T, D])
        f_bd = sb("f_bd", [T, D])
        r_w = sb("r_w", [128, KD, 3 * D])
        r_wr = sb("r_wr", [128, KD, 2 * D])
        r_wo = sb("r_wo", [128, KD, D])
        c_wq = sb("c_wq", [128, KD, D])
        c_wk = sb("c_wk", [128, KD, D])
        c_wv = sb("c_wv", [128, KD, D])
        m_wgu = sb("m_wgu", [128, KD, 2, FF])
        m_wd = sb("m_wd", [128, 6, D])
        m_rs = sb("m_rs", [128, 64])

        stats = sb("stats", [T, G, 6])
        meanvar = sb("meanvar", [T, G, 2])
        logvar = sb("logvar", [T, G])
        rstd = sb("rstd", [T, G])
        xn = sb("xn", [T, G, D])
        xnT = sb("xnT", [128, KD, G * T])
        tick_v = sb("tick_v", [1, 1])
        tick_g = sb("tick_g", [1, 3])
        eps_ln = sb("eps_ln", [128, 1])
        eps_rms = sb("eps_rms", [128, 1])

        qT = sb("qT", [128, KD, 4 * T])
        kT = sb("kT", [128, KD, T + TC])
        vv = sb("vv", [KT, NK + 1, H, HD + 1])
        qm = sb("qm", [128, H, T])
        ctxn = sb("ctxn", [KT, NK, D])
        ctxT = sb("ctxT", [128, KD, TC])
        prob = sb("prob", [T, 2, 2, T + TC])
        probT = sb("probT", [KT, 2, NK + 1, T])
        negmax = sb("negmax", [T, H, 2])
        sums = sb("sums", [T, 2, 2, H])
        rden = sb("rden", [T, 2, H])
        o_main = sb("o_main", [T, H, HD])
        o_aux = sb("o_aux", [T, H, HD])
        oT = sb("oT", [128, KD, T])
        xnall = sb("xnall", [128, B, D])
        big = sb("big", [128, 8704])

        o = 2 * 3 * 4 * T
        qm_b = big[:, o:o + H * T].rearrange("p (h t) -> p h t", h=H)
        o += H * T
        kT_b = big[:, o:o + KD * (T + TC)].rearrange("p (k t) -> p k t", k=KD)
        o += KD * (T + TC)
        vv_b = big[0:KT, o:o + (NK + 1) * H * (HD + 1)].rearrange("p (t h e) -> p t h e", t=NK + 1, h=H)
        o += (NK + 1) * H * (HD + 1)
        rms = big[:, o:o + KD * (T + TC)].rearrange("p (k t) -> p k t", k=KD)

        def ln_vector(v, n, src, w, nb, dst=None):
            for j in range(nb):
                last = v.bn_stats(stats[:, j, :], src(j))
            last.then_inc(s("ln_stats"), 1)
            v.wait_ge(s("ln_stats"), w + NORMS[n])
            v.memset(tick_v[:], 0.0)
            for j in range(nb):
                last = v.bn_aggr(meanvar[:, j, :], stats[:, j, :])
            last.then_inc(s("ln_meanvar"), 1)
            v.wait_ge(s("ln_rstd"), w + NORMS[n])
            for j in range(nb):
                last = v.tensor_scalar(dst(j) if dst else xn[:, j, :], src(j), meanvar[:, j, 0:1], rstd[:, j:j + 1],
                                       ALU.subtract, ALU.mult)
            last.then_inc(s("ln_xn"), 1)

        def ln_scalar(act, n, w, nb):
            act.wait_ge(s("ln_meanvar"), w + NORMS[n])
            act.activation(logvar[:, 0:nb], meanvar[:, 0:nb, 1], ACT.Ln,
                           bias=eps_ln[0:T, :]).then_inc(s("ln_logvar"), 1)
            act.wait_ge(s("ln_logvar"), w + NORMS[n])
            act.activation(rstd[:, 0:nb], logvar[:, 0:nb], ACT.Exp,
                           scale=-0.5).then_inc(s("ln_rstd"), 1)

        def ln_tensor(pe, n, w, nb, src=xn):
            pe.wait_ge(s("ln_xn"), w + NORMS[n])
            for k in range(KD):
                for j in range(nb):
                    last = pe.transpose(PS[:, k, j * T:(j + 1) * T], src[:, j, k * 128:(k + 1) * 128],
                                        ident[0:T, 0:T])
            last.then_inc(s("ln_tr"), 1)

        def ln_copy(act, n, w, nb):
            act.wait_ge(s("ln_tr"), w + TURNS[n])
            act.activation(xnT[:, :, 0:nb * T], PS[:, 0:KD, 0:nb * T], ACT.Copy).then_inc(s("ln_xnT"), 1)

        def take_wait(gp):
            gp.tensor_tensor(tick_g[:, 0:1], tick_g[:, 1:2], tick_g[:, 2:3], ALU.add)

        def p1_vector(v):
            with v.Fori(0, NG, 1) as g:
                w = g + 1
                if True:
                    ln_vector(v, "a", lambda j: Xg[:, g, j, :], w, G)
                v.wait_ge(s("a_qkv"), w)
                v.tensor_scalar(kT[0:HS, 0, 0:G * T], PS[0:HS, 3, 0:G * T], a_bqk[:, 1:2], None,
                                ALU.add).then_inc(s("a_k"), 1)
                v.tensor_tensor(p1v, PO[0:T, 0, 0:G * HS].rearrange("p (j h) -> p j h", j=G),
                                bcast(a_bv[:], 1, G), ALU.add).then_inc(s("a_v"), 1)
                v.wait_ge(s("a_scores"), w)
                v.scalar_tensor_tensor(out=p1s, in0=PT[0:T, 0, 0:G * T].rearrange("p (j k) -> p j k", j=G),
                                       scalar=HS ** -0.5, in1=bcast(causal[:], 1, G),
                                       op0=ALU.mult, op1=ALU.add).then_inc(s("a_masked"), 1)
                v.wait_ge(s("a_masked"), w)
                v.tensor_reduce(negmax[:, 0:G, 0], p1s, AX.X, ALU.max, negate=True).then_inc(s("a_max"), 1)
                v.wait_ge(s("a_probs"), w)
                v.reciprocal(rden[:, 0, 0:G], sums[:, 0, 0, 0:G]).then_inc(s("a_rden"), 1)
                v.wait_ge(s("a_rden"), w)
                v.wait_ge(s("a_out"), w)
                v.wait_ge(s("a_xb"), w)
                for j in range(G):
                    last = v.scalar_tensor_tensor(out=Xg[:, g, j, :], in0=PS[0:T, j // 2, (j % 2) * D:(j % 2 + 1) * D],
                                                  scalar=rden[:, 0, j:j + 1], in1=Xg[:, g, j, :],
                                                  op0=ALU.mult, op1=ALU.add)
                last.then_inc(s("a_x"), 1)

        def p1_gpsimd(gp):
            with gp.Fori(0, NG, 1) as g:
                gp.wait_ge(s("ln_xn"), g + 1 + NORMS["a"])
                take_wait(gp)
                gp.tensor_tensor(Xg[:, g, :, :], Xg[:, g, :, :], bcast(a_bo[:], 1, G),
                                 ALU.add).then_inc(s("a_xb"), 1)

        def p1_scalar(act):
            with act.Fori(0, NG, 1) as g:
                w = g + 1
                ln_scalar(act, "a", w, G)
                ln_copy(act, "a", w, G)
                act.wait_ge(s("a_qkv"), w)
                act.activation(qT[0:HS, 0, 0:G * T], PS[0:HS, 2, 0:G * T], ACT.Identity,
                               bias=a_bqk[:, 0:1]).then_inc(s("a_q"), 1)
                act.wait_ge(s("a_max"), w)
                for j in range(G):
                    last = act.activation(p1p[:, j, :], p1s[:, j, :], ACT.Exp, bias=negmax[:, j, 0:1],
                                          accum_out=sums[:, 0, 0, j:j + 1])
                last.then_inc(s("a_probs"), 1)
                act.wait_ge(s("a_ptr"), w)
                act.activation(p1pT, PT[0:T, 1, 0:G * T], ACT.Copy).then_inc(s("a_pT"), 1)
                act.wait_ge(s("a_z"), w)
                act.activation(p1z, PO[0:HS, 1, 0:G * T], ACT.Copy).then_inc(s("a_zT"), 1)

        def p1_tensor(pe):
            with pe.Fori(0, NG, 1) as g:
                w = g + 1
                ln_tensor(pe, "a", w, G)
                pe.wait_ge(s("ln_xnT"), w + TURNS["a"])
                for i in range(2):
                    for k in range(KD):
                        pe.matmul(PS[0:HS, 2 + i, 0:G * T], a_wqk[:, k, i, :], xnT[:, k, :],
                                  start=k == 0, stop=k == KD - 1)
                for j in range(G):
                    for k in range(KD):
                        last = pe.matmul(PO[0:T, 0, j * HS:(j + 1) * HS], xnT[:, k, j * T:(j + 1) * T],
                                         a_wv[:, k, :], start=k == 0, stop=k == KD - 1)
                last.then_inc(s("a_qkv"), 1)
                pe.wait_ge(s("a_q"), w)
                pe.wait_ge(s("a_k"), w)
                for j in range(G):
                    last = pe.matmul(PT[0:T, 0, j * T:(j + 1) * T], qT[0:HS, 0, j * T:(j + 1) * T],
                                     kT[0:HS, 0, j * T:(j + 1) * T], start=True, stop=True)
                last.then_inc(s("a_scores"), 1)
                pe.wait_ge(s("a_probs"), w)
                for j in range(G):
                    last = pe.transpose(PT[0:T, 1, j * T:(j + 1) * T], p1p[:, j, :], ident[0:T, 0:T])
                last.then_inc(s("a_ptr"), 1)
                pe.wait_ge(s("a_pT"), w)
                pe.wait_ge(s("a_v"), w)
                for j in range(G):
                    last = pe.matmul(PO[0:HS, 1, j * T:(j + 1) * T], p1v[:, j, :],
                                     p1pT[:, j * T:(j + 1) * T], start=True, stop=True)
                last.then_inc(s("a_z"), 1)
                pe.wait_ge(s("a_zT"), w)
                for j in range(G):
                    last = pe.matmul(PS[0:T, j // 2, (j % 2) * D:(j % 2 + 1) * D],
                                     p1z[:, j * T:(j + 1) * T], a_wo[:], start=True, stop=True)
                last.then_inc(s("a_out"), 1)

        NP = H // 2

        ctx_tiles = a["ctx_1024"].rearrange("b (k p) d -> b p k d", p=KT)

        def ctx_load(sp, read, each, at):
            with sp.Fori(0, B - 1, 1) as b:
                sp.wait_ge(s(read), b * each + at)
                sp.dma_start(ctxn[:], ctx_tiles[b + 1]).then_inc(s("ctx"), 16)

        def queries_gpsimd(gp, n, b, qm=qm):
            gp.wait_ge(s("queries"), b + 1 + HEADS[n])
            for m in range(KD):
                last = gp.tensor_tensor(qm[:, m * 8:(m + 1) * 8, :], bcast(qT[:, m, 0:T], 1, 8),
                                        bcast(headmask[:], 2, T), ALU.mult)
            last.then_inc(s("queries_by_head"), 1)

        def fills(r, i):
            if isinstance(r, int) and r >= B:
                return B * NP + 2 * (r - B) + (i - 1)
            return r * NP + (i + 1)

        def rounds(engine, body):
            body(0, 1, True, False, False)
            body(1, 0, True, True, False)
            with engine.Fori(2, B, 2) as r:
                body(r, 1, True, True, True)
                body(r + 1, 0, True, True, True)
            body(B, 1, False, True, True)
            body(B + 1, 0, False, False, True)

        def p2_tensor(pe):
            def scores(q, k, i):
                for e in range(2):
                    h = 2 * i + e
                    last = pe.matmul(PS[0:T, 2 * (i % 2) + e, 0:T + TC], q[:, h, :], k[:, h // 8, :],
                                     start=True, stop=True)
                last.then_inc(s("x_scores"), 1)

            def fill(r, i, ins, outs):
                if not ins and (not outs or i not in (2, 3)):
                    return
                if not (isinstance(r, int) and r == 0 and i == 0):
                    pe.wait_ge(s("x_empty"), fills(r, i) - 1)
                if i < 2:
                    if i == 0:
                        pe.wait_ge(s("ctx"), r * 16 + 16)
                    for t in range(NK):
                        last = pe.transpose(PH[:, t * KT:(t + 1) * KT], ctxn[:, t, i * 128:(i + 1) * 128],
                                            ident[0:KT, 0:KT])
                if i == 2 and ins:
                    pe.wait_ge(s("x_xs"), r + 1)
                    for k in range(KD):
                        last = pe.transpose(PH[:, k * T:(k + 1) * T], xn[:, 0, k * 128:(k + 1) * 128], ident[0:T, 0:T])
                if i == 2 and outs:
                    pe.wait_ge(s("x_o"), (r - 2) * 4 + 4)
                    for k in range(KD):
                        last = pe.transpose(PH[:, (KD + k) * T:(KD + k + 1) * T],
                                            o_main[:].rearrange("p h e -> p (h e)")[:, k * 128:(k + 1) * 128],
                                            ident[0:T, 0:T])
                if i == 3 and ins:
                    for m in range(KD):
                        for k in range(KD):
                            last = pe.matmul(PH[:, m * T:(m + 1) * T], x_w[:, k, m * 128:(m + 1) * 128], xnT[:, k, 0:T],
                                             start=k == 0, stop=k == KD - 1)
                if i == 3 and outs:
                    for k in range(KD):
                        last = pe.matmul(PH[0:T, D:2 * D], oT[:, k, :], x_wo[:, k, :], start=k == 0, stop=k == KD - 1)
                if i in (4, 5):
                    m = i - 4
                    for k in range(KD):
                        pe.matmul(PH[:, 0:T], x_w[:, k, D + m * 128:D + (m + 1) * 128], xnT[:, k, 0:T],
                                  start=k == 0, stop=k == KD - 1)
                    for k in range(KD):
                        last = pe.matmul(PH[:, T:T + TC], x_wa[:, k, m * 128:(m + 1) * 128], ctxT[:, k, :],
                                         start=k == 0, stop=k == KD - 1)
                if i == 6:
                    for k in range(KD):
                        pe.matmul(PH[0:T, D:2 * D], xnT[:, k, 0:T], x_w[:, k, 2 * D:3 * D], start=k == 0, stop=k == KD - 1)
                if i in (6, 7):
                    for t in ((0,), (1, 2))[i - 6]:
                        for k in range(KD):
                            last = pe.matmul(PH[0:KT, (t + 1) % 2 * D:((t + 1) % 2 + 1) * D] if i == 7 else PH[0:KT, 0:D],
                                             ctxT[:, k, t * KT:(t + 1) * KT], x_wa[:, k, D:2 * D],
                                             start=k == 0, stop=k == KD - 1)
                last.then_inc(s("x_fill"), 1)

            def body(r, own, ins, heads, outs):
                q, k, v = heads_in[own]
                q2, k2, _ = heads_in[1 - own]
                for i in range(NP):
                    if heads:
                        pe.wait_ge(s("x_probs"), (r - 1) * NP + (i + 1))
                        for e in range(2):
                            for t in range(NK):
                                pe.transpose(PT[0:KT, e, t * T:(t + 1) * T],
                                             prob[:, i % 2, e, T + t * KT:T + (t + 1) * KT], ident[0:T, 0:T])
                            last = pe.transpose(PT[0:T, e, NK * T:(NK + 1) * T], prob[:, i % 2, e, 0:T], ident[0:T, 0:T])
                        last.then_inc(s("x_ptr"), 1)
                    fill(r, i, ins, outs)
                    if heads and i + 2 < NP:
                        scores(q, k, i + 2)
                    if ins and i + 2 >= NP:
                        if i + 2 == NP:
                            pe.wait_ge(s("queries_by_head"), r + (1 + HEADS["x"]))
                        scores(q2, k2, i + 2 - NP)
                    if heads:
                        if i == 0 and outs:
                            pe.wait_ge(s("x_o"), (r - 2) * 4 + 3)
                        pe.wait_ge(s("x_pTs"), (r - 1) * NP + (i + 1))
                        pe.wait_ge(s("x_pTv"), (r - 1) * NP + (i + 1))
                        for e in range(2):
                            h = 2 * i + e
                            pe.matmul(PO[0:T, 0, h * HD:(h + 1) * HD], probT[0:T, e, NK, :], v[0:T, NK, h, 0:HD],
                                      start=True, stop=True)
                            for t in range(NK):
                                last = pe.matmul(PO[0:T, 0, D + h * HD:D + (h + 1) * HD], probT[:, e, t, :],
                                                 v[:, t, h, 0:HD], start=t == 0, stop=t == NK - 1)
                        last.then_inc(s("x_pv"), 1)

            rounds(pe, body)

        def p2_scalar(act):
            def body(r, own, ins, heads, outs):
                for i in range(NP if heads else 0):
                    at = (r - 1) * NP + (i + 1)
                    act.wait_ge(s("x_max"), at)
                    for e in range(2):
                        for part, (lo, hi) in enumerate(((0, T), (T, T + TC))):
                            last = act.activation(prob[:, i % 2, e, lo:hi], PS[0:T, 2 * (i % 2) + e, lo:hi], ACT.Exp,
                                                  bias=negmax[:, 2 * i + e, part:part + 1],
                                                  accum_out=sums[:, own, part, 2 * i + e:2 * i + e + 1])
                    last.then_inc(s("x_probs"), 1)
                    act.wait_ge(s("x_ptr"), at)
                    act.activation(probT[:, 0, :, :].rearrange("p t q -> p (t q)"), PT[0:KT, 0, 0:(NK + 1) * T],
                                   ACT.Copy).then_inc(s("x_pTs"), 1)

            rounds(act, body)

        def p2_vector(v):
            def maxima(r, i):
                v.wait_ge(s("x_scores"), (r - 1) * NP + (i + 1))
                for part, (lo, hi) in enumerate(((0, T), (T, T + TC))):
                    last = v.tensor_reduce(negmax[:, 2 * i:2 * i + 2, part],
                                           PS[0:T, 2 * (i % 2):2 * (i % 2) + 2, lo:hi], AX.X, ALU.max, negate=True)
                last.then_inc(s("x_max"), 1)

            def outputs(r, which):
                at = (r - 2) * 4
                v.wait_ge(s("x_probs"), (r - 1) * NP)
                v.reciprocal(rden[:], sums[:, which]).then_inc(s("x_o"), 1)
                v.wait_ge(s("x_o"), at + 1)
                v.tensor_tensor(rden[:], rden[:], x_gate[:], ALU.mult).then_inc(s("x_o"), 1)
                v.wait_ge(s("x_o"), at + 2)
                v.wait_ge(s("x_pv"), (r - 1) * NP)
                v.tensor_tensor(o_main[:], PO[0:T, 0, 0:D].rearrange("p (h e) -> p h e", h=H),
                                bcast(rden[:, 0, :], 2, HD), ALU.mult)
                v.tensor_tensor(o_aux[:], PO[0:T, 0, D:2 * D].rearrange("p (h e) -> p h e", h=H),
                                bcast(rden[:, 1, :], 2, HD), ALU.mult).then_inc(s("x_o"), 1)
                v.wait_ge(s("x_o"), at + 3)
                v.tensor_tensor(o_main[:], o_main[:], o_aux[:], ALU.add).then_inc(s("x_o"), 1)

            def empty(r, i, k, vals, ins, outs):
                if not ins and (not outs or i not in (2, 3)):
                    return
                v.wait_ge(s("x_fill"), fills(r, i))
                if i < 2:
                    last = v.tensor_copy(ctxT[:, i, :], PH[:, 0:TC])
                if i == 2 and ins:
                    last = v.tensor_copy(xnT[:, :, 0:T], PH[:, 0:KD * T].rearrange("p (k t) -> p k t", k=KD))
                if i == 2 and outs:
                    last = v.tensor_copy(oT[:].rearrange("p k t -> p (k t)"), PH[:, KD * T:2 * KD * T])
                if i == 3 and ins:
                    if not (isinstance(r, int) and r == 0):
                        v.wait_ge(s("queries_by_head"), r + HEADS["x"])
                    for m in range(KD):
                        last = v.tensor_scalar(qT[:, m, 0:T], PH[:, m * T:(m + 1) * T], x_bqk[:, 0, m:m + 1], None, ALU.add)
                    last.then_inc(s("queries"), 1)
                if i == 3 and outs:
                    v.wait_ge(s("x_xb"), r - 1)
                    v.tensor_tensor(X[:, r - 2, :], PH[0:T, D:2 * D], X[:, r - 2, :], ALU.add).then_inc(s("x_x"), 1)
                if i == 3:
                    last = v.memset(tick_v[:], 0.0)
                if i in (4, 5):
                    m = i - 4
                    v.tensor_scalar(k[:, m, 0:T], PH[:, 0:T], x_bqk[:, 1, m:m + 1], None, ALU.add)
                    last = v.tensor_scalar(k[:, m, T:T + TC], PH[:, T:T + TC], x_bka[:, m:m + 1], None, ALU.add)
                if i == 6:
                    v.tensor_tensor(vals[0:T, NK, :, 0:HD], PH[0:T, D:2 * D].rearrange("p (h e) -> p h e", h=H),
                                    x_bv[:].rearrange("p (h e) -> p h e", h=H), ALU.add)
                    last = v.tensor_tensor(vals[:, 0, :, 0:HD], PH[0:KT, 0:D].rearrange("p (h e) -> p h e", h=H),
                                           x_bva[:].rearrange("p (h e) -> p h e", h=H), ALU.add)
                if i == 7:
                    last = v.tensor_tensor(vals[:, 1:3, :, 0:HD], PH[0:KT, :].rearrange("p (t h e) -> p t h e", t=2, h=H),
                                           bcast(x_bva[:].rearrange("p (h e) -> p h e", h=H), 1, 2), ALU.add)
                last.then_inc(s("x_empty"), 1)

            def body(r, own, ins, heads, outs):
                _, k, vals = heads_in[1 - own]
                if outs:
                    outputs(r, 1 - own)
                for i in range(NP):
                    if heads and i + 1 < NP:
                        maxima(r, i + 1)
                    if heads:
                        if i == 7 and ins:
                            maxima(r + 1, 0)
                        v.wait_ge(s("x_ptr"), (r - 1) * NP + (i + 1))
                        v.tensor_copy(probT[:, 1, :, :].rearrange("p t q -> p (t q)"),
                                      PT[0:KT, 1, 0:(NK + 1) * T]).then_inc(s("x_pTv"), 1)
                    empty(r, i, k, vals, ins, outs)
                if ins and not heads:
                    maxima(r + 1, 0)

            rounds(v, body)

        def p2_gpsimd(gp):
            def body(b, q, first=False):
                if first:
                    gp.wait_ge(s("ln_xn"), 1 + NORMS["x"])
                else:
                    gp.wait_ge(s("x_fill"), (b - 1) * NP + 3)
                take_wait(gp)
                gp.tensor_copy(xn[:, 0, :], xnall[0:T, b, :]).then_inc(s("x_xs"), 1)
                gp.tensor_tensor(X[:, b, :], X[:, b, :], x_bo[:], ALU.add).then_inc(s("x_xb"), 1)
                queries_gpsimd(gp, "x", b, q)

            body(0, heads_in[0][0], True)
            gp.wait_ge(s("ln_xn"), NG + NORMS["x"])
            with gp.Fori(1, B - 1, 2) as b:
                body(b, heads_in[1][0])
                body(b + 1, heads_in[0][0])
            body(B - 1, heads_in[1][0])

        def norm_all_vector(v, n):
            with v.Fori(0, NG, 1) as g:
                ln_vector(v, n, lambda j: Xg[:, g, j, :], g + 1, G, dst=lambda j: xnallg[:, g, j, :])

        def norm_all_scalar(act, n):
            with act.Fori(0, NG, 1) as g:
                ln_scalar(act, n, g + 1, G)

        def p3_tensor(pe):
            with pe.Fori(0, NG, 1) as g:
                w = g + 1
                pe.wait_ge(s("f_xs"), w)
                for k in range(KD):
                    for j in range(G):
                        last = pe.transpose(PT[:, k, j * T:(j + 1) * T], xn[:, j, k * 128:(k + 1) * 128],
                                            ident[0:T, 0:T])
                last.then_inc(s("f_tr"), 1)
                pe.wait_ge(s("f_xnT"), w)
                for t in range(NHT):
                    if t >= 4:
                        pe.wait_ge(s("f_h"), g * NHT + (t - 3))
                    for k in range(KD):
                        last = pe.matmul(PS[:, t % 4, 0:G * T], f_up[:, k, t * 128:(t + 1) * 128], xnT[:, k, :],
                                         start=k == 0, stop=k == KD - 1)
                    last.then_inc(s("f_hp"), 1)
                pe.wait_ge(s("f_h"), g * NHT + NHT)
                for j in range(G):
                    if j >= 2:
                        pe.wait_ge(s("f_x"), g * G + (j - 1))
                    for t in range(NHT):
                        last = pe.matmul(PO[0:T, j % 2, 0:D], hT[:, t, j * T:(j + 1) * T], f_down[:, t, :],
                                         start=t == 0, stop=t == NHT - 1)
                    last.then_inc(s("f_y"), 1)

        def p3_scalar(act):
            with act.Fori(0, NG, 1) as g:
                for t in range(NHT):
                    act.wait_ge(s("f_hp"), g * NHT + (t + 1))
                    act.activation(hT[:, t, :], PS[:, t % 4, 0:G * T], ACT.Gelu,
                                   bias=f_hb[:, t:t + 1]).then_inc(s("f_h"), 1)

        def p3_vector(v):
            with v.Fori(0, NG, 1) as g:
                w = g + 1
                v.wait_ge(s("f_tr"), w + 1)
                v.tensor_copy(xnT[:], PT[:, :, 0:G * T]).then_inc(s("f_xnT"), 1)
                v.wait_ge(s("f_xb"), w)
                for j in range(G):
                    v.wait_ge(s("f_y"), g * G + (j + 1))
                    v.tensor_tensor(Xg[:, g, j, :], PO[0:T, j % 2, 0:D], Xg[:, g, j, :], ALU.add).then_inc(s("f_x"), 1)

        def p3_gpsimd(gp):
            gp.sem_inc(s("f_tr"), 1)
            with gp.Fori(0, NG, 1) as g:
                w = g + 1
                gp.wait_ge(s("ln_xn"), w + NORMS["f"])
                gp.wait_ge(s("f_tr"), w)
                take_wait(gp)
                gp.tensor_copy(xn[:], xnallg[:, g, :, :]).then_inc(s("f_xs"), 1)
                gp.tensor_tensor(Xg[:, g, :, :], Xg[:, g, :, :], bcast(f_bo[:], 1, G), ALU.add).then_inc(s("f_xb"), 1)

        NQ = H // 4
        prob4 = prob[:].rearrange("p s e c -> p s (e c)")[:, :, 0:4 * T]
        probT4 = probT[:].rearrange("p s t q -> p s (t q)")

        def fills4(r, f):
            if isinstance(r, int) and r >= B:
                return B * 4 + 2 * (r - B) + (1 if f == 0 else 2)
            return r * 4 + (f + 1)

        def by_half(gp, n, b, q):
            for m in range(KD):
                gp.wait_ge(s(n + "_q"), b * 2 + (m + 1))
                gp.tensor_tensor(q[:, m * 8:(m + 1) * 8, :], bcast(qT[:, m, 0:T], 1, 8),
                                 bcast(headmask[:], 2, T), ALU.mult).then_inc(s(n + "_qm"), 1)

        def p4_tensor(pe):
            def scores(q, k, i):
                pe.matmul(PS[0:T, i % 2, 0:4 * T], identb[:], causal4[:].rearrange("p h k -> p (h k)"),
                          start=True, stop=False, skip_group_check=True)
                for e in range(4):
                    h = 4 * i + e
                    last = pe.matmul(PS[0:T, i % 2, e * T:(e + 1) * T], q[:, h, :], k[:, h // 8, 0:T],
                                     start=False, stop=e == 3, skip_group_check=True)
                last.then_inc(s("r_scores"), 1)

            def fill(r, f, ins, outs):
                if not ins and (not outs or f not in (0, 3)):
                    return
                if not (isinstance(r, int) and r == 0 and f == 0) and (f < 2 or not ins):
                    pe.wait_ge(s("r_empty"), fills4(r, f) - 1)
                if f == 0 and ins:
                    pe.wait_ge(s("r_xs"), r + 1)
                    for k in range(KD):
                        last = pe.transpose(PS[:, 2, k * T:(k + 1) * T], xn[:, 0, k * 128:(k + 1) * 128], ident[0:T, 0:T])
                if f == 0 and outs:
                    pe.wait_ge(s("r_o"), (r - 2) * 2 + 2)
                    for k in range(KD):
                        last = pe.transpose(PS[:, 2, (KD + k) * T:(KD + k + 1) * T],
                                            o_main[:].rearrange("p h e -> p (h e)")[:, k * 128:(k + 1) * 128],
                                            ident[0:T, 0:T])
                if f in (1, 2):
                    for j, wt in enumerate((r_w, r_wr)):
                        for m in range(KD):
                            c0 = (f - 1) * D + m * 128
                            for k in range(KD):
                                last = pe.matmul(PS[:, 1 + f, (KD * j + m) * T:(KD * j + m + 1) * T],
                                                 wt[:, k, c0:c0 + 128], xnT[:, k, 0:T], start=k == 0, stop=k == KD - 1)
                if f == 3 and ins:
                    for k in range(KD):
                        last = pe.matmul(PH[0:T, 0:D], xnT[:, k, 0:T], r_w[:, k, 2 * D:3 * D],
                                         start=k == 0, stop=k == KD - 1)
                if f == 3 and outs:
                    for k in range(KD):
                        last = pe.matmul(PH[0:T, D:2 * D], oT[:, k, :], r_wo[:, k, :], start=k == 0, stop=k == KD - 1)
                last.then_inc(s("r_fill"), 1)

            def body(r, own, ins, heads, outs):
                q, k, v = heads_in[own]
                q2, k2, _ = heads_in[1 - own]
                for i in range(NQ):
                    if heads:
                        pe.wait_ge(s("r_probs"), (r - 1) * NQ + (i + 1))
                        for e in range(4):
                            last = pe.transpose(PT[0:T, i % 2, e * T:(e + 1) * T], prob4[:, i % 2, e * T:(e + 1) * T],
                                                ident[0:T, 0:T])
                        last.then_inc(s("r_ptr"), 1)
                        if i + 2 < NQ:
                            if i == 0:
                                pe.wait_ge(s("r_qm"), (r - 1) * 2 + 2)
                            scores(q, k, i + 2)
                        if i == 0 and outs:
                            pe.wait_ge(s("r_o"), (r - 2) * 2 + 2)
                        pe.wait_ge(s("r_pT"), (r - 1) * NQ + (i + 1))
                        for e in range(4):
                            h = 4 * i + e
                            last = pe.matmul(PO[0:T, 0, h * HD:(h + 1) * HD], probT4[0:T, i % 2, e * T:(e + 1) * T],
                                             v[0:T, NK, h, 0:HD], start=True, stop=True)
                        last.then_inc(s("r_pv"), 1)
                    for f in ((0,), (1, 2), (3,), ())[i]:
                        fill(r, f, ins, outs)
                if ins:
                    pe.wait_ge(s("r_qm"), r * 2 + 1)
                    pe.wait_ge(s("r_empty"), r * 4 + 4)
                    scores(q2, k2, 0)
                    scores(q2, k2, 1)

            rounds(pe, body)

        def p4_scalar(act):
            def body(r, own, ins, heads, outs):
                for i in range(NQ if heads else 0):
                    at = (r - 1) * NQ + (i + 1)
                    act.wait_ge(s("r_max"), at)
                    for e in range(4):
                        h = 4 * i + e
                        last = act.activation(prob4[:, i % 2, e * T:(e + 1) * T], PS[0:T, i % 2, e * T:(e + 1) * T],
                                              ACT.Exp, bias=negmax[:, h, 0:1], accum_out=sums[:, own, 0, h:h + 1])
                    last.then_inc(s("r_probs"), 1)
                    act.wait_ge(s("r_ptr"), at)
                    act.activation(probT4[0:T, i % 2, :], PT[0:T, i % 2, 0:4 * T], ACT.Copy).then_inc(s("r_pT"), 1)

            rounds(act, body)

        def p4_vector(v):
            def maxima(r, i):
                v.wait_ge(s("r_scores"), (r - 1) * NQ + (i + 1))
                v.tensor_reduce(negmax[:, 4 * i:4 * i + 4, 0], PS[0:T, i % 2, 0:4 * T].rearrange("p (h k) -> p h k", h=4),
                                AX.X, ALU.max, negate=True).then_inc(s("r_max"), 1)

            def outputs(r, which):
                v.wait_ge(s("r_probs"), (r - 1) * NQ)
                v.reciprocal(rden[:, 0, :], sums[:, which, 0, :]).then_inc(s("r_o"), 1)
                v.wait_ge(s("r_o"), (r - 2) * 2 + 1)
                v.wait_ge(s("r_pv"), (r - 1) * NQ)
                v.tensor_tensor(o_main[:], PO[0:T, 0, 0:D].rearrange("p (h e) -> p h e", h=H),
                                bcast(rden[:, 0, :], 2, HD), ALU.mult).then_inc(s("r_o"), 1)

            def empty(r, f, k2, vals, ins, outs):
                if not ins and (not outs or f not in (0, 3)):
                    return
                v.wait_ge(s("r_fill"), fills4(r, f))
                if f == 0 and ins:
                    last = v.tensor_copy(xnT[:, :, 0:T], PS[:, 2, 0:KD * T].rearrange("p (k t) -> p k t", k=KD))
                if f == 0 and outs:
                    last = v.tensor_copy(oT[:].rearrange("p k t -> p (k t)"), PS[:, 2, KD * T:2 * KD * T])
                if f in (1, 2):
                    for j, table in enumerate((cosq, sinq)):
                        last = v.tensor_tensor(rot[:, j, 2 * f - 2:2 * f, :],
                                               PS[:, 1 + f, j * KD * T:(j + 1) * KD * T].rearrange("p (m t) -> p m t", m=KD),
                                               bcast(table[:], 1, KD), ALU.mult)
                    last.then_inc(s("r_rot"), 1)
                    v.wait_ge(s("r_rot"), r * 2 + f)
                    if f == 1 and not (isinstance(r, int) and r == 0):
                        v.wait_ge(s("r_qm"), r * 2)
                    if f == 1:
                        v.tensor_tensor(qT[:, :, 0:T], rot[:, 0, 0:2, :], rot[:, 1, 0:2, :], ALU.add).then_inc(s("r_q"), 2)
                        last = v.memset(tick_v[:], 0.0)
                    else:
                        last = v.tensor_tensor(k2[:, :, 0:T], rot[:, 0, 2:4, :], rot[:, 1, 2:4, :], ALU.add)
                if f == 3 and ins:
                    last = v.tensor_copy(vals[0:T, NK, :, 0:HD], PH[0:T, 0:D].rearrange("p (h e) -> p h e", h=H))
                if f == 3 and outs:
                    v.tensor_tensor(X[:, r - 2, :], PH[0:T, D:2 * D], X[:, r - 2, :], ALU.add).then_inc(s("r_x"), 1)
                    last = v.memset(tick_v[:], 0.0)
                last.then_inc(s("r_empty"), 1)

            def body(r, own, ins, heads, outs):
                _, k2, vals = heads_in[1 - own]
                if outs:
                    outputs(r, 1 - own)
                for i in range(NQ):
                    if heads and i + 2 < NQ:
                        maxima(r, i + 2)
                    for f in ((0,), (1, 2), (3,), ())[i]:
                        empty(r, f, k2, vals, ins, outs)
                if ins:
                    maxima(r + 1, 0)
                    maxima(r + 1, 1)

            rounds(v, body)

        def p4_gpsimd(gp):
            def body(b, q, first=False):
                if not first:
                    gp.wait_ge(s("r_fill"), (b - 1) * 4 + 1)
                    take_wait(gp)
                gp.tensor_copy(xn[:, 0, :], xnall[0:T, b, :]).then_inc(s("r_xs"), 1)
                by_half(gp, "r", b, q)

            gp.wait_ge(s("ln_xn"), NORMS["c"])
            body(0, heads_in[0][0], True)
            with gp.Fori(1, B - 1, 2) as b:
                body(b, heads_in[1][0])
                body(b + 1, heads_in[0][0])
            body(B - 1, heads_in[1][0])

        NT5 = NQ * NK
        prob5 = big[:, 0:2 * NK * 4 * T].rearrange("p (s t q) -> p s t q", s=2, t=NK)

        NF5 = 9
        STEP5 = ((0, 1), (2,), (3,), (4,), (5,), (6,), (7,), (8,))
        BANK_A, BANK_B = PT[:, 0, :], PT[:, 1, :]

        def p5_tensor(pe):
            def scores(q, k, n):
                i, t = n // NK, n % NK
                pe.matmul(PS[0:KT, n % 4, 0:4 * T], k[:, i // 2, T + t * KT:T + (t + 1) * KT],
                          q[:, 4 * i:4 * i + 4, :].rearrange("p h q -> p (h q)"),
                          start=True, stop=True).then_inc(s("c_scores"), 1)

            def fill(r, f):
                first = isinstance(r, int) and r == 0
                if f < 2:
                    if f == 0:
                        pe.wait_ge(s("ctx"), r * 16 + 16 * (B + 1))
                        if not first:
                            pe.wait_ge(s("c_emptyv"), r * 7)
                    for t in range(NK):
                        last = pe.transpose((BANK_A, BANK_B)[f][:, t * KT:(t + 1) * KT],
                                            ctxn[:, t, f * 128:(f + 1) * 128], ident[0:KT, 0:KT])
                if f == 2:
                    pe.wait_ge(s("c_xs"), r + 1)
                    for k in range(KD):
                        last = pe.transpose(PH[:, k * T:(k + 1) * T], xn[:, 0, k * 128:(k + 1) * 128], ident[0:T, 0:T])
                if f in (3, 4):
                    m = f - 3
                    if f == 3:
                        pe.wait_ge(s("c_emptyv"), r * 7 + 3)
                        if not first:
                            pe.wait_ge(s("c_rs"), r * 2)
                    bank = (BANK_A, BANK_B)[m]
                    for k in range(KD):
                        pe.matmul(bank[:, 0:T], c_wq[:, k, m * 128:(m + 1) * 128], xnT[:, k, 0:T],
                                  start=k == 0, stop=k == KD - 1)
                    for k in range(KD):
                        last = pe.matmul(bank[:, T:T + TC], c_wk[:, k, m * 128:(m + 1) * 128], ctxT[:, k, :],
                                         start=k == 0, stop=k == KD - 1)
                if f == 6:
                    pe.wait_ge(s("c_emptys"), r * 4 + 1)
                    pe.wait_ge(s("c_emptyv"), r * 7 + 4)
                if f == 7:
                    pe.wait_ge(s("c_emptys"), r * 4 + 3)
                if f in (6, 7):
                    last = pe.matmul(PH[:, 0:T + TC], headsum[:], sq[:, f - 6, :], start=True, stop=True)
                if f == 8:
                    pe.wait_ge(s("c_emptys"), r * 4 + 4)
                if f in (5, 8):
                    for t in ((0, 1) if f == 5 else (2,)):
                        for k in range(KD):
                            last = pe.matmul(PH[0:KT, t % 2 * D:(t % 2 + 1) * D], ctxT[:, k, t * KT:(t + 1) * KT],
                                             c_wv[:, k, :], start=k == 0, stop=k == KD - 1)
                last.then_inc(s("c_fill"), 1)

            def body(r, own, ins, heads, outs):
                q, k, v = heads_in[own]
                q2, k2, _ = heads_in[1 - own]
                for n in range(NT5):
                    if ins and n < len(STEP5):
                        for f in STEP5[n]:
                            fill(r, f)
                    if heads:
                        pe.wait_ge(s("c_probs"), (r - 1) * NT5 + (n + 1))
                        if n == 2:
                            pe.wait_ge(s("c_emptyv"), (r - 1) * 7 + 7)
                            pe.wait_ge(s("c_qm"), (r - 1) * 2 + 2)
                        if n + 4 < NT5:
                            scores(q, k, n + 4)
                    if ins and n + 4 >= NT5:
                        if n + 4 == NT5:
                            pe.wait_ge(s("c_qm"), r * 2 + 1)
                            pe.wait_ge(s("c_emptyv"), r * 7 + 5)
                        scores(q2, k2, n + 4 - NT5)
                    if heads and n % NK == NK - 1:
                        i = n // NK
                        if i == 0 and outs:
                            pe.wait_ge(s("c_o"), (r - 2) * 2 + 2)
                        for e in range(4):
                            h = 4 * i + e
                            for t in range(NK):
                                last = pe.matmul(PO[0:T, 0, h * (HD + 1):(h + 1) * (HD + 1)],
                                                 prob5[0:KT, i % 2, t, e * T:(e + 1) * T], v[:, t, h, :],
                                                 start=t == 0, stop=t == NK - 1)
                        last.then_inc(s("c_pv"), 1)

            rounds(pe, body)

        def p5_scalar(act):
            def body(r, own, ins, heads, outs):
                def inputs(n):
                    if n in (3, 4):
                        m = n - 3
                        act.wait_ge(s("c_fill"), r * NF5 + (4 + m))
                        act.activation(sq[:, m, :], (BANK_A, BANK_B)[m][:, 0:T + TC], ACT.Square).then_inc(s("c_emptys"), 1)
                    if n in (6, 7):
                        m = n - 6
                        act.wait_ge(s("c_fill"), r * NF5 + (7 + m))
                        if m == 0 and not (isinstance(r, int) and r == 0):
                            act.wait_ge(s("c_emptyv"), r * 7)
                        act.activation(rms[:, m, :], PH[:, 0:T + TC], ACT.Ln, scale=1.0 / HD,
                                       bias=eps_rms[:]).then_inc(s("c_emptys"), 1)
                        act.wait_ge(s("c_emptys"), r * 4 + (3 + m))
                        act.activation(rms[:, m, :], rms[:, m, :], ACT.Exp, scale=-0.5).then_inc(s("c_rs"), 1)

                for n in range(NT5 if heads or ins else 0):
                    if heads:
                        i, t = n // NK, n % NK
                        act.wait_ge(s("c_scores"), (r - 1) * NT5 + (n + 1))
                        if t == 0 and (i >= 2 or outs):
                            act.wait_ge(s("c_pv"), (r - 1) * NQ + (i - 1))
                        act.activation(prob5[0:KT, i % 2, t, :], PS[0:KT, n % 4, 0:4 * T], ACT.Exp).then_inc(s("c_probs"), 1)
                    if ins:
                        inputs(n)

            rounds(act, body)

        def p5_vector(v):
            v.memset(vv_b[:, :, :, HD:HD + 1], 1.0).then_inc(s("c_ones"), 1)
            v.wait_ge(s("c_ones"), 1)

            def outputs(r):
                v.wait_ge(s("c_pv"), (r - 1) * NQ)
                o5 = PO[0:T, 0, 0:H * (HD + 1)].rearrange("p (h e) -> p h e", h=H)
                v.reciprocal(rden[:, 0, :], o5[:, :, HD]).then_inc(s("c_o"), 1)
                v.wait_ge(s("c_o"), (r - 2) * 2 + 1)
                v.tensor_tensor(o_main[:], o5[:, :, 0:HD], bcast(rden[:, 0, :], 2, HD), ALU.mult).then_inc(s("c_o"), 1)
                v.wait_ge(s("c_o"), (r - 2) * 2 + 2)
                v.tensor_tensor(X[:, r - 2, :], o_main[:].rearrange("p h e -> p (h e)"), X[:, r - 2, :],
                                ALU.add).then_inc(s("c_x"), 1)

            def body(r, own, ins, heads, outs):
                _, k2, vals = heads_in[1 - own]
                if outs:
                    outputs(r)
                if not ins:
                    return
                first = isinstance(r, int) and r == 0
                for f in range(2):
                    v.wait_ge(s("c_fill"), r * NF5 + (1 + f))
                    v.tensor_copy(ctxT[:, f, :], (BANK_A, BANK_B)[f][:, 0:TC]).then_inc(s("c_emptyv"), 1)
                v.wait_ge(s("c_fill"), r * NF5 + 3)
                v.tensor_copy(xnT[:, :, 0:T], PH[:, 0:KD * T].rearrange("p (k t) -> p k t", k=KD)).then_inc(s("c_emptyv"), 1)
                v.wait_ge(s("c_fill"), r * NF5 + 6)
                v.tensor_copy(vals[:, 0:2, :, 0:HD], PH[0:KT, :].rearrange("p (t h e) -> p t h e", t=2, h=H)).then_inc(s("c_emptyv"), 1)
                for m in range(KD):
                    v.wait_ge(s("c_rs"), r * 2 + (1 + m))
                    if not first:
                        v.wait_ge(s("c_qm"), r * 2)
                    bank = (BANK_A, BANK_B)[m]
                    v.tensor_tensor(qT[:, m, 0:T], bank[:, 0:T], rms[:, m, 0:T], ALU.mult).then_inc(s("c_q"), 1)
                    v.tensor_tensor(k2[:, m, T:T + TC], bank[:, T:T + TC], rms[:, m, T:T + TC], ALU.mult).then_inc(s("c_emptyv"), 1)
                v.wait_ge(s("c_fill"), r * NF5 + 9)
                v.tensor_copy(vals[:, 2, :, 0:HD], PH[0:KT, 0:D].rearrange("p (h e) -> p h e", h=H)).then_inc(s("c_emptyv"), 1)

            rounds(v, body)

        def p5_gpsimd(gp):
            def body(b, q, first=False):
                if not first:
                    gp.wait_ge(s("c_fill"), (b - 1) * NF5 + 3)
                    take_wait(gp)
                gp.tensor_copy(xn[:, 0, :], xnall[0:T, b, :]).then_inc(s("c_xs"), 1)
                by_half(gp, "c", b, q)

            gp.wait_ge(s("ln_xn"), NORMS["m"])
            body(0, heads_in[0][0], True)
            with gp.Fori(1, B - 1, 2) as b:
                body(b, heads_in[1][0])
                body(b + 1, heads_in[0][0])
            body(B - 1, heads_in[1][0])

        def quantize(v, done, at, src, dst, rs, sc, xr, xa, sg, cc, dst_read=None):
            k = [0]

            def step(ins):
                ins.then_inc(done, 1)
                k[0] += 1
                v.wait_ge(done, at + k[0])

            step(v.tensor_reduce(sc, src, AX.X, ALU.max, apply_absolute_value=True))
            step(v.tensor_scalar(sc, sc, 1.0 / 6.0, 1e-12, ALU.mult, ALU.max))
            step(v.reciprocal(rs, sc))
            step(v.tensor_tensor(xr, src, bcast(rs, 2, BLK), ALU.mult))
            v.tensor_scalar(sg, xr, 0.0, None, ALU.is_ge)
            step(v.scalar_tensor_tensor(out=xa, in0=xr, scalar=-1.0, in1=xr, op0=ALU.mult, op1=ALU.max))
            v.tensor_scalar(sg, sg, 2.0, -1.0, ALU.mult, ALU.add)
            v.tensor_scalar(cc, xa, MIDS[6], 4.0, ALU.is_gt, ALU.mult)
            step(v.tensor_scalar(xr, xa, MIDS[5], 2.0, ALU.is_gt, ALU.mult))
            step(v.tensor_tensor(cc, cc, xr, ALU.add))
            step(v.tensor_scalar(xr, xa, MIDS[4], 2.0, ALU.is_gt, ALU.mult))
            step(v.tensor_tensor(cc, cc, xr, ALU.add))
            for m in MIDS[0:4]:
                step(v.scalar_tensor_tensor(out=cc, in0=xa, scalar=m, in1=cc, op0=ALU.is_gt, op1=ALU.add))
            step(v.scalar_tensor_tensor(out=cc, in0=cc, scalar=0.5, in1=sg, op0=ALU.mult, op1=ALU.mult))
            if dst_read:
                v.wait_ge(*dst_read)
            step(v.tensor_tensor(dst, cc, bcast(sc, 2, BLK), ALU.mult))
            return k[0]

        NQB = FF // BLK
        NTD = -(-FF // 128)
        FH = FF // 2
        xq = big[0:T, 0:D]
        gated = big[0:T, 256:256 + FF]
        hid = big[0:T, 1024:1024 + FF]
        prod = big[0:T, 1792:1792 + FF]
        qwork = [big[:, 2560 + i * 1024:2560 + (i + 1) * 1024] for i in range(4)]
        hqT = big[:, 6656:6656 + 6 * T].rearrange("p (t q) -> p t q", t=6)
        NQX = 15

        def blocks(ap, n):
            return ap[:, 0:n * BLK].rearrange("p (n e) -> p n e", e=BLK)

        def p6_tensor(pe):
            def gate_up(b):
                pe.wait_ge(s("m_xs"), b + 1)
                for k in range(KD):
                    last = pe.transpose(PO[:, 1, k * T:(k + 1) * T], xq[:, k * 128:(k + 1) * 128], ident[0:T, 0:T])
                last.then_inc(s("m_tr"), 1)
                pe.wait_ge(s("m_xT"), b + 1)
                pe.wait_ge(s("m_h"), b + 1)
                for gu in range(2):
                    for i in range(2):
                        for k in range(KD):
                            last = pe.matmul(PS[0:T, 2 * gu + i, 0:FH], xnT[:, k, 0:T],
                                             m_wgu[:, k, gu, i * FH:(i + 1) * FH], start=k == 0, stop=k == KD - 1)
                last.then_inc(s("m_gu"), 1)

            def down(b):
                pe.wait_ge(s("m_hq"), NQX * (b + 1))
                for t in range(NTD):
                    n = min(128, FF - t * 128)
                    last = pe.transpose(PT[0:n, t // 4, (t % 4) * T:(t % 4 + 1) * T], hid[:, t * 128:t * 128 + n],
                                        ident[0:T, 0:T])
                last.then_inc(s("m_htr"), 1)
                pe.wait_ge(s("m_hT"), b + 1)
                pe.wait_ge(s("m_x"), b + 1)
                for t in range(NTD):
                    n = min(128, FF - t * 128)
                    last = pe.matmul(PO[0:T, 0, 0:D], hqT[0:n, t, :], m_wd[0:n, t, :], start=t == 0, stop=t == NTD - 1)
                last.then_inc(s("m_out"), 1)

            gate_up(0)
            with pe.Fori(0, B - 1, 1) as b:
                gate_up(b + 1)
                down(b)
            down(B - 1)

        def p6_scalar(act):
            def gate(b):
                act.wait_ge(s("m_tr"), b + 2)
                act.activation(xnT[:, :, 0:T], PO[:, 1, 0:KD * T].rearrange("p (k t) -> p k t", k=KD),
                               ACT.Copy).then_inc(s("m_xT"), 1)
                act.wait_ge(s("m_gu"), b + 1)
                act.activation(gated.rearrange("p (i n) -> p i n", i=2), PS[0:T, 0:2, 0:FH], ACT.Silu).then_inc(s("m_silu"), 1)

            def turn(b):
                act.wait_ge(s("m_htr"), b + 1)
                act.activation(hqT[:, 0:4, :], PT[:, 0, 0:4 * T].rearrange("p (t q) -> p t q", t=4), ACT.Copy)
                act.activation(hqT[:, 4:6, :], PT[:, 1, 0:2 * T].rearrange("p (t q) -> p t q", t=2),
                               ACT.Copy).then_inc(s("m_hT"), 1)

            gate(0)
            with act.Fori(0, B - 1, 1) as b:
                gate(b + 1)
                turn(b)
            turn(B - 1)

        def p6_quantize_tokens(v):
            with v.Fori(0, NG, 1) as g:
                src = xnallg[:, g, :, :].rearrange("p j (n e) -> p (j n) e", e=BLK)
                n = quantize(v, s("m_xq"), g * NQX, src, src, m_rs[0:T, :], m_sc[0:T, :],
                             *[blocks(q[0:T], G * D // BLK) for q in qwork])
                assert n == NQX

        def p6_vector(v):
            def hidden(b, hid_read=None):
                v.wait_ge(s("m_silu"), b + 1)
                v.tensor_tensor(prod.rearrange("p (i n) -> p i n", i=2), PS[0:T, 2:4, 0:FH],
                                gated.rearrange("p (i n) -> p i n", i=2), ALU.mult).then_inc(s("m_h"), 1)
                v.wait_ge(s("m_h"), b + 2)
                quantize(v, s("m_hq"), b * NQX, blocks(prod, NQB), blocks(hid, NQB),
                         m_rs[0:T, 0:NQB], m_sc[0:T, 0:NQB], *[blocks(q[0:T], NQB) for q in qwork], dst_read=hid_read)

            def add(b):
                v.wait_ge(s("m_out"), b + 1)
                v.tensor_tensor(X[:, b, :], PO[0:T, 0, 0:D], X[:, b, :], ALU.add).then_inc(s("m_x"), 1)

            hidden(0)
            with v.Fori(0, B - 1, 1) as b:
                hidden(b + 1, (s("m_htr"), b + 1))
                add(b)
            add(B - 1)

        def p6_gpsimd(gp):
            gp.sem_inc(s("m_tr"), 1)
            gp.sem_inc(s("m_h"), 1)
            gp.sem_inc(s("m_x"), 1)
            with gp.Fori(0, B, 1) as b:
                gp.wait_ge(s("m_xq"), NG * NQX)
                gp.wait_ge(s("m_tr"), b + 1)
                take_wait(gp)
                gp.tensor_copy(xq, xnall[0:T, b, :]).then_inc(s("m_xs"), 1)

        NS = 7
        W2 = 2 * NHT
        pair_sel = xnall[0:64, 0:7, :].rearrange("p k (r f) -> p k r f", r=2)
        pong = xnall[:].rearrange("p b d -> p (b d)")[:, 1792:1792 + NHT * (D + 1)].rearrange("p (t d) -> p t d", t=NHT)
        o = 0
        perm = big[:, 0:NS * 256].rearrange("p (k r f) -> p k r f", k=NS, r=2)
        stage = big[:, 1792:1792 + 2048].rearrange("p (u f) -> p u f", u=W2)
        chain = big[:, 3840:3840 + 2048].rearrange("p (u f) -> p u f", u=W2)
        wexpT = big[:, 5888:5888 + NHT * (D + 1)].rearrange("p (t d) -> p t d", t=NHT)
        pair_w = big[0:64, 7944:7944 + NS * W2 * 4].rearrange("p (k u c) -> p k u c", k=NS, u=W2)
        row_w = big[:, 8392:8392 + NS * W2 * 2].rearrange("p (k u c) -> p k u c", k=NS, u=W2)
        raw_r = big[:, 0:8 * D].rearrange("p (m d) -> p m d", m=8)
        raw_gu = big[0:88, 0:4096].rearrange("p (g t d) -> p g t d", g=2, t=8)
        raw_d = xnall[:].rearrange("p b d -> p (b d)")[:, 0:2 * FF].rearrange("p (m k) -> p m k", m=2)
        raw_kv = sb("raw_kv", [128, KD, 2 * D])
        high_w = sb("high_w", [128, 2, 3, 4, 4])
        f_upb = sb("f_upb", [128, NHT])
        m_sc = sb("m_sc", [128, 64])
        swork = [big[:, 4096 + i * 1024:4096 + (i + 1) * 1024] for i in range(4)]

        def setup_loads_1(sp):
            sp.dma_start(f_up[:], a["L0_ffn_W_exp"].rearrange("(k p) n -> p k n", p=128)).then_inc(s("ld_f"), 16)
            sp.dma_start(f_down[:], a["L0_ffn_W_con"].rearrange("(t p) n -> p t n", p=128)).then_inc(s("ld_f"), 16)
            for i, n in enumerate(("up", "down")):
                src = a[f"L0_ffn_{n}_weights"]
                for k in range(NS):
                    sp.dma_start(pair_w[:, k, i * NHT:(i + 1) * NHT, :],
                                 src[k].rearrange("(t p) r c -> p t (r c)", p=64)).then_inc(s("ld_f"), 16)
                for k in range(3):
                    sp.dma_start(high_w[:, i, k, :, :],
                                 src[NS + k].rearrange("(q p) r c -> p q (r c)", p=128)).then_inc(s("ld_f"), 16)
            sp.dma_start(perm, c["perm"]).then_inc(s("ld_f"), 16)
            sp.dma_start(pair_sel, c["pair_sel"]).then_inc(s("ld_f"), 16)
            sp.dma_start(wexpT[:, :, D], a["L0_ffn_b_exp"].rearrange("(t p) -> p t", p=128)).then_inc(s("ld_f"), 16)
            sp.dma_start(f_upb[:], a["L0_ffn_up_bias"].rearrange("(t p) -> p t", p=128)).then_inc(s("ld_f"), 16)
            sp.dma_start(f_bo[:], a["L0_ffn_b_con"].partition_broadcast(T)).then_inc(s("ld_f"), 16)
            sp.dma_start(f_bd[:], a["L0_ffn_down_bias"].partition_broadcast(T)).then_inc(s("ld_f"), 16)

        NF = 2 + 2 * (NS + 3) + 6

        def fold_scalar(act):
            act.wait_ge(s("ld_f"), 16 * NF)
            act.wait_ge(s("row_w"), 1)
            for n, k in enumerate(reversed(range(NS))):
                if n > 0:
                    act.wait_ge(s("chain_mm"), n)
                for u in range(W2):
                    last = act.activation(stage[:, u, :], perm[:, k, 0, :], ACT.Copy, scale=row_w[:, k, u, 0:1])
                last.then_inc(s("stage_a"), 1)
                act.wait_ge(s("chain_mm"), n + 1)
                act.activation(chain, PS[:].rearrange("p b (u f) -> p (b u) f", f=128), ACT.Copy).then_inc(s("chain"), 1)
            act.wait_ge(s("wexp_tr"), 1)
            act.activation(wexpT[:, :, 0:D], PS[:].rearrange("p b (t d) -> p (b t) d", d=D), ACT.Copy).then_inc(s("wexpT"), 1)
            for i in range(2):
                act.wait_ge(s("up_low"), i + 1)
                act.activation(wexpT[:, 4 * i:4 * i + 4, :], PS[:, :, 0:D + 1], ACT.Copy).then_inc(s("up_lowc"), 1)
            act.wait_ge(s("up_tr"), 1)
            act.activation(f_up[:], PS[:].rearrange("p (k i) n -> p k (i n)", k=KD), ACT.Copy).then_inc(s("f_ready"), 1)
            for i in range(2):
                act.wait_ge(s("down_low"), i + 1)
                act.activation(f_down[:, 4 * i:4 * i + 4, :], PS[:, :, 0:D], ACT.Copy).then_inc(s("down_lowc"), 1)

        def fold_tensor(pe):
            pe.wait_ge(s("ld_f"), 16 * NF)
            for k in range(NS):
                for r in range(2):
                    last = pe.matmul(PT[:, 0, k * 32:(k + 1) * 32], pair_sel[:, k, r, :],
                                     pair_w[:, k, :, 2 * r:2 * r + 2], start=r == 0, stop=r == 1)
            last.then_inc(s("row_wp"), 1)
            for n, k in enumerate(reversed(range(NS))):
                pe.wait_ge(s("stage_b"), n + 1)
                if n > 0:
                    pe.wait_ge(s("chain"), n)
                for u in range(W2):
                    before = ident[:] if n == 0 else chain[:, u, :]
                    left, right = stage[:, u, :], before
                    if k == 0 and u >= NHT:
                        left, right = before, stage[:, u, :]
                    last = pe.matmul(PS[:, u // 4, (u % 4) * 128:(u % 4 + 1) * 128], left, right, start=True, stop=True)
                last.then_inc(s("chain_mm"), 1)
            pe.wait_ge(s("chain"), NS)
            for t in range(NHT):
                for k in range(KD):
                    last = pe.transpose(PS[:, t // 2, (t % 2) * D + k * 128:(t % 2) * D + (k + 1) * 128],
                                        f_up[:, k, t * 128:(t + 1) * 128], ident[:])
            last.then_inc(s("wexp_tr"), 1)
            pe.wait_ge(s("wexpT"), 1)
            for i in range(2):
                if i > 0:
                    pe.wait_ge(s("up_lowc"), i)
                for t in range(4 * i, 4 * i + 4):
                    last = pe.matmul(PS[:, t % 4, 0:D + 1], chain[:, t, :], wexpT[:, t, :], start=True, stop=True)
                last.then_inc(s("up_low"), 1)
            pe.wait_ge(s("up_lowc"), 2)
            pe.wait_ge(s("high"), 6)
            for k in range(KD):
                for t in range(NHT):
                    last = pe.transpose(PS[:, 2 * k + t // 4, (t % 4) * 128:(t % 4 + 1) * 128],
                                        pong[:, t, k * 128:(k + 1) * 128], ident[:])
            last.then_inc(s("up_tr"), 1)
            pe.wait_ge(s("f_ready"), 1)
            pe.wait_ge(s("high"), 13)
            for i in range(2):
                if i > 0:
                    pe.wait_ge(s("down_lowc"), i)
                for t in range(4 * i, 4 * i + 4):
                    last = pe.matmul(PS[:, t % 4, 0:D], chain[:, NHT + t, :], pong[:, t, 0:D], start=True, stop=True)
                last.then_inc(s("down_low"), 1)

        def fold_vector(v):
            v.wait_ge(s("ld_f"), 16 * NF)
            v.wait_ge(s("row_wp"), 1)
            v.tensor_copy(row_w, PT[:, 0, 0:NS * 32].rearrange("p (k u c) -> p k u c", k=NS, u=W2)).then_inc(s("row_w"), 1)
            v.wait_ge(s("row_w"), 1)
            for n, k in enumerate(reversed(range(NS))):
                v.wait_ge(s("stage_a"), n + 1)
                for u in range(W2):
                    last = v.scalar_tensor_tensor(out=stage[:, u, :], in0=perm[:, k, 1, :], scalar=row_w[:, k, u, 1:2],
                                                  in1=stage[:, u, :], op0=ALU.mult, op1=ALU.add)
                last.then_inc(s("stage_b"), 1)
            done = [0]

            def high(src, dst, i, k, width):
                pairs = [(lo, lo | 1 << k) for lo in range(NHT) if not lo >> k & 1]

                def coef(q, r, col):
                    at = 2 * r + col if i == 0 else 2 * col + r
                    return high_w[:, i, k, q, at:at + 1]

                for q, ab in enumerate(pairs):
                    for r in range(2):
                        last = v.tensor_scalar(dst[:, ab[r], 0:width], src[:, ab[1], 0:width], coef(q, r, 1), None, ALU.mult)
                last.then_inc(s("high"), 1)
                done[0] += 1
                v.wait_ge(s("high"), done[0])
                for q, ab in enumerate(pairs):
                    for r in range(2):
                        last = v.scalar_tensor_tensor(out=dst[:, ab[r], 0:width], in0=src[:, ab[0], 0:width],
                                                      scalar=coef(q, r, 0), in1=dst[:, ab[r], 0:width],
                                                      op0=ALU.mult, op1=ALU.add)
                last.then_inc(s("high"), 1)
                done[0] += 1
                v.wait_ge(s("high"), done[0])

            v.wait_ge(s("up_lowc"), 2)
            high(wexpT, pong, 0, 0, D + 1)
            high(pong, wexpT, 0, 1, D + 1)
            high(wexpT, pong, 0, 2, D + 1)
            v.tensor_tensor(f_hb[:], pong[:, :, D], f_upb[:], ALU.add).then_inc(s("high"), 1)
            done[0] += 1
            v.wait_ge(s("high"), done[0])
            v.wait_ge(s("up_tr"), 1)
            high(f_down, pong, 1, 2, D)
            high(pong, f_down, 1, 1, D)
            high(f_down, pong, 1, 0, D)

        def setup_loads_2(sp):
            sp.dma_start(raw_kv[:], a["L1_xattn_W_kv"].rearrange("(k p) n -> p k n", p=128)).then_inc(s("ld_r"), 16)
            sp.dma_start(c_wq[:], a["L1_xattn_W_q"].rearrange("(k p) n -> p k n", p=128)).then_inc(s("ld_r"), 16)
            sp.wait_ge(s("down_lowc"), 2)
            sp.dma_start(raw_r[:, 0:6, :], a["L1_attn_qkv_w"].rearrange("(m p) d -> p m d", p=128)).then_inc(s("ld_r"), 16)
            sp.dma_start(raw_r[:, 6:8, :], a["L1_attn_out_w"].rearrange("(m p) d -> p m d", p=128)).then_inc(s("ld_r"), 16)
            sp.dma_start(raw_d, a["L1_ffn_w_down"].rearrange("(m p) k -> p m k", p=128)).then_inc(s("ld_d"), 16)
            sp.wait_ge(s("r_wtr"), 1)
            for i, n in enumerate(("gate", "up")):
                sp.dma_start(raw_gu[:, i, :, :], a["L1_ffn_w_" + n].rearrange("(t p) d -> p t d", p=88)).then_inc(s("ld_d"), 16)

        def weights_tensor(pe):
            pe.wait_ge(s("ld_r"), 64)
            pe.wait_ge(s("down_lowc"), 2)
            for k in range(KD):
                for m in range(8):
                    last = pe.transpose(PS[:, 2 * k + m // 4, (m % 4) * 128:(m % 4 + 1) * 128],
                                        raw_r[:, m, k * 128:(k + 1) * 128], ident[:])
            last.then_inc(s("r_wtr"), 1)
            for i in range(2):
                pe.wait_ge(s("m_wcopy"), i + 1)
                pe.wait_ge(s("m_wq"), NQX * 2 * (i + 1))
                for k in range(KD):
                    for t in range(8):
                        last = pe.transpose(PS[:, 2 * k + t // 4, (t % 4) * 88:(t % 4 + 1) * 88],
                                            raw_gu[:, i, t, k * 128:(k + 1) * 128], ident[0:88, 0:88])
                last.then_inc(s("m_wtr"), 1)
            pe.wait_ge(s("m_wcopy"), 3)
            pe.wait_ge(s("m_wq"), NQX * 6)
            for t in range(NTD):
                n = min(128, FF - t * 128)
                for m in range(2):
                    last = pe.transpose(PS[0:n, t // 2, (t % 2) * D + m * 128:(t % 2) * D + (m + 1) * 128],
                                        raw_d[:, m, t * 128:t * 128 + n], ident[:])
            last.then_inc(s("m_wtr"), 1)

        def weights_vector(v):
            v.memset(vv[:, :, :, HD:HD + 1], 1.0).then_inc(s("consts2"), 1)
            v.wait_ge(s("consts2"), 1)
            v.wait_ge(s("r_wtr"), 1)
            for k in range(KD):
                v.tensor_copy(r_w[:, k, 0:512], PS[:, 2 * k, :])
                v.tensor_copy(r_w[:, k, 512:768], PS[:, 2 * k + 1, 0:256])
                last = v.tensor_copy(r_wo[:, k, :], PS[:, 2 * k + 1, 256:512])
            last.then_inc(s("m_wcopy"), 1)
            v.wait_ge(s("m_wcopy"), 1)
            for k in range(KD):
                pairs = r_w[:, k, 0:512].rearrange("p (n e) -> p n e", e=2)
                turned = r_wr[:, k, :].rearrange("p (n e) -> p n e", e=2)
                v.tensor_scalar(turned[:, :, 0], pairs[:, :, 1], -1.0, None, ALU.mult)
                v.tensor_copy(turned[:, :, 1], pairs[:, :, 0])
            v.wait_ge(s("ld_r"), 64)
            v.tensor_copy(c_wk[:], raw_kv[:].rearrange("p k (n e) -> p k n e", e=2)[:, :, :, 0])
            v.tensor_copy(c_wv[:], raw_kv[:].rearrange("p k (n e) -> p k n e", e=2)[:, :, :, 1]).then_inc(s("w_done"), 1)
            v.wait_ge(s("ld_d"), 48)
            at = 0
            for i in range(2):
                for half in range(2):
                    src = raw_gu[:, i, 4 * half:4 * half + 4, :].rearrange("p t (n e) -> p (t n) e", e=BLK)
                    at += quantize(v, s("m_wq"), at, src, src, m_rs[0:88, 0:64], m_sc[0:88, :],
                                   *[blocks(q[0:88], 64) for q in swork])
            for m in range(2):
                src = raw_d[:, m, :].rearrange("p (n e) -> p n e", e=BLK)
                at += quantize(v, s("m_wq"), at, src, src, m_rs[:, 0:NQB], m_sc[:, 0:NQB],
                               *[blocks(q, NQB) for q in swork])
            for i in range(2):
                v.wait_ge(s("m_wtr"), i + 1)
                for k in range(KD):
                    for j in range(2):
                        last = v.tensor_copy(m_wgu[:, k, i, j * FH:(j + 1) * FH], PS[:, 2 * k + j, 0:FH])
                last.then_inc(s("m_wcopy"), 1)
            v.wait_ge(s("m_wtr"), 3)
            v.tensor_copy(m_wd[:, 0:4, :], PS[:, 0:2, :].rearrange("p b (t n) -> p (b t) n", n=D))
            v.tensor_copy(m_wd[:, 4, :], PS[:, 2, 0:D])
            v.tensor_copy(m_wd[0:64, 5, :], PS[0:64, 2, D:2 * D]).then_inc(s("w_done"), 1)

        heads_in = ((qm, kT, vv), (qm_b, kT_b, vv_b))
        PH = PO[:, 1, :]
        Xg = X[:].rearrange("p (g j) d -> p g j d", j=G)
        xnallg = xnall[0:T].rearrange("p (g j) d -> p g j d", j=G)
        hT = big[:, 0:NHT * G * T].rearrange("p (t q) -> p t q", t=NHT)
        rot = big[:, 0:2 * 4 * T].rearrange("p (r i t) -> p r i t", r=2, i=4)
        sq = sb("sq", [128, KD, T + TC])
        p1v = sb("p1v", [T, G, HS])[:]
        p1s = sb("p1s", [T, G, T])[:]
        p1p = sb("p1p", [T, G, T])
        p1pT = sb("p1pT", [T, G * T])[:]
        p1z = sb("p1z", [HS, G * T])[:]

        NCONST, NW = 6, 10
        block = ctx.enter_context(nc.Block())

        @block.sync
        def _(sp):
            with nc.allow_non_contiguous_dma(reason="small biases, feature on partition"):
                sp.dma_start(X[:], a["x"].rearrange("b t d -> t b d")).then_inc(s("ld_x"), 16)
                for i, n in enumerate(("wq", "wk")):
                    sp.dma_start(a_wqk[:, :, i, :], a["L0_attn_" + n].rearrange("(k p) h -> p k h", p=128)).then_inc(s("ld_a"), 16)
                sp.dma_start(a_wv[:], a["L0_attn_wv"].rearrange("(k p) h -> p k h", p=128)).then_inc(s("ld_a"), 16)
                sp.dma_start(a_wo[:], a["L0_attn_wo"]).then_inc(s("ld_a"), 16)
                sp.dma_start(a_bqk[:, 0:1], a["L0_attn_bq"].unsqueeze(1)).then_inc(s("ld_a"), 16)
                sp.dma_start(a_bqk[:, 1:2], a["L0_attn_bk"].unsqueeze(1)).then_inc(s("ld_a"), 16)
                sp.dma_start(a_bv[:], a["L0_attn_bv"].partition_broadcast(T)).then_inc(s("ld_a"), 16)
                sp.dma_start(a_bo[:], a["L0_attn_bo"].partition_broadcast(T)).then_inc(s("ld_a"), 16)
                for t, src in ((x_w, a["L0_xattn_Wqkv"]), (x_wa, a["L0_xattn_Wqkv_aux"][:, D:3 * D]), (x_wo, a["L0_xattn_Wo"])):
                    sp.dma_start(t[:], src.rearrange("(k p) n -> p k n", p=128)).then_inc(s("ld_w"), 16)
                for i in range(2):
                    sp.dma_start(x_bqk[:, i, :], a["L0_xattn_bqkv"][i * D:(i + 1) * D].rearrange("(m p) -> p m", p=128)).then_inc(s("ld_w"), 16)
                sp.dma_start(x_bka[:], a["L0_xattn_bqkv_aux"][D:2 * D].rearrange("(m p) -> p m", p=128)).then_inc(s("ld_w"), 16)
                sp.dma_start(x_bv[:], a["L0_xattn_bqkv"][2 * D:3 * D].partition_broadcast(T)).then_inc(s("ld_w"), 16)
                sp.dma_start(x_bva[:], a["L0_xattn_bqkv_aux"][2 * D:3 * D].partition_broadcast(KT)).then_inc(s("ld_w"), 16)
                sp.dma_start(x_bo[:], a["L0_xattn_bo"].partition_broadcast(T)).then_inc(s("ld_w"), 16)
                sp.dma_start(x_g[:], a["L0_xattn_g"].partition_broadcast(T)).then_inc(s("ld_w"), 16)
                setup_loads_1(sp)
                setup_loads_2(sp)
            sp.dma_start(ctxn[:], ctx_tiles[0]).then_inc(s("ctx"), 16)
            ctx_load(sp, "x_fill", NP, 2)
            sp.wait_ge(s("x_fill"), (B - 1) * NP + 2)
            sp.dma_start(ctxn[:], ctx_tiles[0]).then_inc(s("ctx"), 16)
            ctx_load(sp, "c_fill", NF5, 2)
            sp.wait_ge(s(FINAL[parts][0]), FINAL[parts][1])
            sp.dma_start(out.rearrange("b t d -> t b d"), X[:]).then_inc(s("stored"), 16)
            sp.wait_ge(s("stored"), 16)

        @block.gpsimd
        def _(gp):
            gp.memset(tick_g[:], 0.0).then_inc(s("tick"), 1)
            gp.wait_ge(s("tick"), 1)
            for t, n in ((ident, "ident"), (causal, "causal"), (headmask, "headmask"), (headsum, "headsum")):
                gp.dma_start(t[:], c[n]).then_inc(s("ld_c"), 16)
            gp.dma_start(cosq[:], c["cos"]).then_inc(s("ld_c"), 16)
            gp.dma_start(sinq[:], c["sin"]).then_inc(s("ld_c"), 16)
            gp.wait_ge(s("ld_a"), 16 * 8)
            gp.wait_ge(s("ld_c"), 16 * NCONST)
            gp.wait_ge(s("ld_w"), 16 * NW)
            gp.wait_ge(s("ld_f"), 16 * NF)
            gp.tensor_tensor(f_bo[:], f_bo[:], f_bd[:], ALU.add).then_inc(s("f_bias"), 1)
            p1_gpsimd(gp)
            p2_gpsimd(gp)
            gp.wait_ge(s("f_bias"), 1)
            p3_gpsimd(gp)
            p4_gpsimd(gp)
            p5_gpsimd(gp)
            p6_gpsimd(gp)

        @block.scalar
        def _(act):
            act.wait_ge(s("ld_a"), 16 * 8)
            act.wait_ge(s("ld_w"), 16 * NW)
            act.wait_ge(s("consts"), 3)
            act.preload_act_table_set("natural_log_exp_and_others")
            act.activation(x_gate[:, 1, :], x_g[:], ACT.Exp, scale=-1.0).then_inc(s("gate_exp"), 1)
            fold_scalar(act)
            p1_scalar(act)
            norm_all_scalar(act, "x")
            p2_scalar(act)
            norm_all_scalar(act, "f")
            act.preload_act_table(ACT.Gelu)
            p3_scalar(act)
            act.preload_act_table_set("natural_log_exp_and_others")
            norm_all_scalar(act, "r")
            p4_scalar(act)
            norm_all_scalar(act, "c")
            p5_scalar(act)
            norm_all_scalar(act, "m")
            act.preload_act_table(ACT.Silu)
            p6_scalar(act)

        @block.vector
        def _(v):
            v.memset(eps_ln[:], LN_EPS).then_inc(s("consts"), 1)
            v.memset(eps_rms[:], RMS_EPS).then_inc(s("consts"), 1)
            v.memset(PT[:], 0.0).then_inc(s("consts"), 1)
            v.wait_ge(s("ld_x"), 16)
            v.wait_ge(s("ld_a"), 16 * 8)
            v.wait_ge(s("ld_c"), 16 * NCONST)
            v.wait_ge(s("ld_w"), 16 * NW)
            v.tensor_copy(identb[:], ident[0:T, 0:T]).then_inc(s("consts"), 1)
            v.tensor_scalar(causal4[:], bcast(causal[:], 1, 4), 1e19, None, ALU.mult).then_inc(s("consts"), 1)
            v.wait_ge(s("gate_exp"), 1)
            v.tensor_scalar(x_gate[:, 1, :], x_gate[:, 1, :], 1.0, None, ALU.add).then_inc(s("gate"), 1)
            v.wait_ge(s("gate"), 1)
            v.reciprocal(x_gate[:, 1, :], x_gate[:, 1, :]).then_inc(s("gate"), 1)
            v.wait_ge(s("gate"), 2)
            v.tensor_scalar(x_gate[:, 0, :], x_gate[:, 1, :], -1.0, 1.0, ALU.mult, ALU.add).then_inc(s("gate"), 1)
            fold_vector(v)
            weights_vector(v)
            v.wait_ge(s("w_done"), 2)
            p1_vector(v)
            v.wait_ge(s("a_x"), NG)
            norm_all_vector(v, "x")
            v.wait_ge(s("gate"), 3)
            p2_vector(v)
            v.wait_ge(s("x_x"), B)
            norm_all_vector(v, "f")
            p3_vector(v)
            v.wait_ge(s("f_x"), B)
            norm_all_vector(v, "r")
            p4_vector(v)
            v.wait_ge(s("r_x"), B)
            norm_all_vector(v, "c")
            p5_vector(v)
            v.wait_ge(s("c_x"), B)
            norm_all_vector(v, "m")
            v.wait_ge(s("ln_xn"), NG + NORMS["m"])
            p6_quantize_tokens(v)
            p6_vector(v)

        @block.tensor
        def _(pe):
            pe.wait_ge(s("ld_a"), 16 * 8)
            pe.wait_ge(s("ld_c"), 16 * NCONST)
            pe.wait_ge(s("ld_w"), 16 * NW)
            pe.wait_ge(s("consts"), 5)
            fold_tensor(pe)
            weights_tensor(pe)
            p1_tensor(pe)
            p2_tensor(pe)
            p3_tensor(pe)
            p4_tensor(pe)
            p5_tensor(pe)
            p6_tensor(pe)


def constants():
    import numpy as np
    c = {}
    c["ident"] = np.eye(128, dtype=np.float32)
    up = np.triu(np.ones((T, T), np.float32), 1)
    c["causal"] = up * np.float32(-1e11)
    head = np.arange(128) // HD
    c["headmask"] = (head[:, None] == np.arange(8)[None, :]).astype(np.float32) * np.float32(HD ** -0.5)
    c["headsum"] = (head[:, None] == head[None, :]).astype(np.float32)
    freq = 1.0 / np.float32(10000.0) ** (np.arange(0, HD, 2, dtype=np.float32) / np.float32(HD))
    angle = np.outer(np.arange(T, dtype=np.float32), freq.astype(np.float32)).astype(np.float32)
    rows = angle.T[(np.arange(128) % HD) % (HD // 2)]
    c["cos"], c["sin"] = np.cos(rows).astype(np.float32), np.sin(rows).astype(np.float32)
    p = np.arange(128)
    perm, sel = np.zeros((128, 7, 2, 128), np.float32), np.zeros((64, 7, 2, 128), np.float32)
    for k in range(7):
        perm[p, k, 0, p & ~(1 << k)] = 1
        perm[p, k, 1, p | (1 << k)] = 1
        sel[((p >> (k + 1)) << k) + (p & ((1 << k) - 1)), k, (p >> k) & 1, p] = 1
    c["perm"], c["pair_sel"] = perm, sel
    return c


def kernel(**inputs):
    import numpy as _np
    import concourse.bacc as _bacc
    from concourse import mybir as _mybir
    from concourse.bass_utils import run_bass_kernel_spmd as _run

    nc = _bacc.Bacc("TRN2", target_bir_lowering=False, num_devices=1)
    arrays, args, consts = {}, {}, {}
    for name, value in inputs.items():
        v = _np.ascontiguousarray(value)
        arrays[f"in_{name}"] = v
        args[name] = nc.dram_tensor(f"in_{name}", v.shape, _mybir.dt.from_np(v.dtype), kind="ExternalInput").ap()
    for name, v in constants().items():
        arrays[f"const_{name}"] = v
        consts[name] = nc.dram_tensor(f"const_{name}", v.shape, _mybir.dt.from_np(v.dtype), kind="ExternalInput").ap()
    out = nc.dram_tensor("out", (B, T, D), F32, kind="ExternalOutput").ap()
    build(nc, args, consts, out)
    r = _run(nc, [arrays], core_ids=[0])
    return r.results[0]["out"]
```

```python
from contextlib import ExitStack

import concourse.bass as bass
from concourse import mybir

F32 = mybir.dt.float32
BF16 = mybir.dt.bfloat16
ACT = mybir.ActivationFunctionType
ALU = mybir.AluOpType
AX = mybir.AxisListType

B, T, D = 16, 112, 256
TC, KT = 375, 125
NK = TC // KT
KD = D // 128
G = 4
NG = B // G
H, HD = 16, 16
HS = 64
HID = 1024
NHT = HID // 128
FF = 704
BLK = 16
LN_EPS = 1e-5
RMS_EPS = 1e-6
NQX = 11
NQV = 12
NCH = (B - 2) // 2
CHB = -(-3 * FF * D // 128 // BLK // NCH)
MIDS = (0.25, 0.75, 1.25, 1.75, 2.5, 3.5, 5.0)

FINAL = {1: ("a_x", NG), 2: ("x_x", B), 3: ("f_x", B), 4: ("r_x", B), 5: ("c_x", B), 6: ("m_x", B + 1)}

NORMS = {"a": 0, "x": NG, "f": 2 * NG, "r": 2 * NG + B, "c": 3 * NG + B, "m": 3 * NG + 2 * B}


class Sems:

    def __init__(self, nc, ctx):
        self.nc, self.ctx, self.made = nc, ctx, {}

    def __call__(self, name):
        if name not in self.made:
            self.made[name] = self.ctx.enter_context(self.nc.semaphore(name))
        return self.made[name]


def bcast(ap, dim, n):
    shape = list(ap.shape)
    shape.insert(dim, n)
    return ap.unsqueeze(dim).broadcast_to(shape)


def build(nc, a, c, out, parts=6):
    with ExitStack() as ctx:
        def sb(name, shape, dt=F32):
            return ctx.enter_context(nc.sbuf_tensor(name, shape, dt))

        def ps(name, shape, dt=F32):
            return ctx.enter_context(nc.psum_tensor(name, shape, dt))

        s = Sems(nc, ctx)

        PS = ps("PS", [128, 4, 512])
        PT = ps("PT", [128, 2, 512])
        PO = ps("PO", [128, 2, 512])

        X = sb("X", [T, B, D])
        ident = sb("ident", [128, 128])
        identb = sb("identb", [T, T], BF16)
        causal = sb("causal", [T, T])
        causal4 = sb("causal4", [T, 4, T], BF16)
        headmask = sb("headmask", [128, 8])
        headsum = sb("headsum", [128, 128])
        cosq = sb("cosq", [128, T])
        sinq = sb("sinq", [128, T])

        a_wqk = sb("a_wqk", [128, KD, 2, HS])
        a_wv = sb("a_wv", [128, KD, HS])
        a_wo = sb("a_wo", [HS, D])
        a_bqk = sb("a_bqk", [HS, 2])
        a_bv = sb("a_bv", [T, HS])
        a_bo = sb("a_bo", [T, D])
        x_w = sb("x_w", [128, KD, 3 * D])
        x_wa = sb("x_wa", [128, KD, 2 * D])
        x_wo = sb("x_wo", [128, KD, D])
        x_bqk = sb("x_bqk", [128, 2, KD])
        x_bka = sb("x_bka", [128, KD])
        x_bv = sb("x_bv", [T, D])
        x_bva = sb("x_bva", [KT, D])
        x_bo = sb("x_bo", [T, D])
        x_g = sb("x_g", [T, H])
        x_gate = sb("x_gate", [T, 2, H])

        f_up = sb("f_up", [128, KD, HID])
        f_down = sb("f_down", [128, NHT, D])
        f_hb = sb("f_hb", [128, NHT])
        f_bo = sb("f_bo", [T, D])
        f_bd = sb("f_bd", [T, D])
        r_w = sb("r_w", [128, KD, 3 * D])
        r_wr = sb("r_wr", [128, KD, 2 * D])
        r_wo = sb("r_wo", [128, KD, D])
        c_wq = sb("c_wq", [128, KD, D])
        c_wk = sb("c_wk", [128, KD, D])
        c_wv = sb("c_wv", [128, KD, D])
        m_raw = sb("m_raw", [128, NCH, CHB * BLK])
        m_wgu = (f_up[:, :, 0:FF], f_down[:].rearrange("p t d -> p (t d)")[:, 0:KD * FF].rearrange("p (k n) -> p k n", k=KD))
        m_wd = x_w[:].rearrange("p k n -> p (k n)").rearrange("p (t d) -> p t d", d=D)
        m_rs = sb("m_rs", [128, 64])
        m_sc = sb("m_sc", [128, 64])

        stats = sb("stats", [T, G, 6])
        meanvar = sb("meanvar", [T, G, 2])
        logvar = sb("logvar", [T, G])
        rstd = sb("rstd", [T, G])
        xn = sb("xn", [T, G, D])
        xnT = sb("xnT", [128, KD, G * T])
        tick_v = sb("tick_v", [1, 3])
        tick_g = sb("tick_g", [1, 5])
        eps_ln = sb("eps_ln", [128, 1])
        eps_rms = sb("eps_rms", [128, 1])

        qT = sb("qT", [128, KD, 4 * T])
        kT = sb("kT", [128, KD, T + TC])
        vv = sb("vv", [KT, NK + 1, H, HD + 1])
        qm = sb("qm", [128, H, T])
        ctxn = sb("ctxn", [KT, NK, D])
        ctxT = sb("ctxT", [128, KD, TC])
        prob = sb("prob", [T, 2, 2, T + TC])
        probT = sb("probT", [KT, 2, NK + 1, T])
        negmax = sb("negmax", [T, H, 2])
        sums = sb("sums", [T, 2, 2, H])
        rden = sb("rden", [T, 2, H])
        o_main = sb("o_main", [T, H, HD])
        o_aux = sb("o_aux", [T, H, HD])
        oT = sb("oT", [128, KD, T])
        xnall = sb("xnall", [128, B, D])
        big = sb("big", [128, 8704])

        o = 2 * 3 * 4 * T
        qm_b = big[:, o:o + H * T].rearrange("p (h t) -> p h t", h=H)
        o += H * T
        kT_b = big[:, o:o + KD * (T + TC)].rearrange("p (k t) -> p k t", k=KD)
        o += KD * (T + TC)
        vv_b = big[0:KT, o:o + (NK + 1) * H * (HD + 1)].rearrange("p (t h e) -> p t h e", t=NK + 1, h=H)
        o += (NK + 1) * H * (HD + 1)
        rms = big[:, o:o + KD * (T + TC)].rearrange("p (k t) -> p k t", k=KD)

        def ln_vector(v, n, src, w, nb, dst=None):
            ln_measure(v, n, src, w, nb)
            ln_apply(v, n, src, w, nb, dst)

        def ln_measure(v, n, src, w, nb=1):
            for j in range(nb):
                last = v.bn_stats(stats[:, j, :], src(j))
            last.then_inc(s("ln_stats"), 1)
            v.wait_ge(s("ln_stats"), w + NORMS[n])
            v.memset(tick_v[:, 0:1], 0.0)
            for j in range(nb):
                last = v.bn_aggr(meanvar[:, j, :], stats[:, j, :])
            last.then_inc(s("ln_meanvar"), 1)

        def ln_apply(v, n, src, w, nb=1, dst=None):
            v.wait_ge(s("ln_rstd"), w + NORMS[n])
            for j in range(nb):
                last = v.tensor_scalar(dst(j) if dst else xn[:, j, :], src(j), meanvar[:, j, 0:1], rstd[:, j:j + 1],
                                       ALU.subtract, ALU.mult)
            last.then_inc(s("ln_xn"), 1)

        def ln_scalar(act, n, w, nb):
            act.wait_ge(s("ln_meanvar"), w + NORMS[n])
            act.activation(logvar[:, 0:nb], meanvar[:, 0:nb, 1], ACT.Ln,
                           bias=eps_ln[0:T, :]).then_inc(s("ln_logvar"), 1)
            act.wait_ge(s("ln_logvar"), w + NORMS[n])
            act.activation(rstd[:, 0:nb], logvar[:, 0:nb], ACT.Exp,
                           scale=-0.5).then_inc(s("ln_rstd"), 1)

        def ln_tensor(pe, count, nb, src=xn):
            pe.wait_ge(s("ln_xn"), count)
            for k in range(KD):
                for j in range(nb):
                    last = pe.transpose(PS[:, k, j * T:(j + 1) * T], src[:, j, k * 128:(k + 1) * 128],
                                        ident[0:T, 0:T])
            last.then_inc(s("ln_tr"), 1)

        def ln_copy(act, n, w, nb):
            act.wait_ge(s("ln_tr"), w)
            act.activation(xnT[:, :, 0:nb * T], PS[:, 0:KD, 0:nb * T], ACT.Copy).then_inc(s("ln_xnT"), 1)

        def take_wait(gp, at=0):
            gp.tensor_tensor(tick_g[:, at:at + 1], tick_g[:, 3:4], tick_g[:, 4:5], ALU.add)

        def norm_a(g):
            return g + 1 if isinstance(g, int) and g < 2 else g * 2 - 1

        def groups(engine, body):
            body(0, norm_a(1), None)
            with engine.Fori(1, NG - 1, 1) as g:
                body(g, g * 2 + 1, g * 2 + 2)
            body(NG - 1, None, 2 * NG - 1)

        def p1_vector(v):
            def norm_next(g, w):
                ln_vector(v, "a", lambda j: Xg[:, g, j, :], w, G)

            def norm_last(g, w):
                v.wait_ge(s("a_x"), g + 1)
                v.memset(tick_v[:, 1:2], 0.0)
                ln_vector(v, "a", lambda j: Xg[:, g, j, :], w, G, dst=lambda j: xnallg[:, g, j, :])

            def body(g, w_next, w_last):
                w = g + 1
                v.wait_ge(s("a_qkv"), w)
                v.tensor_scalar(kT[0:HS, 0, 0:G * T], PS[0:HS, 3, 0:G * T], a_bqk[:, 1:2], None,
                                ALU.add).then_inc(s("a_k"), 1)
                v.tensor_tensor(p1v, PO[0:T, 0, 0:G * HS].rearrange("p (j h) -> p j h", j=G),
                                bcast(a_bv[:], 1, G), ALU.add).then_inc(s("a_v"), 1)
                v.wait_ge(s("a_scores"), w)
                v.scalar_tensor_tensor(out=p1s, in0=PT[0:T, 0, 0:G * T].rearrange("p (j k) -> p j k", j=G),
                                       scalar=HS ** -0.5, in1=bcast(causal[:], 1, G),
                                       op0=ALU.mult, op1=ALU.add).then_inc(s("a_masked"), 1)
                v.wait_ge(s("a_masked"), w)
                v.tensor_reduce(negmax[:, 0:G, 0], p1s, AX.X, ALU.max, negate=True).then_inc(s("a_max"), 1)
                v.wait_ge(s("a_probs"), w)
                v.reciprocal(rden[:, 0, 0:G], sums[:, 0, 0, 0:G]).then_inc(s("a_rden"), 1)
                if w_next is not None:
                    if isinstance(g, int):
                        v.wait_ge(s("ld_x"), 16)
                    norm_next(g + 1, w_next)
                if w_last is not None:
                    norm_last(g - 1, w_last)
                v.wait_ge(s("a_rden"), w)
                v.wait_ge(s("a_out"), w)
                v.wait_ge(s("a_xb"), w)
                for j in range(G):
                    last = v.scalar_tensor_tensor(out=Xg[:, g, j, :], in0=PS[0:T, j // 2, (j % 2) * D:(j % 2 + 1) * D],
                                                  scalar=rden[:, 0, j:j + 1], in1=Xg[:, g, j, :],
                                                  op0=ALU.mult, op1=ALU.add)
                last.then_inc(s("a_x"), 1)

            norm_next(0, 1)
            groups(v, body)
            norm_last(NG - 1, 2 * NG)

        def p1_gpsimd(gp):
            for g in range(NG):
                gp.wait_ge(s("ln_xn"), norm_a(g))
                gp.tensor_tensor(Xg[:, g, :, :], Xg[:, g, :, :], bcast(a_bo[:], 1, G), ALU.add).then_inc(s("a_xb"), 1)

        def p1_scalar(act):
            def body(g, w_next, w_last):
                w = g + 1
                ln_copy(act, "a", w, G)
                act.wait_ge(s("a_qkv"), w)
                act.activation(qT[0:HS, 0, 0:G * T], PS[0:HS, 2, 0:G * T], ACT.Identity,
                               bias=a_bqk[:, 0:1]).then_inc(s("a_q"), 1)
                act.wait_ge(s("a_max"), w)
                for j in range(G):
                    last = act.activation(p1p[:, j, :], p1s[:, j, :], ACT.Exp, bias=negmax[:, j, 0:1],
                                          accum_out=sums[:, 0, 0, j:j + 1])
                last.then_inc(s("a_probs"), 1)
                act.wait_ge(s("a_ptr"), w)
                act.activation(p1pT, PT[0:T, 1, 0:G * T], ACT.Copy).then_inc(s("a_pT"), 1)
                if w_next is not None:
                    ln_scalar(act, "a", w_next, G)
                act.wait_ge(s("a_z"), w)
                act.activation(p1z, PO[0:HS, 1, 0:G * T], ACT.Copy).then_inc(s("a_zT"), 1)
                if w_last is not None:
                    ln_scalar(act, "a", w_last, G)

            ln_scalar(act, "a", 1, G)
            groups(act, body)
            ln_scalar(act, "a", 2 * NG, G)

        def p1_tensor(pe):
            def body(g):
                w = g + 1
                if not isinstance(g, int) or g > 0:
                    pe.wait_ge(s("a_x"), g)
                ln_tensor(pe, norm_a(g), G)
                pe.wait_ge(s("ln_xnT"), w)
                for i in range(2):
                    for k in range(KD):
                        pe.matmul(PS[0:HS, 2 + i, 0:G * T], a_wqk[:, k, i, :], xnT[:, k, :],
                                  start=k == 0, stop=k == KD - 1)
                for j in range(G):
                    for k in range(KD):
                        last = pe.matmul(PO[0:T, 0, j * HS:(j + 1) * HS], xnT[:, k, j * T:(j + 1) * T],
                                         a_wv[:, k, :], start=k == 0, stop=k == KD - 1)
                last.then_inc(s("a_qkv"), 1)
                pe.wait_ge(s("a_q"), w)
                pe.wait_ge(s("a_k"), w)
                for j in range(G):
                    last = pe.matmul(PT[0:T, 0, j * T:(j + 1) * T], qT[0:HS, 0, j * T:(j + 1) * T],
                                     kT[0:HS, 0, j * T:(j + 1) * T], start=True, stop=True)
                last.then_inc(s("a_scores"), 1)
                pe.wait_ge(s("a_probs"), w)
                for j in range(G):
                    last = pe.transpose(PT[0:T, 1, j * T:(j + 1) * T], p1p[:, j, :], ident[0:T, 0:T])
                last.then_inc(s("a_ptr"), 1)
                pe.wait_ge(s("a_pT"), w)
                pe.wait_ge(s("a_v"), w)
                for j in range(G):
                    last = pe.matmul(PO[0:HS, 1, j * T:(j + 1) * T], p1v[:, j, :],
                                     p1pT[:, j * T:(j + 1) * T], start=True, stop=True)
                last.then_inc(s("a_z"), 1)
                pe.wait_ge(s("a_zT"), w)
                for j in range(G):
                    last = pe.matmul(PS[0:T, j // 2, (j % 2) * D:(j % 2 + 1) * D],
                                     p1z[:, j * T:(j + 1) * T], a_wo[:], start=True, stop=True)
                last.then_inc(s("a_out"), 1)

            body(0)
            body(1)
            with pe.Fori(2, NG, 1) as g:
                body(g)

        NP = H // 2

        ctx_tiles = a["ctx_1024"].rearrange("b (k p) d -> b p k d", p=KT)

        def ctx_load(sp, read, each, at):
            with sp.Fori(0, B - 1, 1) as b:
                sp.wait_ge(s(read), b * each + at)
                sp.dma_start(ctxn[:], ctx_tiles[b + 1]).then_inc(s("ctx"), 16)

        def queries_gpsimd(gp, n, b, qm=qm):
            gp.wait_ge(s("queries"), b + 1)
            for m in range(KD):
                last = gp.tensor_tensor(qm[:, m * 8:(m + 1) * 8, :], bcast(qT[:, m, 0:T], 1, 8),
                                        bcast(headmask[:], 2, T), ALU.mult)
            last.then_inc(s("queries_by_head"), 1)

        def fills(r, i):
            if isinstance(r, int) and r >= B:
                return B * NP + 2 * (r - B) + (i - 1)
            return r * NP + (i + 1)

        def rounds(engine, body, side=None):
            body(0, 1, True, False, False)
            body(1, 0, True, True, False)
            with engine.Fori(0, NCH, 1) as c:
                body(c * 2 + 2, 1, True, True, True, *([lambda i: side(c, i)] if side else []))
                body(c * 2 + 3, 0, True, True, True, *([lambda i: side(c, NP + i)] if side else []))
            body(B, 1, False, True, True)
            body(B + 1, 0, False, False, True)

        def p2_tensor(pe):
            def scores(q, k, i):
                for e in range(2):
                    h = 2 * i + e
                    last = pe.matmul(PS[0:T, 2 * (i % 2) + e, 0:T + TC], q[:, h, :], k[:, h // 8, :],
                                     start=True, stop=True)
                last.then_inc(s("x_scores"), 1)

            def fill(r, i, ins, outs):
                if not ins and (not outs or i not in (2, 3)):
                    return
                if not (isinstance(r, int) and r == 0 and i == 0):
                    pe.wait_ge(s("x_empty"), fills(r, i) - 1)
                if i < 2:
                    if i == 0:
                        pe.wait_ge(s("ctx"), r * 16 + 16)
                    for t in range(NK):
                        last = pe.transpose(PH[:, t * KT:(t + 1) * KT], ctxn[:, t, i * 128:(i + 1) * 128],
                                            ident[0:KT, 0:KT])
                if i == 2 and ins:
                    pe.wait_ge(s("x_xs"), r + 1)
                    for k in range(KD):
                        last = pe.transpose(PH[:, k * T:(k + 1) * T], xn[:, 0, k * 128:(k + 1) * 128], ident[0:T, 0:T])
                if i == 2 and outs:
                    pe.wait_ge(s("x_o"), (r - 2) * 4 + 4)
                    for k in range(KD):
                        last = pe.transpose(PH[:, (KD + k) * T:(KD + k + 1) * T],
                                            o_main[:].rearrange("p h e -> p (h e)")[:, k * 128:(k + 1) * 128],
                                            ident[0:T, 0:T])
                if i == 3 and ins:
                    for m in range(KD):
                        for k in range(KD):
                            last = pe.matmul(PH[:, m * T:(m + 1) * T], x_w[:, k, m * 128:(m + 1) * 128], xnT[:, k, 0:T],
                                             start=k == 0, stop=k == KD - 1)
                if i == 3 and outs:
                    for k in range(KD):
                        last = pe.matmul(PH[0:T, D:2 * D], oT[:, k, :], x_wo[:, k, :], start=k == 0, stop=k == KD - 1)
                if i in (4, 5):
                    m = i - 4
                    for k in range(KD):
                        pe.matmul(PH[:, 0:T], x_w[:, k, D + m * 128:D + (m + 1) * 128], xnT[:, k, 0:T],
                                  start=k == 0, stop=k == KD - 1)
                    for k in range(KD):
                        last = pe.matmul(PH[:, T:T + TC], x_wa[:, k, m * 128:(m + 1) * 128], ctxT[:, k, :],
                                         start=k == 0, stop=k == KD - 1)
                if i == 6:
                    for k in range(KD):
                        pe.matmul(PH[0:T, D:2 * D], xnT[:, k, 0:T], x_w[:, k, 2 * D:3 * D], start=k == 0, stop=k == KD - 1)
                if i in (6, 7):
                    for t in ((0,), (1, 2))[i - 6]:
                        for k in range(KD):
                            last = pe.matmul(PH[0:KT, (t + 1) % 2 * D:((t + 1) % 2 + 1) * D] if i == 7 else PH[0:KT, 0:D],
                                             ctxT[:, k, t * KT:(t + 1) * KT], x_wa[:, k, D:2 * D],
                                             start=k == 0, stop=k == KD - 1)
                last.then_inc(s("x_fill"), 1)

            def body(r, own, ins, heads, outs):
                q, k, v = heads_in[own]
                q2, k2, _ = heads_in[1 - own]
                for i in range(NP):
                    if heads:
                        pe.wait_ge(s("x_probs"), (r - 1) * NP + (i + 1))
                        for e in range(2):
                            for t in range(NK):
                                pe.transpose(PT[0:KT, e, t * T:(t + 1) * T],
                                             prob[:, i % 2, e, T + t * KT:T + (t + 1) * KT], ident[0:T, 0:T])
                            last = pe.transpose(PT[0:T, e, NK * T:(NK + 1) * T], prob[:, i % 2, e, 0:T], ident[0:T, 0:T])
                        last.then_inc(s("x_ptr"), 1)
                    fill(r, i, ins, outs)
                    if heads and i + 2 < NP:
                        scores(q, k, i + 2)
                    if ins and i + 2 >= NP:
                        if i + 2 == NP:
                            pe.wait_ge(s("queries_by_head"), r + 1)
                        scores(q2, k2, i + 2 - NP)
                    if heads:
                        if i == 0 and outs:
                            pe.wait_ge(s("x_o"), (r - 2) * 4 + 3)
                        pe.wait_ge(s("x_pTs"), (r - 1) * NP + (i + 1))
                        pe.wait_ge(s("x_pTv"), (r - 1) * NP + (i + 1))
                        for e in range(2):
                            h = 2 * i + e
                            pe.matmul(PO[0:T, 0, h * HD:(h + 1) * HD], probT[0:T, e, NK, :], v[0:T, NK, h, 0:HD],
                                      start=True, stop=True)
                            for t in range(NK):
                                last = pe.matmul(PO[0:T, 0, D + h * HD:D + (h + 1) * HD], probT[:, e, t, :],
                                                 v[:, t, h, 0:HD], start=t == 0, stop=t == NK - 1)
                        last.then_inc(s("x_pv"), 1)

            rounds(pe, body)

        def p2_scalar(act):
            def body(r, own, ins, heads, outs):
                for i in range(NP):
                    if outs and i == 6:
                        ln_scalar(act, "f", r - 1, 1)
                    if not heads:
                        continue
                    at = (r - 1) * NP + (i + 1)
                    act.wait_ge(s("x_max"), at)
                    for e in range(2):
                        for part, (lo, hi) in enumerate(((0, T), (T, T + TC))):
                            last = act.activation(prob[:, i % 2, e, lo:hi], PS[0:T, 2 * (i % 2) + e, lo:hi], ACT.Exp,
                                                  bias=negmax[:, 2 * i + e, part:part + 1],
                                                  accum_out=sums[:, own, part, 2 * i + e:2 * i + e + 1])
                    last.then_inc(s("x_probs"), 1)
                    act.wait_ge(s("x_ptr"), at)
                    act.activation(probT[:, 0, :, :].rearrange("p t q -> p (t q)"), PT[0:KT, 0, 0:(NK + 1) * T],
                                   ACT.Copy).then_inc(s("x_pTs"), 1)

            rounds(act, body)

        def p2_vector(v):
            def maxima(r, i):
                v.wait_ge(s("x_scores"), (r - 1) * NP + (i + 1))
                for part, (lo, hi) in enumerate(((0, T), (T, T + TC))):
                    last = v.tensor_reduce(negmax[:, 2 * i:2 * i + 2, part],
                                           PS[0:T, 2 * (i % 2):2 * (i % 2) + 2, lo:hi], AX.X, ALU.max, negate=True)
                last.then_inc(s("x_max"), 1)

            def outputs(r, which):
                at = (r - 2) * 4
                v.wait_ge(s("x_probs"), (r - 1) * NP)
                v.reciprocal(rden[:], sums[:, which]).then_inc(s("x_o"), 1)
                v.wait_ge(s("x_o"), at + 1)
                v.tensor_tensor(rden[:], rden[:], x_gate[:], ALU.mult).then_inc(s("x_o"), 1)
                v.wait_ge(s("x_o"), at + 2)
                v.wait_ge(s("x_pv"), (r - 1) * NP)
                v.tensor_tensor(o_main[:], PO[0:T, 0, 0:D].rearrange("p (h e) -> p h e", h=H),
                                bcast(rden[:, 0, :], 2, HD), ALU.mult)
                v.tensor_tensor(o_aux[:], PO[0:T, 0, D:2 * D].rearrange("p (h e) -> p h e", h=H),
                                bcast(rden[:, 1, :], 2, HD), ALU.mult).then_inc(s("x_o"), 1)
                v.wait_ge(s("x_o"), at + 3)
                v.tensor_tensor(o_main[:], o_main[:], o_aux[:], ALU.add).then_inc(s("x_o"), 1)

            def empty(r, i, k, vals, ins, outs):
                if not ins and (not outs or i not in (2, 3)):
                    return
                v.wait_ge(s("x_fill"), fills(r, i))
                if i < 2:
                    last = v.tensor_copy(ctxT[:, i, :], PH[:, 0:TC])
                if i == 2 and ins:
                    last = v.tensor_copy(xnT[:, :, 0:T], PH[:, 0:KD * T].rearrange("p (k t) -> p k t", k=KD))
                if i == 2 and outs:
                    last = v.tensor_copy(oT[:].rearrange("p k t -> p (k t)"), PH[:, KD * T:2 * KD * T])
                if i == 3 and ins:
                    if not (isinstance(r, int) and r == 0):
                        v.wait_ge(s("queries_by_head"), r)
                    for m in range(KD):
                        last = v.tensor_scalar(qT[:, m, 0:T], PH[:, m * T:(m + 1) * T], x_bqk[:, 0, m:m + 1], None, ALU.add)
                    last.then_inc(s("queries"), 1)
                if i == 3 and outs:
                    v.wait_ge(s("x_xb"), r - 1)
                    v.tensor_tensor(X[:, r - 2, :], PH[0:T, D:2 * D], X[:, r - 2, :], ALU.add).then_inc(s("x_x"), 1)
                if i == 3:
                    last = v.memset(tick_v[:, 0:1], 0.0)
                if i in (4, 5):
                    m = i - 4
                    v.tensor_scalar(k[:, m, 0:T], PH[:, 0:T], x_bqk[:, 1, m:m + 1], None, ALU.add)
                    last = v.tensor_scalar(k[:, m, T:T + TC], PH[:, T:T + TC], x_bka[:, m:m + 1], None, ALU.add)
                if i == 6:
                    v.tensor_tensor(vals[0:T, NK, :, 0:HD], PH[0:T, D:2 * D].rearrange("p (h e) -> p h e", h=H),
                                    x_bv[:].rearrange("p (h e) -> p h e", h=H), ALU.add)
                    last = v.tensor_tensor(vals[:, 0, :, 0:HD], PH[0:KT, 0:D].rearrange("p (h e) -> p h e", h=H),
                                           x_bva[:].rearrange("p (h e) -> p h e", h=H), ALU.add)
                if i == 7:
                    last = v.tensor_tensor(vals[:, 1:3, :, 0:HD], PH[0:KT, :].rearrange("p (t h e) -> p t h e", t=2, h=H),
                                           bcast(x_bva[:].rearrange("p (h e) -> p h e", h=H), 1, 2), ALU.add)
                last.then_inc(s("x_empty"), 1)

            def quantize_weights(c, step):
                if step >= NQX:
                    return
                src = m_raw[:, c, :].rearrange("p (n e) -> p n e", e=BLK)
                if step > 0:
                    v.wait_ge(s("m_wq"), c * NQX + step)
                quantize_step(v, step, src, src, m_rs[:, 0:CHB], m_sc[:, 0:CHB],
                              *[blocks(q, CHB) for q in swork]).then_inc(s("m_wq"), 1)

            def body(r, own, ins, heads, outs, side=None):
                _, k, vals = heads_in[1 - own]
                if outs:
                    outputs(r, 1 - own)
                for i in range(NP):
                    if heads and i + 1 < NP:
                        maxima(r, i + 1)
                    if heads:
                        if i == 7 and ins:
                            maxima(r + 1, 0)
                        v.wait_ge(s("x_ptr"), (r - 1) * NP + (i + 1))
                        v.tensor_copy(probT[:, 1, :, :].rearrange("p t q -> p (t q)"),
                                      PT[0:KT, 1, 0:(NK + 1) * T]).then_inc(s("x_pTv"), 1)
                    empty(r, i, k, vals, ins, outs)
                    if outs and i == 3:
                        v.wait_ge(s("x_x"), r - 1)
                        v.memset(tick_v[:, 1:2], 0.0)
                        ln_measure(v, "f", lambda j: X[:, r - 2, :], r - 1)
                    if outs and i == 6:
                        ln_apply(v, "f", lambda j: X[:, r - 2, :], r - 1, dst=lambda j: xnall[0:T, r - 2, :])
                    if side:
                        side(i)
                if ins and not heads:
                    maxima(r + 1, 0)

            rounds(v, body, quantize_weights)

        def p2_gpsimd(gp):
            def body(b, q, first=False):
                if first:
                    gp.wait_ge(s("ln_xn"), 1 + NORMS["x"])
                    gp.wait_ge(s("a_x"), NG)
                else:
                    gp.wait_ge(s("x_fill"), (b - 1) * NP + 3)
                take_wait(gp)
                gp.tensor_copy(xn[:, 0, :], xnall[0:T, b, :]).then_inc(s("x_xs"), 1)
                gp.tensor_tensor(X[:, b, :], X[:, b, :], x_bo[:], ALU.add).then_inc(s("x_xb"), 1)
                queries_gpsimd(gp, "x", b, q)

            body(0, heads_in[0][0], True)
            gp.wait_ge(s("ln_xn"), NG + NORMS["x"])
            with gp.Fori(1, B - 1, 2) as b:
                body(b, heads_in[1][0])
                body(b + 1, heads_in[0][0])
            body(B - 1, heads_in[1][0])

        def p3_tensor(pe):
            with pe.Fori(0, NG, 1) as g:
                w = g + 1
                pe.wait_ge(s("f_xs"), w)
                for k in range(KD):
                    for j in range(G):
                        last = pe.transpose(PT[:, k, j * T:(j + 1) * T], xn[:, j, k * 128:(k + 1) * 128],
                                            ident[0:T, 0:T])
                last.then_inc(s("f_tr"), 1)
                pe.wait_ge(s("f_xnT"), w)
                for t in range(NHT):
                    if t >= 4:
                        pe.wait_ge(s("f_h"), g * NHT + (t - 3))
                    for k in range(KD):
                        last = pe.matmul(PS[:, t % 4, 0:G * T], f_up[:, k, t * 128:(t + 1) * 128], xnT[:, k, :],
                                         start=k == 0, stop=k == KD - 1)
                    last.then_inc(s("f_hp"), 1)
                pe.wait_ge(s("f_h"), g * NHT + NHT)
                for j in range(G):
                    if j >= 2:
                        pe.wait_ge(s("f_x"), g * G + (j - 1))
                    for t in range(NHT):
                        last = pe.matmul(PO[0:T, j % 2, 0:D], hT[:, t, j * T:(j + 1) * T], f_down[:, t, :],
                                         start=t == 0, stop=t == NHT - 1)
                    last.then_inc(s("f_y"), 1)

        def p3_scalar(act):
            def norm(g):
                act.preload_act_table_set("natural_log_exp_and_others")
                ln_scalar(act, "r", g + 1, G)

            def hidden(g):
                act.preload_act_table(ACT.Gelu)
                for t in range(NHT):
                    act.wait_ge(s("f_hp"), g * NHT + (t + 1))
                    act.activation(hT[:, t, :], PS[:, t % 4, 0:G * T], ACT.Gelu,
                                   bias=f_hb[:, t:t + 1]).then_inc(s("f_h"), 1)

            hidden(0)
            with act.Fori(1, NG, 1) as g:
                norm(g - 1)
                hidden(g)
            norm(NG - 1)

        def p3_vector(v):
            def norm(g):
                v.wait_ge(s("f_x"), g * G + G)
                v.memset(tick_v[:, 1:2], 0.0)
                ln_vector(v, "r", lambda j: Xg[:, g, j, :], g + 1, G, dst=lambda j: xnallg[:, g, j, :])

            def body(g, norm_last):
                w = g + 1
                v.wait_ge(s("f_tr"), w + 1)
                v.tensor_copy(xnT[:], PT[:, :, 0:G * T]).then_inc(s("f_xnT"), 1)
                if norm_last:
                    norm(g - 1)
                v.wait_ge(s("f_xb"), w)
                for j in range(G):
                    v.wait_ge(s("f_y"), g * G + (j + 1))
                    v.tensor_tensor(Xg[:, g, j, :], PO[0:T, j % 2, 0:D], Xg[:, g, j, :], ALU.add).then_inc(s("f_x"), 1)

            body(0, False)
            with v.Fori(1, NG, 1) as g:
                body(g, True)
            norm(NG - 1)

        def p3_gpsimd(gp):
            gp.sem_inc(s("f_tr"), 1)
            with gp.Fori(0, NG, 1) as g:
                w = g + 1
                gp.wait_ge(s("ln_xn"), g * G + (G + NORMS["f"]))
                gp.wait_ge(s("f_tr"), w)
                take_wait(gp)
                gp.tensor_copy(xn[:], xnallg[:, g, :, :]).then_inc(s("f_xs"), 1)
                gp.tensor_tensor(Xg[:, g, :, :], Xg[:, g, :, :], bcast(f_bo[:], 1, G), ALU.add).then_inc(s("f_xb"), 1)

        NQ = H // 4
        prob4 = prob[:].rearrange("p s e c -> p s (e c)")[:, :, 0:4 * T]
        probT4 = probT[:].rearrange("p s t q -> p s (t q)")

        def fills4(r, f):
            if isinstance(r, int) and r >= B:
                return B * 4 + 2 * (r - B) + (1 if f == 0 else 2)
            return r * 4 + (f + 1)

        def by_half(gp, n, b, q):
            for m in range(KD):
                gp.wait_ge(s(n + "_q"), b * 2 + (m + 1))
                gp.tensor_tensor(q[:, m * 8:(m + 1) * 8, :], bcast(qT[:, m, 0:T], 1, 8),
                                 bcast(headmask[:], 2, T), ALU.mult).then_inc(s(n + "_qm"), 1)

        def p4_tensor(pe):
            def scores(q, k, i):
                pe.matmul(PS[0:T, i % 2, 0:4 * T], identb[:], causal4[:].rearrange("p h k -> p (h k)"),
                          start=True, stop=False, skip_group_check=True)
                for e in range(4):
                    h = 4 * i + e
                    last = pe.matmul(PS[0:T, i % 2, e * T:(e + 1) * T], q[:, h, :], k[:, h // 8, 0:T],
                                     start=False, stop=e == 3, skip_group_check=True)
                last.then_inc(s("r_scores"), 1)

            def fill(r, f, ins, outs):
                if not ins and (not outs or f not in (0, 3)):
                    return
                if not (isinstance(r, int) and r == 0 and f == 0) and (f < 2 or not ins):
                    pe.wait_ge(s("r_empty"), fills4(r, f) - 1)
                if f == 0 and ins:
                    pe.wait_ge(s("r_xs"), r + 1)
                    for k in range(KD):
                        last = pe.transpose(PS[:, 2, k * T:(k + 1) * T], xn[:, 0, k * 128:(k + 1) * 128], ident[0:T, 0:T])
                if f == 0 and outs:
                    pe.wait_ge(s("r_o"), (r - 2) * 2 + 2)
                    for k in range(KD):
                        last = pe.transpose(PS[:, 2, (KD + k) * T:(KD + k + 1) * T],
                                            o_main[:].rearrange("p h e -> p (h e)")[:, k * 128:(k + 1) * 128],
                                            ident[0:T, 0:T])
                if f in (1, 2):
                    for j, wt in enumerate((r_w, r_wr)):
                        for m in range(KD):
                            c0 = (f - 1) * D + m * 128
                            for k in range(KD):
                                last = pe.matmul(PS[:, 1 + f, (KD * j + m) * T:(KD * j + m + 1) * T],
                                                 wt[:, k, c0:c0 + 128], xnT[:, k, 0:T], start=k == 0, stop=k == KD - 1)
                if f == 3 and ins:
                    for k in range(KD):
                        last = pe.matmul(PH[0:T, 0:D], xnT[:, k, 0:T], r_w[:, k, 2 * D:3 * D],
                                         start=k == 0, stop=k == KD - 1)
                if f == 3 and outs:
                    for k in range(KD):
                        last = pe.matmul(PH[0:T, D:2 * D], oT[:, k, :], r_wo[:, k, :], start=k == 0, stop=k == KD - 1)
                last.then_inc(s("r_fill"), 1)

            def body(r, own, ins, heads, outs):
                q, k, v = heads_in[own]
                q2, k2, _ = heads_in[1 - own]
                for i in range(NQ):
                    if heads:
                        pe.wait_ge(s("r_probs"), (r - 1) * NQ + (i + 1))
                        for e in range(4):
                            last = pe.transpose(PT[0:T, i % 2, e * T:(e + 1) * T], prob4[:, i % 2, e * T:(e + 1) * T],
                                                ident[0:T, 0:T])
                        last.then_inc(s("r_ptr"), 1)
                        if i + 2 < NQ:
                            if i == 0:
                                pe.wait_ge(s("r_qm"), (r - 1) * 2 + 2)
                            scores(q, k, i + 2)
                        if i == 0 and outs:
                            pe.wait_ge(s("r_o"), (r - 2) * 2 + 2)
                        pe.wait_ge(s("r_pT"), (r - 1) * NQ + (i + 1))
                        for e in range(4):
                            h = 4 * i + e
                            last = pe.matmul(PO[0:T, 0, h * HD:(h + 1) * HD], probT4[0:T, i % 2, e * T:(e + 1) * T],
                                             v[0:T, NK, h, 0:HD], start=True, stop=True)
                        last.then_inc(s("r_pv"), 1)
                    for f in ((0,), (1, 2), (3,), ())[i]:
                        fill(r, f, ins, outs)
                if ins:
                    pe.wait_ge(s("r_qm"), r * 2 + 1)
                    pe.wait_ge(s("r_empty"), r * 4 + 4)
                    scores(q2, k2, 0)
                    scores(q2, k2, 1)

            rounds(pe, body)

        def p4_scalar(act):
            def body(r, own, ins, heads, outs):
                for i in range(NQ if heads else 0):
                    at = (r - 1) * NQ + (i + 1)
                    act.wait_ge(s("r_max"), at)
                    for e in range(4):
                        h = 4 * i + e
                        last = act.activation(prob4[:, i % 2, e * T:(e + 1) * T], PS[0:T, i % 2, e * T:(e + 1) * T],
                                              ACT.Exp, bias=negmax[:, h, 0:1], accum_out=sums[:, own, 0, h:h + 1])
                    last.then_inc(s("r_probs"), 1)
                    act.wait_ge(s("r_ptr"), at)
                    act.activation(probT4[0:T, i % 2, :], PT[0:T, i % 2, 0:4 * T], ACT.Copy).then_inc(s("r_pT"), 1)
                if outs:
                    ln_scalar(act, "c", r - 1, 1)

            rounds(act, body)

        def p4_vector(v):
            def maxima(r, i):
                v.wait_ge(s("r_scores"), (r - 1) * NQ + (i + 1))
                v.tensor_reduce(negmax[:, 4 * i:4 * i + 4, 0], PS[0:T, i % 2, 0:4 * T].rearrange("p (h k) -> p h k", h=4),
                                AX.X, ALU.max, negate=True).then_inc(s("r_max"), 1)

            def outputs(r, which):
                v.wait_ge(s("r_probs"), (r - 1) * NQ)
                v.reciprocal(rden[:, 0, :], sums[:, which, 0, :]).then_inc(s("r_o"), 1)
                v.wait_ge(s("r_o"), (r - 2) * 2 + 1)
                v.wait_ge(s("r_pv"), (r - 1) * NQ)
                v.tensor_tensor(o_main[:], PO[0:T, 0, 0:D].rearrange("p (h e) -> p h e", h=H),
                                bcast(rden[:, 0, :], 2, HD), ALU.mult).then_inc(s("r_o"), 1)

            def empty(r, f, k2, vals, ins, outs):
                if not ins and (not outs or f not in (0, 3)):
                    return
                v.wait_ge(s("r_fill"), fills4(r, f))
                if f == 0 and ins:
                    last = v.tensor_copy(xnT[:, :, 0:T], PS[:, 2, 0:KD * T].rearrange("p (k t) -> p k t", k=KD))
                if f == 0 and outs:
                    last = v.tensor_copy(oT[:].rearrange("p k t -> p (k t)"), PS[:, 2, KD * T:2 * KD * T])
                if f in (1, 2):
                    for j, table in enumerate((cosq, sinq)):
                        last = v.tensor_tensor(rot[:, j, 2 * f - 2:2 * f, :],
                                               PS[:, 1 + f, j * KD * T:(j + 1) * KD * T].rearrange("p (m t) -> p m t", m=KD),
                                               bcast(table[:], 1, KD), ALU.mult)
                    last.then_inc(s("r_rot"), 1)
                    v.wait_ge(s("r_rot"), r * 2 + f)
                    if f == 1 and not (isinstance(r, int) and r == 0):
                        v.wait_ge(s("r_qm"), r * 2)
                    if f == 1:
                        v.tensor_tensor(qT[:, :, 0:T], rot[:, 0, 0:2, :], rot[:, 1, 0:2, :], ALU.add).then_inc(s("r_q"), 2)
                        last = v.memset(tick_v[:, 0:1], 0.0)
                    else:
                        last = v.tensor_tensor(k2[:, :, 0:T], rot[:, 0, 2:4, :], rot[:, 1, 2:4, :], ALU.add)
                if f == 3 and ins:
                    last = v.tensor_copy(vals[0:T, NK, :, 0:HD], PH[0:T, 0:D].rearrange("p (h e) -> p h e", h=H))
                if f == 3 and outs:
                    v.tensor_tensor(X[:, r - 2, :], PH[0:T, D:2 * D], X[:, r - 2, :], ALU.add).then_inc(s("r_x"), 1)
                    last = v.memset(tick_v[:, 0:1], 0.0)
                last.then_inc(s("r_empty"), 1)

            def body(r, own, ins, heads, outs):
                _, k2, vals = heads_in[1 - own]
                if outs:
                    outputs(r, 1 - own)
                for i in range(NQ):
                    if heads and i + 2 < NQ:
                        maxima(r, i + 2)
                    for f in ((0,), (1, 2), (3,), ())[i]:
                        empty(r, f, k2, vals, ins, outs)
                    if outs and i == 2:
                        v.wait_ge(s("r_x"), r - 1)
                        v.memset(tick_v[:, 1:2], 0.0)
                        ln_measure(v, "c", lambda j: X[:, r - 2, :], r - 1)
                if ins:
                    maxima(r + 1, 0)
                    maxima(r + 1, 1)
                if outs:
                    ln_apply(v, "c", lambda j: X[:, r - 2, :], r - 1, dst=lambda j: xnall[0:T, r - 2, :])

            rounds(v, body)

        def p4_gpsimd(gp):
            def body(b, q, first=False):
                if not first:
                    gp.wait_ge(s("r_fill"), (b - 1) * 4 + 1)
                    take_wait(gp)
                gp.tensor_copy(xn[:, 0, :], xnall[0:T, b, :]).then_inc(s("r_xs"), 1)
                by_half(gp, "r", b, q)

            gp.wait_ge(s("ln_xn"), NORMS["c"])
            body(0, heads_in[0][0], True)
            with gp.Fori(1, B - 1, 2) as b:
                body(b, heads_in[1][0])
                body(b + 1, heads_in[0][0])
            body(B - 1, heads_in[1][0])

        NT5 = NQ * NK
        prob5 = big[:, 0:2 * NK * 4 * T].rearrange("p (s t q) -> p s t q", s=2, t=NK)

        NF5 = 9
        STEP5 = ((0, 1), (2,), (3,), (4,), (5,), (6,), (7,), (8,))
        BANK_A, BANK_B = PT[:, 0, :], PT[:, 1, :]

        def p5_tensor(pe):
            def scores(q, k, n):
                i, t = n // NK, n % NK
                pe.matmul(PS[0:KT, n % 4, 0:4 * T], k[:, i // 2, T + t * KT:T + (t + 1) * KT],
                          q[:, 4 * i:4 * i + 4, :].rearrange("p h q -> p (h q)"),
                          start=True, stop=True).then_inc(s("c_scores"), 1)

            def fill(r, f):
                first = isinstance(r, int) and r == 0
                if f < 2:
                    if f == 0:
                        pe.wait_ge(s("ctx"), r * 16 + 16 * (B + 1))
                        if not first:
                            pe.wait_ge(s("c_emptyv"), r * 7)
                    for t in range(NK):
                        last = pe.transpose((BANK_A, BANK_B)[f][:, t * KT:(t + 1) * KT],
                                            ctxn[:, t, f * 128:(f + 1) * 128], ident[0:KT, 0:KT])
                if f == 2:
                    pe.wait_ge(s("c_xs"), r + 1)
                    for k in range(KD):
                        last = pe.transpose(PH[:, k * T:(k + 1) * T], xn[:, 0, k * 128:(k + 1) * 128], ident[0:T, 0:T])
                if f in (3, 4):
                    m = f - 3
                    if f == 3:
                        pe.wait_ge(s("c_emptyv"), r * 7 + 3)
                        if not first:
                            pe.wait_ge(s("c_rs"), r * 2)
                    bank = (BANK_A, BANK_B)[m]
                    for k in range(KD):
                        pe.matmul(bank[:, 0:T], c_wq[:, k, m * 128:(m + 1) * 128], xnT[:, k, 0:T],
                                  start=k == 0, stop=k == KD - 1)
                    for k in range(KD):
                        last = pe.matmul(bank[:, T:T + TC], c_wk[:, k, m * 128:(m + 1) * 128], ctxT[:, k, :],
                                         start=k == 0, stop=k == KD - 1)
                if f == 6:
                    pe.wait_ge(s("c_emptys"), r * 4 + 1)
                    pe.wait_ge(s("c_emptyv"), r * 7 + 4)
                if f == 7:
                    pe.wait_ge(s("c_emptys"), r * 4 + 3)
                if f in (6, 7):
                    last = pe.matmul(PH[:, 0:T + TC], headsum[:], sq[:, f - 6, :], start=True, stop=True)
                if f == 8:
                    pe.wait_ge(s("c_emptys"), r * 4 + 4)
                if f in (5, 8):
                    for t in ((0, 1) if f == 5 else (2,)):
                        for k in range(KD):
                            last = pe.matmul(PH[0:KT, t % 2 * D:(t % 2 + 1) * D], ctxT[:, k, t * KT:(t + 1) * KT],
                                             c_wv[:, k, :], start=k == 0, stop=k == KD - 1)
                last.then_inc(s("c_fill"), 1)

            def body(r, own, ins, heads, outs):
                q, k, v = heads_in[own]
                q2, k2, _ = heads_in[1 - own]
                for n in range(NT5):
                    if ins and n < len(STEP5):
                        for f in STEP5[n]:
                            fill(r, f)
                    if heads:
                        pe.wait_ge(s("c_probs"), (r - 1) * NT5 + (n + 1))
                        if n == 2:
                            pe.wait_ge(s("c_emptyv"), (r - 1) * 7 + 7)
                            pe.wait_ge(s("c_qm"), (r - 1) * 2 + 2)
                        if n + 4 < NT5:
                            scores(q, k, n + 4)
                    if ins and n + 4 >= NT5:
                        if n + 4 == NT5:
                            pe.wait_ge(s("c_qm"), r * 2 + 1)
                            pe.wait_ge(s("c_emptyv"), r * 7 + 5)
                        scores(q2, k2, n + 4 - NT5)
                    if heads and n % NK == NK - 1:
                        i = n // NK
                        if i == 0 and outs:
                            pe.wait_ge(s("c_o"), (r - 2) * 2 + 2)
                        for e in range(4):
                            h = 4 * i + e
                            for t in range(NK):
                                last = pe.matmul(PO[0:T, 0, h * (HD + 1):(h + 1) * (HD + 1)],
                                                 prob5[0:KT, i % 2, t, e * T:(e + 1) * T], v[:, t, h, :],
                                                 start=t == 0, stop=t == NK - 1)
                        last.then_inc(s("c_pv"), 1)

            rounds(pe, body)

        def p5_scalar(act):
            def body(r, own, ins, heads, outs):
                def inputs(n):
                    if n in (3, 4):
                        m = n - 3
                        act.wait_ge(s("c_fill"), r * NF5 + (4 + m))
                        act.activation(sq[:, m, :], (BANK_A, BANK_B)[m][:, 0:T + TC], ACT.Square).then_inc(s("c_emptys"), 1)
                    if n in (6, 7):
                        m = n - 6
                        act.wait_ge(s("c_fill"), r * NF5 + (7 + m))
                        if m == 0 and not (isinstance(r, int) and r == 0):
                            act.wait_ge(s("c_emptyv"), r * 7)
                        act.activation(rms[:, m, :], PH[:, 0:T + TC], ACT.Ln, scale=1.0 / HD,
                                       bias=eps_rms[:]).then_inc(s("c_emptys"), 1)
                        act.wait_ge(s("c_emptys"), r * 4 + (3 + m))
                        act.activation(rms[:, m, :], rms[:, m, :], ACT.Exp, scale=-0.5).then_inc(s("c_rs"), 1)

                for n in range(NT5 if heads or ins else 0):
                    if heads:
                        i, t = n // NK, n % NK
                        act.wait_ge(s("c_scores"), (r - 1) * NT5 + (n + 1))
                        if t == 0 and (i >= 2 or outs):
                            act.wait_ge(s("c_pv"), (r - 1) * NQ + (i - 1))
                        act.activation(prob5[0:KT, i % 2, t, :], PS[0:KT, n % 4, 0:4 * T], ACT.Exp).then_inc(s("c_probs"), 1)
                    if ins:
                        inputs(n)
                    if outs and n == 4:
                        ln_scalar(act, "m", r - 1, 1)
                if outs and not heads:
                    ln_scalar(act, "m", r - 1, 1)

            rounds(act, body)

        def p5_vector(v):
            v.memset(vv_b[:, :, :, HD:HD + 1], 1.0).then_inc(s("c_ones"), 1)
            v.wait_ge(s("c_ones"), 1)

            def outputs(r):
                v.wait_ge(s("c_pv"), (r - 1) * NQ)
                o5 = PO[0:T, 0, 0:H * (HD + 1)].rearrange("p (h e) -> p h e", h=H)
                v.reciprocal(rden[:, 0, :], o5[:, :, HD]).then_inc(s("c_o"), 1)
                v.wait_ge(s("c_o"), (r - 2) * 2 + 1)
                v.tensor_tensor(o_main[:], o5[:, :, 0:HD], bcast(rden[:, 0, :], 2, HD), ALU.mult).then_inc(s("c_o"), 1)
                v.wait_ge(s("c_o"), (r - 2) * 2 + 2)
                v.tensor_tensor(X[:, r - 2, :], o_main[:].rearrange("p h e -> p (h e)"), X[:, r - 2, :],
                                ALU.add).then_inc(s("c_x"), 1)

            def quantize_tokens(b):
                src = xnall[0:T, b, :].rearrange("p (n e) -> p n e", e=BLK)
                for k in range(NQX):
                    if k == 0:
                        v.wait_ge(s("ln_xn"), b + (1 + NORMS["m"]))
                        v.memset(tick_v[:, 2:3], 0.0)
                    else:
                        v.wait_ge(s("m_tokens"), b * NQX + k)
                    quantize_step(v, k, src, src, m_rs[0:T, 0:D // BLK], m_sc[0:T, 0:D // BLK],
                                  *twork).then_inc(s("m_tokens"), 1)

            def measure(r):
                v.wait_ge(s("c_x"), r - 1)
                v.memset(tick_v[:, 1:2], 0.0)
                ln_measure(v, "m", lambda j: X[:, r - 2, :], r - 1)

            def body(r, own, ins, heads, outs):
                _, k2, vals = heads_in[1 - own]
                if outs:
                    outputs(r)
                if not ins:
                    measure(r)
                    ln_apply(v, "m", lambda j: X[:, r - 2, :], r - 1, dst=lambda j: xnall[0:T, r - 2, :])
                    quantize_tokens(r - 2)
                    return
                first = isinstance(r, int) and r == 0
                for f in range(2):
                    v.wait_ge(s("c_fill"), r * NF5 + (1 + f))
                    v.tensor_copy(ctxT[:, f, :], (BANK_A, BANK_B)[f][:, 0:TC]).then_inc(s("c_emptyv"), 1)
                v.wait_ge(s("c_fill"), r * NF5 + 3)
                v.tensor_copy(xnT[:, :, 0:T], PH[:, 0:KD * T].rearrange("p (k t) -> p k t", k=KD)).then_inc(s("c_emptyv"), 1)
                if outs:
                    measure(r)
                v.wait_ge(s("c_fill"), r * NF5 + 6)
                v.tensor_copy(vals[:, 0:2, :, 0:HD], PH[0:KT, :].rearrange("p (t h e) -> p t h e", t=2, h=H)).then_inc(s("c_emptyv"), 1)
                if outs:
                    ln_apply(v, "m", lambda j: X[:, r - 2, :], r - 1, dst=lambda j: xnall[0:T, r - 2, :])
                for m in range(KD):
                    v.wait_ge(s("c_rs"), r * 2 + (1 + m))
                    if not first:
                        v.wait_ge(s("c_qm"), r * 2)
                    bank = (BANK_A, BANK_B)[m]
                    v.tensor_tensor(qT[:, m, 0:T], bank[:, 0:T], rms[:, m, 0:T], ALU.mult).then_inc(s("c_q"), 1)
                    v.tensor_tensor(k2[:, m, T:T + TC], bank[:, T:T + TC], rms[:, m, T:T + TC], ALU.mult).then_inc(s("c_emptyv"), 1)
                v.wait_ge(s("c_fill"), r * NF5 + 9)
                v.tensor_copy(vals[:, 2, :, 0:HD], PH[0:KT, 0:D].rearrange("p (h e) -> p h e", h=H)).then_inc(s("c_emptyv"), 1)
                if outs:
                    quantize_tokens(r - 2)

            rounds(v, body)

        def p5_gpsimd(gp):
            def body(b, q, first=False):
                if not first:
                    gp.wait_ge(s("c_fill"), (b - 1) * NF5 + 3)
                    take_wait(gp)
                gp.tensor_copy(xn[:, 0, :], xnall[0:T, b, :]).then_inc(s("c_xs"), 1)
                by_half(gp, "c", b, q)

            gp.wait_ge(s("ln_xn"), NORMS["m"])
            body(0, heads_in[0][0], True)
            with gp.Fori(1, B - 1, 2) as b:
                body(b, heads_in[1][0])
                body(b + 1, heads_in[0][0])
            body(B - 1, heads_in[1][0])

        def above(e, dst, xa, m, more=None):
            if more is None:
                return e.tensor_scalar(dst, xa, m, None, ALU.is_gt)
            return e.scalar_tensor_tensor(out=dst, in0=xa, scalar=m, in1=more, op0=ALU.is_gt, op1=ALU.add)

        def quantize_step(v, k, src, dst, rs, sc, xr, xa, sg, ones):
            twos = xr
            if k == 0:
                return v.tensor_reduce(sc, src, AX.X, ALU.max, apply_absolute_value=True)
            if k == 1:
                return v.tensor_scalar(sc, sc, 1.0 / 6.0, 1e-12, ALU.mult, ALU.max)
            if k == 2:
                return v.reciprocal(rs, sc)
            if k == 3:
                return v.tensor_tensor(xr, src, bcast(rs, 2, BLK), ALU.mult)
            if k == 4:
                v.tensor_scalar(sg, xr, 0.0, None, ALU.is_ge)
                return v.scalar_tensor_tensor(out=xa, in0=xr, scalar=-1.0, in1=xr, op0=ALU.mult, op1=ALU.max)
            if k == 5:
                v.tensor_scalar(sg, sg, 2.0, -1.0, ALU.mult, ALU.add)
                above(v, ones, xa, MIDS[0])
                return v.tensor_scalar(twos, xa, MIDS[6], 2.0, ALU.is_gt, ALU.mult)
            if k in (6, 7):
                above(v, ones, xa, MIDS[k - 5], ones)
                return above(v, twos, xa, MIDS[11 - k], twos)
            if k == 8:
                above(v, ones, xa, MIDS[3], ones)
                return v.tensor_tensor(sg, sg, bcast(sc, 2, BLK), ALU.mult)
            if k == 9:
                return v.scalar_tensor_tensor(out=twos, in0=ones, scalar=0.5, in1=twos, op0=ALU.mult, op1=ALU.add)
            return v.tensor_tensor(dst, twos, sg, ALU.mult)

        def quantize_vector(v, k, n, b, src, dst, rs, sc, xr, xa, sg, ones, ready=None):
            twos = xr
            if k not in (0, 4):
                v.wait_ge(s(n + "_v"), b * NQV + k)
            if k == 0:
                step = v.tensor_reduce(sc, src, AX.X, ALU.max, apply_absolute_value=True)
            elif k == 1:
                step = v.tensor_scalar(sc, sc, 1.0 / 6.0, 1e-12, ALU.mult, ALU.max)
            elif k == 2:
                step = v.reciprocal(rs, sc)
            elif k == 3:
                step = v.tensor_tensor(xr, src, bcast(rs, 2, BLK), ALU.mult)
            elif k == 4:
                v.wait_ge(s(n + "_a"), b + 1)
                step = v.tensor_scalar(twos, xa, MIDS[6], 2.0, ALU.is_gt, ALU.mult)
            elif k in (5, 6):
                step = above(v, twos, xa, MIDS[10 - k], twos)
            elif k in (7, 8, 9):
                if k == 7:
                    v.wait_ge(s(n + "_g"), b * 2 + 1)
                step = above(v, ones, xa, MIDS[k - 6], ones)
            elif k == 10:
                step = v.scalar_tensor_tensor(out=twos, in0=ones, scalar=0.5, in1=twos, op0=ALU.mult, op1=ALU.add)
            elif k == 11:
                v.wait_ge(s(n + "_g"), b * 2 + 2)
                if ready:
                    v.wait_ge(*ready)
                step = v.tensor_tensor(dst, twos, sg, ALU.mult)
            step.then_inc(s(n + "_v"), 1)

        def quantize_scalar(act, n, b, xr, xa, sg):
            act.wait_ge(s(n + "_v"), b * NQV + 4)
            act.activation(xa, xr, ACT.Abs)
            act.activation(sg, xr, ACT.Sign).then_inc(s(n + "_a"), 1)

        def quantize_gpsimd(gp, n, b, sc, xa, sg, ones):
            gp.wait_ge(s(n + "_a"), b + 1)
            take_wait(gp, 1)
            above(gp, ones, xa, MIDS[0]).then_inc(s(n + "_g"), 1)
            gp.tensor_tensor(sg, sg, bcast(sc, 2, BLK), ALU.mult).then_inc(s(n + "_g"), 1)

        NQB = FF // BLK
        NTD = -(-FF // 128)
        FH = FF // 2
        xq = big[0:T, 0:D]
        gated = big[0:T, 256:256 + FF]
        hid = big[0:T, 1024:1024 + FF]
        prod = big[0:T, 1792:1792 + FF]
        qwork = [big[:, 2560 + i * 1024:2560 + (i + 1) * 1024] for i in range(4)]
        hqT = big[:, 6656:6656 + 6 * T].rearrange("p (t q) -> p t q", t=6)


        def blocks(ap, n):
            return ap[:, 0:n * BLK].rearrange("p (n e) -> p n e", e=BLK)

        hwork = [blocks(q[0:T], NQB) for q in qwork]
        twork = [big[0:T, 7520 + i * D:7520 + (i + 1) * D].rearrange("p (n e) -> p n e", e=BLK) for i in range(4)]

        def p6_tensor(pe):
            def gate_up(b):
                pe.wait_ge(s("m_xs"), b + 1)
                for k in range(KD):
                    last = pe.transpose(PO[:, 1, k * T:(k + 1) * T], xq[:, k * 128:(k + 1) * 128], ident[0:T, 0:T])
                last.then_inc(s("m_tr"), 1)
                pe.wait_ge(s("m_xT"), b + 1)
                pe.wait_ge(s("m_h"), b + 1)
                for gu in range(2):
                    for i in range(2):
                        for k in range(KD):
                            last = pe.matmul(PS[0:T, 2 * gu + i, 0:FH], xnT[:, k, 0:T],
                                             m_wgu[gu][:, k, i * FH:(i + 1) * FH], start=k == 0, stop=k == KD - 1)
                last.then_inc(s("m_gu"), 1)

            def down(b):
                pe.wait_ge(s("m_hid_v"), b * NQV + NQV)
                for t in range(NTD):
                    n = min(128, FF - t * 128)
                    last = pe.transpose(PT[0:n, t // 4, (t % 4) * T:(t % 4 + 1) * T], hid[:, t * 128:t * 128 + n],
                                        ident[0:T, 0:T])
                last.then_inc(s("m_htr"), 1)
                pe.wait_ge(s("m_hT"), b + 1)
                pe.wait_ge(s("m_x"), b + 1)
                for t in range(NTD):
                    n = min(128, FF - t * 128)
                    last = pe.matmul(PO[0:T, 0, 0:D], hqT[0:n, t, :], m_wd[0:n, t, :], start=t == 0, stop=t == NTD - 1)
                last.then_inc(s("m_out"), 1)

            gate_up(0)
            with pe.Fori(0, B - 1, 1) as b:
                gate_up(b + 1)
                down(b)
            down(B - 1)

        def p6_scalar(act):
            def gate(b):
                act.wait_ge(s("m_tr"), b + 2)
                act.activation(xnT[:, :, 0:T], PO[:, 1, 0:KD * T].rearrange("p (k t) -> p k t", k=KD),
                               ACT.Copy).then_inc(s("m_xT"), 1)
                act.wait_ge(s("m_gu"), b + 1)
                act.activation(gated.rearrange("p (i n) -> p i n", i=2), PS[0:T, 0:2, 0:FH], ACT.Silu).then_inc(s("m_silu"), 1)

            def turn(b):
                act.wait_ge(s("m_htr"), b + 1)
                act.activation(hqT[:, 0:4, :], PT[:, 0, 0:4 * T].rearrange("p (t q) -> p t q", t=4), ACT.Copy)
                act.activation(hqT[:, 4:6, :], PT[:, 1, 0:2 * T].rearrange("p (t q) -> p t q", t=2),
                               ACT.Copy).then_inc(s("m_hT"), 1)

            def signs(b):
                quantize_scalar(act, "m_hid", b, hwork[0], hwork[1], hwork[2])

            gate(0)
            signs(0)
            with act.Fori(0, B - 1, 1) as b:
                gate(b + 1)
                turn(b)
                signs(b + 1)
            turn(B - 1)

        def p6_vector(v):
            def hidden(b, hid_read=None):
                v.wait_ge(s("m_silu"), b + 1)
                v.tensor_tensor(prod.rearrange("p (i n) -> p i n", i=2), PS[0:T, 2:4, 0:FH],
                                gated.rearrange("p (i n) -> p i n", i=2), ALU.mult).then_inc(s("m_h"), 1)
                for k in range(NQV):
                    if k == 0:
                        v.wait_ge(s("m_h"), b + 2)
                    quantize_vector(v, k, "m_hid", b, blocks(prod, NQB), blocks(hid, NQB), m_rs[0:T, 0:NQB],
                                    m_sc[0:T, 0:NQB], *hwork, ready=hid_read)

            def add(b):
                v.wait_ge(s("m_out"), b + 1)
                v.tensor_tensor(X[:, b, :], PO[0:T, 0, 0:D], X[:, b, :], ALU.add).then_inc(s("m_x"), 1)

            hidden(0)
            with v.Fori(0, B - 1, 1) as b:
                hidden(b + 1, (s("m_htr"), b + 1))
                add(b)
            add(B - 1)

        def p6_gpsimd(gp):
            gp.sem_inc(s("m_tr"), 1)
            gp.sem_inc(s("m_h"), 1)
            gp.sem_inc(s("m_x"), 1)
            gp.wait_ge(s("m_tokens"), B * NQX)

            def tokens(b):
                gp.wait_ge(s("m_tr"), b + 1)
                take_wait(gp)
                gp.tensor_copy(xq, xnall[0:T, b, :]).then_inc(s("m_xs"), 1)

            def hidden(b):
                quantize_gpsimd(gp, "m_hid", b, m_sc[0:T, 0:NQB], *hwork[1:])

            tokens(0)
            tokens(1)
            hidden(0)
            with gp.Fori(0, B - 2, 1) as b:
                tokens(b + 2)
                hidden(b + 1)
            hidden(B - 1)

        NS = 7
        W2 = 2 * NHT
        pair_sel = qm[0:64].rearrange("p h t -> p (h t)").rearrange("p (k r f) -> p k r f", k=NS, r=2)
        pong = big[:, 0:NHT * (D + 1)].rearrange("p (t d) -> p t d", t=NHT)
        perm = big[:, 0:NS * 256].rearrange("p (k r f) -> p k r f", k=NS, r=2)
        m_flat = m_raw[:].rearrange("p c n -> p (c n)")
        stages = (big[:, 1792:1792 + 2048].rearrange("p (u f) -> p u f", u=W2),
                  m_flat[:, 0:2048].rearrange("p (u f) -> p u f", u=W2))
        down_b = m_flat[:, 2048:4096].rearrange("p (t d) -> p t d", t=NHT)
        chain = big[:, 3840:3840 + 2048].rearrange("p (u f) -> p u f", u=W2)
        wexpT = big[:, 5888:5888 + NHT * (D + 1)].rearrange("p (t d) -> p t d", t=NHT)
        pair_w = big[0:64, 7944:7944 + NS * W2 * 4].rearrange("p (k u c) -> p k u c", k=NS, u=W2)
        row_w = big[:, 8392:8392 + NS * W2 * 2].rearrange("p (k u c) -> p k u c", k=NS, u=W2)
        raw_r = big[:, 0:8 * D].rearrange("p (m d) -> p m d", m=8)
        raw_d = m_flat[:, 2 * FF // 128 * D:3 * FF * D // 128].rearrange("p (m k) -> p m k", m=2)
        raw_kv = sb("raw_kv", [128, KD, 2 * D])
        high_w = sb("high_w", [128, 2, 3, 4, 4])
        f_upb = sb("f_upb", [128, NHT])
        swork = [big[:, i * CHB * BLK:(i + 1) * CHB * BLK] for i in range(4)]

        def setup_loads_1(sp):
            sp.dma_start(f_up[:], a["L0_ffn_W_exp"].rearrange("(k p) n -> p k n", p=128)).then_inc(s("ld_f"), 16)
            sp.dma_start(f_down[:], a["L0_ffn_W_con"].rearrange("(t p) n -> p t n", p=128)).then_inc(s("ld_f"), 16)
            for i, n in enumerate(("up", "down")):
                src = a[f"L0_ffn_{n}_weights"]
                for k in range(NS):
                    sp.dma_start(pair_w[:, k, i * NHT:(i + 1) * NHT, :],
                                 src[k].rearrange("(t p) r c -> p t (r c)", p=64)).then_inc(s("ld_f"), 16)
                for k in range(3):
                    sp.dma_start(high_w[:, i, k, :, :],
                                 src[NS + k].rearrange("(q p) r c -> p q (r c)", p=128)).then_inc(s("ld_f"), 16)
            sp.dma_start(perm, c["perm"]).then_inc(s("ld_f"), 16)
            sp.dma_start(pair_sel, c["pair_sel"]).then_inc(s("ld_f"), 16)
            sp.dma_start(wexpT[:, :, D], a["L0_ffn_b_exp"].rearrange("(t p) -> p t", p=128)).then_inc(s("ld_f"), 16)
            sp.dma_start(f_upb[:], a["L0_ffn_up_bias"].rearrange("(t p) -> p t", p=128)).then_inc(s("ld_f"), 16)
            sp.dma_start(f_bo[:], a["L0_ffn_b_con"].partition_broadcast(T)).then_inc(s("ld_f"), 16)
            sp.dma_start(f_bd[:], a["L0_ffn_down_bias"].partition_broadcast(T)).then_inc(s("ld_f"), 16)

        NF = 2 + 2 * (NS + 3) + 6

        def fold_scalar(act):
            act.wait_ge(s("ld_f"), 16 * NF)
            act.wait_ge(s("row_w"), 1)
            for n, k in enumerate(reversed(range(NS))):
                for u in range(W2):
                    last = act.activation(stages[n % 2][:, u, :], perm[:, k, 0, :], ACT.Copy, scale=row_w[:, k, u, 0:1])
                last.then_inc(s("stage_a"), 1)
                if n == 0:
                    continue
                act.wait_ge(s("chain_mm"), n)
                act.activation(chain, PS[:].rearrange("p b (u f) -> p (b u) f", f=128), ACT.Copy).then_inc(s("chain"), 1)
            act.wait_ge(s("chain_mm"), NS)
            act.activation(chain, PS[:].rearrange("p b (u f) -> p (b u) f", f=128), ACT.Copy).then_inc(s("chain"), 1)
            act.wait_ge(s("wexp_tr"), 1)
            act.activation(wexpT[:, :, 0:D], PS[:].rearrange("p b (t d) -> p (b t) d", d=D), ACT.Copy).then_inc(s("wexpT"), 1)
            for i in range(2):
                act.wait_ge(s("up_low"), i + 1)
                act.activation(wexpT[:, 4 * i:4 * i + 4, :], PS[:, :, 0:D + 1], ACT.Copy).then_inc(s("up_lowc"), 1)
            act.wait_ge(s("up_tr"), 1)
            act.activation(f_up[:], PS[:].rearrange("p (k i) n -> p k (i n)", k=KD), ACT.Copy).then_inc(s("f_ready"), 1)
            for i in range(2):
                act.wait_ge(s("down_low"), i + 1)
                act.activation(f_down[:, 4 * i:4 * i + 4, :], PS[:, :, 0:D], ACT.Copy).then_inc(s("down_lowc"), 1)

        def fold_tensor(pe):
            pe.wait_ge(s("ld_f"), 16 * NF)
            for k in range(NS):
                for r in range(2):
                    last = pe.matmul(PT[:, 0, k * 32:(k + 1) * 32], pair_sel[:, k, r, :],
                                     pair_w[:, k, :, 2 * r:2 * r + 2], start=r == 0, stop=r == 1)
            last.then_inc(s("row_wp"), 1)
            for n, k in enumerate(reversed(range(NS))):
                pe.wait_ge(s("stage_b"), n + 1)
                if n > 0:
                    pe.wait_ge(s("chain"), n)
                for u in range(W2):
                    before = ident[:] if n == 0 else chain[:, u, :]
                    left, right = stages[n % 2][:, u, :], before
                    if k == 0 and u >= NHT:
                        left, right = right, left
                    last = pe.matmul(PS[:, u // 4, (u % 4) * 128:(u % 4 + 1) * 128], left, right, start=True, stop=True)
                last.then_inc(s("chain_mm"), 1)
            pe.wait_ge(s("chain"), NS)
            for t in range(NHT):
                for k in range(KD):
                    last = pe.transpose(PS[:, t // 2, (t % 2) * D + k * 128:(t % 2) * D + (k + 1) * 128],
                                        f_up[:, k, t * 128:(t + 1) * 128], ident[:])
            last.then_inc(s("wexp_tr"), 1)
            pe.wait_ge(s("wexpT"), 1)
            for i in range(2):
                if i > 0:
                    pe.wait_ge(s("up_lowc"), i)
                for t in range(4 * i, 4 * i + 4):
                    last = pe.matmul(PS[:, t % 4, 0:D + 1], chain[:, t, :], wexpT[:, t, :], start=True, stop=True)
                last.then_inc(s("up_low"), 1)
            pe.wait_ge(s("up_lowc"), 2)
            pe.wait_ge(s("high"), 12)
            for k in range(KD):
                for t in range(NHT):
                    last = pe.transpose(PS[:, 2 * k + t // 4, (t % 4) * 128:(t % 4 + 1) * 128],
                                        pong[:, t, k * 128:(k + 1) * 128], ident[:])
            last.then_inc(s("up_tr"), 1)
            pe.wait_ge(s("f_ready"), 1)
            for i in range(2):
                if i > 0:
                    pe.wait_ge(s("down_lowc"), i)
                for t in range(4 * i, 4 * i + 4):
                    last = pe.matmul(PS[:, t % 4, 0:D], chain[:, NHT + t, :], down_b[:, t, :], start=True, stop=True)
                last.then_inc(s("down_low"), 1)

        def fold_vector(v):
            done = [0]

            def half(dst, src, i, k, width, which):
                pairs = [(lo, lo | 1 << k) for lo in range(NHT) if not lo >> k & 1]

                def coef(q, r, col):
                    at = 2 * r + col if i == 0 else 2 * col + r
                    return high_w[:, i, k, q, at:at + 1]

                for q, ab in enumerate(pairs):
                    for r in range(2):
                        if which == 0:
                            last = v.tensor_scalar(dst[:, ab[r], 0:width], src[:, ab[1], 0:width], coef(q, r, 1), None, ALU.mult)
                        else:
                            last = v.scalar_tensor_tensor(out=dst[:, ab[r], 0:width], in0=src[:, ab[0], 0:width],
                                                          scalar=coef(q, r, 0), in1=dst[:, ab[r], 0:width],
                                                          op0=ALU.mult, op1=ALU.add)
                last.then_inc(s("high"), 1)
                done[0] += 1
                v.wait_ge(s("high"), done[0])

            def high(src, dst, i, k, width):
                half(dst, src, i, k, width, 0)
                half(dst, src, i, k, width, 1)

            v.wait_ge(s("ld_f"), 16 * NF)
            v.wait_ge(s("row_wp"), 1)
            v.tensor_copy(row_w, PT[:, 0, 0:NS * 32].rearrange("p (k u c) -> p k u c", k=NS, u=W2)).then_inc(s("row_w"), 1)
            v.wait_ge(s("row_w"), 1)
            for n, k in enumerate(reversed(range(NS))):
                v.wait_ge(s("stage_a"), n + 1)
                stage = stages[n % 2]
                for u in range(W2):
                    last = v.scalar_tensor_tensor(out=stage[:, u, :], in0=perm[:, k, 1, :], scalar=row_w[:, k, u, 1:2],
                                                  in1=stage[:, u, :], op0=ALU.mult, op1=ALU.add)
                last.then_inc(s("stage_b"), 1)
                if n < 6:
                    half(*((down_b, f_down, 1, 2), (f_down, down_b, 1, 1), (down_b, f_down, 1, 0))[n // 2], D, n % 2)

            v.wait_ge(s("up_lowc"), 2)
            high(wexpT, pong, 0, 0, D + 1)
            high(pong, wexpT, 0, 1, D + 1)
            high(wexpT, pong, 0, 2, D + 1)
            v.tensor_tensor(f_hb[:], pong[:, :, D], f_upb[:], ALU.add).then_inc(s("high"), 1)
            done[0] += 1
            v.wait_ge(s("high"), done[0])

        def setup_loads_2(sp):
            sp.dma_start(raw_kv[:], a["L1_xattn_W_kv"].rearrange("(k p) n -> p k n", p=128)).then_inc(s("ld_r"), 16)
            sp.dma_start(c_wq[:], a["L1_xattn_W_q"].rearrange("(k p) n -> p k n", p=128)).then_inc(s("ld_r"), 16)
            sp.wait_ge(s("down_lowc"), 2)
            sp.wait_ge(s("high"), 13)
            sp.dma_start(raw_r[:, 0:6, :], a["L1_attn_qkv_w"].rearrange("(m p) d -> p m d", p=128)).then_inc(s("ld_r"), 16)
            sp.dma_start(raw_r[:, 6:8, :], a["L1_attn_out_w"].rearrange("(m p) d -> p m d", p=128)).then_inc(s("ld_r"), 16)
            n = FF // 128 * 128
            gu = m_flat[:, 0:2 * FF // 128 * D].rearrange("p (t d) -> p t d", d=D)
            gate, up = a["L1_ffn_w_gate"], a["L1_ffn_w_up"]
            for dst, src in ((gu[:, 0:n // 128, :], gate[0:n].rearrange("(t p) d -> p t d", p=128)),
                             (gu[0:FF - n, n // 128, :], gate[n:FF]),
                             (gu[FF - n:128, n // 128, :], up[0:n + 128 - FF]),
                             (gu[:, n // 128 + 1:, :], up[n + 128 - FF:FF].rearrange("(t p) d -> p t d", p=128)),
                             (raw_d, a["L1_ffn_w_down"].rearrange("(m p) k -> p m k", p=128))):
                sp.dma_start(dst, src).then_inc(s("ld_d"), 16)

        def weights_tensor(pe):
            pe.wait_ge(s("ld_r"), 64)
            pe.wait_ge(s("down_lowc"), 2)
            for k in range(KD):
                for m in range(8):
                    last = pe.transpose(PS[:, 2 * k + m // 4, (m % 4) * 128:(m % 4 + 1) * 128],
                                        raw_r[:, m, k * 128:(k + 1) * 128], ident[:])
            last.then_inc(s("r_wtr"), 1)

        def p6_weights_tensor(pe):
            pe.wait_ge(s("m_wq"), NCH * NQX)
            pe.wait_ge(s("c_x"), B)
            for k in range(KD):
                if k > 0:
                    pe.wait_ge(s("m_wcopy"), 1)
                for t in range(2 * FF // 128):
                    last = pe.transpose(PS[:, t // 4, (t % 4) * 128:(t % 4 + 1) * 128],
                                        m_flat[:, t * D + k * 128:t * D + (k + 1) * 128], ident[:])
                last.then_inc(s("m_wtr"), 1)
                if k == 0:
                    for t in range(NTD):
                        n = min(128, FF - t * 128)
                        for m in range(2):
                            dst = (PT[0:n, t // 2, :] if t < 4 else PO[0:n, 0, :])[:, (t % 2) * D + m * 128:(t % 2) * D + (m + 1) * 128]
                            last = pe.transpose(dst, raw_d[:, m, t * 128:t * 128 + n], ident[:])
                    last.then_inc(s("m_wtr"), 1)
            pe.wait_ge(s("m_wcopy"), 2)
            pe.wait_ge(s("m_wdcopy"), 1)

        def p6_weights_scalar(act):
            for k in range(KD):
                act.wait_ge(s("m_wtr"), 2 * k + 1)
                for i in range(2):
                    last = act.activation(m_wgu[i][:, k, :], PS[:].rearrange("p b n -> p (b n)")[:, i * FF:(i + 1) * FF], ACT.Copy)
                last.then_inc(s("m_wcopy"), 1)

        def p6_weights_vector(v):
            v.wait_ge(s("m_wtr"), 2)
            v.tensor_copy(m_wd[:, 0:4, :], PT[:].rearrange("p b (t n) -> p (b t) n", n=D))
            v.tensor_copy(m_wd[:, 4, :], PO[:, 0, 0:D])
            v.tensor_copy(m_wd[0:64, 5, :], PO[0:64, 0, D:2 * D]).then_inc(s("m_wdcopy"), 1)

        def weights_vector(v):
            v.memset(vv[:, :, :, HD:HD + 1], 1.0).then_inc(s("consts2"), 1)
            v.wait_ge(s("consts2"), 1)
            v.wait_ge(s("r_wtr"), 1)
            for k in range(KD):
                v.tensor_copy(r_w[:, k, 0:512], PS[:, 2 * k, :])
                v.tensor_copy(r_w[:, k, 512:768], PS[:, 2 * k + 1, 0:256])
                last = v.tensor_copy(r_wo[:, k, :], PS[:, 2 * k + 1, 256:512])
            last.then_inc(s("r_wcopy"), 1)
            v.wait_ge(s("r_wcopy"), 1)
            for k in range(KD):
                pairs = r_w[:, k, 0:512].rearrange("p (n e) -> p n e", e=2)
                turned = r_wr[:, k, :].rearrange("p (n e) -> p n e", e=2)
                v.tensor_scalar(turned[:, :, 0], pairs[:, :, 1], -1.0, None, ALU.mult)
                v.tensor_copy(turned[:, :, 1], pairs[:, :, 0])
            v.wait_ge(s("ld_r"), 64)
            v.tensor_copy(c_wk[:], raw_kv[:].rearrange("p k (n e) -> p k n e", e=2)[:, :, :, 0])
            v.tensor_copy(c_wv[:], raw_kv[:].rearrange("p k (n e) -> p k n e", e=2)[:, :, :, 1]).then_inc(s("w_done"), 1)
            v.wait_ge(s("ld_d"), 16 * 5)
            v.memset(m_flat[:, 3 * FF * D // 128:], 0.0).then_inc(s("w_done"), 1)

        heads_in = ((qm, kT, vv), (qm_b, kT_b, vv_b))
        PH = PO[:, 1, :]
        Xg = X[:].rearrange("p (g j) d -> p g j d", j=G)
        xnallg = xnall[0:T].rearrange("p (g j) d -> p g j d", j=G)
        hT = big[:, 0:NHT * G * T].rearrange("p (t q) -> p t q", t=NHT)
        rot = big[:, 0:2 * 4 * T].rearrange("p (r i t) -> p r i t", r=2, i=4)
        sq = sb("sq", [128, KD, T + TC])
        p1v = sb("p1v", [T, G, HS])[:]
        p1s = sb("p1s", [T, G, T])[:]
        p1p = sb("p1p", [T, G, T])
        p1pT = sb("p1pT", [T, G * T])[:]
        p1z = sb("p1z", [HS, G * T])[:]

        NCONST, NW = 6, 10
        block = ctx.enter_context(nc.Block())

        @block.sync
        def _(sp):
            with nc.allow_non_contiguous_dma(reason="small biases, feature on partition"):
                sp.dma_start(X[:, 0:G, :], a["x"][0:G].rearrange("b t d -> t b d")).then_inc(s("ld_x0"), 16)
                for i, n in enumerate(("wq", "wk")):
                    sp.dma_start(a_wqk[:, :, i, :], a["L0_attn_" + n].rearrange("(k p) h -> p k h", p=128)).then_inc(s("ld_a"), 16)
                sp.dma_start(a_wv[:], a["L0_attn_wv"].rearrange("(k p) h -> p k h", p=128)).then_inc(s("ld_a"), 16)
                sp.dma_start(a_wo[:], a["L0_attn_wo"]).then_inc(s("ld_a"), 16)
                sp.dma_start(a_bqk[:, 0:1], a["L0_attn_bq"].unsqueeze(1)).then_inc(s("ld_a"), 16)
                sp.dma_start(a_bqk[:, 1:2], a["L0_attn_bk"].unsqueeze(1)).then_inc(s("ld_a"), 16)
                sp.dma_start(a_bv[:], a["L0_attn_bv"].partition_broadcast(T)).then_inc(s("ld_a"), 16)
                sp.dma_start(a_bo[:], a["L0_attn_bo"].partition_broadcast(T)).then_inc(s("ld_a"), 16)
                sp.dma_start(X[:, G:B, :], a["x"][G:B].rearrange("b t d -> t b d")).then_inc(s("ld_x"), 16)
                for t, src in ((x_w, a["L0_xattn_Wqkv"]), (x_wa, a["L0_xattn_Wqkv_aux"][:, D:3 * D]), (x_wo, a["L0_xattn_Wo"])):
                    sp.dma_start(t[:], src.rearrange("(k p) n -> p k n", p=128)).then_inc(s("ld_w"), 16)
                for i in range(2):
                    sp.dma_start(x_bqk[:, i, :], a["L0_xattn_bqkv"][i * D:(i + 1) * D].rearrange("(m p) -> p m", p=128)).then_inc(s("ld_w"), 16)
                sp.dma_start(x_bka[:], a["L0_xattn_bqkv_aux"][D:2 * D].rearrange("(m p) -> p m", p=128)).then_inc(s("ld_w"), 16)
                sp.dma_start(x_bv[:], a["L0_xattn_bqkv"][2 * D:3 * D].partition_broadcast(T)).then_inc(s("ld_w"), 16)
                sp.dma_start(x_bva[:], a["L0_xattn_bqkv_aux"][2 * D:3 * D].partition_broadcast(KT)).then_inc(s("ld_w"), 16)
                sp.dma_start(x_bo[:], a["L0_xattn_bo"].partition_broadcast(T)).then_inc(s("ld_w"), 16)
                sp.dma_start(x_g[:], a["L0_xattn_g"].partition_broadcast(T)).then_inc(s("ld_w"), 16)
                setup_loads_1(sp)
                setup_loads_2(sp)
            sp.dma_start(ctxn[:], ctx_tiles[0]).then_inc(s("ctx"), 16)
            ctx_load(sp, "x_fill", NP, 2)
            sp.wait_ge(s("x_fill"), (B - 1) * NP + 2)
            sp.dma_start(ctxn[:], ctx_tiles[0]).then_inc(s("ctx"), 16)
            ctx_load(sp, "c_fill", NF5, 2)
            sp.wait_ge(s(FINAL[parts][0]), FINAL[parts][1])
            sp.dma_start(out.rearrange("b t d -> t b d"), X[:]).then_inc(s("stored"), 16)
            sp.wait_ge(s("stored"), 16)

        @block.gpsimd
        def _(gp):
            gp.memset(tick_g[:], 0.0).then_inc(s("tick"), 1)
            gp.wait_ge(s("tick"), 1)
            for t, n in ((ident, "ident"), (causal, "causal"), (headmask, "headmask"), (headsum, "headsum")):
                gp.dma_start(t[:], c[n]).then_inc(s("ld_c"), 16)
            gp.dma_start(cosq[:], c["cos"]).then_inc(s("ld_c"), 16)
            gp.dma_start(sinq[:], c["sin"]).then_inc(s("ld_c"), 16)
            gp.wait_ge(s("ld_a"), 16 * 8)
            gp.wait_ge(s("ld_c"), 16 * NCONST)
            p1_gpsimd(gp)
            gp.wait_ge(s("ld_w"), 16 * NW)
            gp.wait_ge(s("ld_f"), 16 * NF)
            gp.tensor_tensor(f_bo[:], f_bo[:], f_bd[:], ALU.add).then_inc(s("f_bias"), 1)
            p2_gpsimd(gp)
            gp.wait_ge(s("f_bias"), 1)
            p3_gpsimd(gp)
            p4_gpsimd(gp)
            p5_gpsimd(gp)
            p6_gpsimd(gp)

        @block.scalar
        def _(act):
            act.wait_ge(s("ld_a"), 16 * 8)
            act.wait_ge(s("consts"), 3)
            act.preload_act_table_set("natural_log_exp_and_others")
            p1_scalar(act)
            act.wait_ge(s("ld_w"), 16 * NW)
            act.activation(x_gate[:, 1, :], x_g[:], ACT.Exp, scale=-1.0).then_inc(s("gate_exp"), 1)
            fold_scalar(act)
            p2_scalar(act)
            p3_scalar(act)
            p4_scalar(act)
            p5_scalar(act)
            p6_weights_scalar(act)
            act.preload_act_table(ACT.Silu)
            p6_scalar(act)

        @block.vector
        def _(v):
            v.memset(eps_ln[:], LN_EPS).then_inc(s("consts"), 1)
            v.memset(eps_rms[:], RMS_EPS).then_inc(s("consts"), 1)
            v.memset(PT[:], 0.0).then_inc(s("consts"), 1)
            v.wait_ge(s("ld_x0"), 16)
            v.wait_ge(s("ld_a"), 16 * 8)
            v.wait_ge(s("ld_c"), 16 * NCONST)
            v.tensor_copy(identb[:], ident[0:T, 0:T]).then_inc(s("consts"), 1)
            v.tensor_scalar(causal4[:], bcast(causal[:], 1, 4), 1e19, None, ALU.mult).then_inc(s("consts"), 1)
            p1_vector(v)
            v.wait_ge(s("a_x"), NG)
            fold_vector(v)
            weights_vector(v)
            v.wait_ge(s("gate_exp"), 1)
            v.tensor_scalar(x_gate[:, 1, :], x_gate[:, 1, :], 1.0, None, ALU.add).then_inc(s("gate"), 1)
            v.wait_ge(s("gate"), 1)
            v.reciprocal(x_gate[:, 1, :], x_gate[:, 1, :]).then_inc(s("gate"), 1)
            v.wait_ge(s("gate"), 2)
            v.tensor_scalar(x_gate[:, 0, :], x_gate[:, 1, :], -1.0, 1.0, ALU.mult, ALU.add).then_inc(s("gate"), 1)
            v.wait_ge(s("w_done"), 2)
            v.wait_ge(s("gate"), 3)
            p2_vector(v)
            v.wait_ge(s("x_x"), B)
            p3_vector(v)
            v.wait_ge(s("f_x"), B)
            p4_vector(v)
            v.wait_ge(s("r_x"), B)
            p5_vector(v)
            v.wait_ge(s("c_x"), B)
            p6_weights_vector(v)
            p6_vector(v)

        @block.tensor
        def _(pe):
            pe.wait_ge(s("ld_a"), 16 * 8)
            pe.wait_ge(s("ld_c"), 16 * NCONST)
            pe.wait_ge(s("consts"), 5)
            p1_tensor(pe)
            fold_tensor(pe)
            weights_tensor(pe)
            pe.wait_ge(s("ld_w"), 16 * NW)
            p2_tensor(pe)
            p3_tensor(pe)
            p4_tensor(pe)
            p5_tensor(pe)
            p6_weights_tensor(pe)
            p6_tensor(pe)


def constants():
    import numpy as np
    c = {}
    c["ident"] = np.eye(128, dtype=np.float32)
    up = np.triu(np.ones((T, T), np.float32), 1)
    c["causal"] = up * np.float32(-1e11)
    head = np.arange(128) // HD
    c["headmask"] = (head[:, None] == np.arange(8)[None, :]).astype(np.float32) * np.float32(HD ** -0.5)
    c["headsum"] = (head[:, None] == head[None, :]).astype(np.float32)
    freq = 1.0 / np.float32(10000.0) ** (np.arange(0, HD, 2, dtype=np.float32) / np.float32(HD))
    angle = np.outer(np.arange(T, dtype=np.float32), freq.astype(np.float32)).astype(np.float32)
    rows = angle.T[(np.arange(128) % HD) % (HD // 2)]
    c["cos"], c["sin"] = np.cos(rows).astype(np.float32), np.sin(rows).astype(np.float32)
    p = np.arange(128)
    perm, sel = np.zeros((128, 7, 2, 128), np.float32), np.zeros((64, 7, 2, 128), np.float32)
    for k in range(7):
        perm[p, k, 0, p & ~(1 << k)] = 1
        perm[p, k, 1, p | (1 << k)] = 1
        sel[((p >> (k + 1)) << k) + (p & ((1 << k) - 1)), k, (p >> k) & 1, p] = 1
    c["perm"], c["pair_sel"] = perm, sel
    return c


def kernel(**inputs):
    import numpy as _np
    import concourse.bacc as _bacc
    from concourse import mybir as _mybir
    from concourse.bass_utils import run_bass_kernel_spmd as _run

    nc = _bacc.Bacc("TRN2", target_bir_lowering=False, num_devices=1)
    arrays, args, consts = {}, {}, {}
    for name, value in inputs.items():
        v = _np.ascontiguousarray(value)
        arrays[f"in_{name}"] = v
        args[name] = nc.dram_tensor(f"in_{name}", v.shape, _mybir.dt.from_np(v.dtype), kind="ExternalInput").ap()
    for name, v in constants().items():
        arrays[f"const_{name}"] = v
        consts[name] = nc.dram_tensor(f"const_{name}", v.shape, _mybir.dt.from_np(v.dtype), kind="ExternalInput").ap()
    out = nc.dram_tensor("out", (B, T, D), F32, kind="ExternalOutput").ap()
    build(nc, args, consts, out)
    r = _run(nc, [arrays], core_ids=[0])
    return r.results[0]["out"]
```
